# Optimizing a Trainium2 kernel written in Bass

```python
import numpy as np
import jax
import jax.numpy as jnp

def _softmax(x, axis=-1):
    return jax.nn.softmax(x, axis=axis)

def _gelu(x):
    return jax.nn.gelu(x, approximate=True)

def _silu(x):
    return jax.nn.silu(x)

def _sigmoid(x):
    return jax.nn.sigmoid(x)

def _layernorm(x, axis=-1, eps=1e-05):
    m = jnp.mean(x, axis=axis, keepdims=True)
    v = jnp.var(x, axis=axis, keepdims=True)
    return (x - m) / jnp.sqrt(v + eps)

def _scatter_add(tgt, idx, src, axis=0):
    return tgt.at[idx].add(src)

def _segment_sum(src, seg, n):
    return jax.ops.segment_sum(src, seg, n)
kernel_name = 'mk_gnn_resnorm_d4_gnn_r64_5678f9'

def setup_inputs(seed: int=0):
    np.random.seed(seed)
    _w = jnp.asarray

    def _rec_inputs():
        import jax
        import jax.numpy as jnp
        _gk = jax.random.key(seed)
        x = -0.0005121 + 1.001 * jax.random.normal(jax.random.fold_in(_gk, 1), (100000, 64), jnp.float32)
        src = jax.random.randint(jax.random.fold_in(_gk, 2), (50000,), 0, 100000, jnp.int32)
        dst = jnp.minimum((100000 * jax.random.uniform(jax.random.fold_in(_gk, 3), (50000,)) ** 2.0).astype(jnp.int32), 99999)
        _o = jnp.argsort(dst, stable=True)
        src = src[_o]
        dst = dst[_o]
        edge_weight = jax.random.uniform(jax.random.fold_in(_gk, 12), (50000,), jnp.float32, 0.0, 0.999998)
        edge_weight_n2 = jax.random.uniform(jax.random.fold_in(_gk, 13), (50000,), jnp.float32, 0.0, 0.999998)
        return (x, src, dst, edge_weight, edge_weight_n2)
    x, src, dst, edge_weight, edge_weight_n2 = _rec_inputs()

    def _L0_gnn_setup():
        import jax, jax.numpy as jnp
        import numpy as np
        N = 50000
        E = 12500
        D = 64
        EPS = 1e-12
        NEG_SLOPE = 0.01

        def sage_conv(x, edge_index, W_l, b_l, W_r):
            src, dst = (edge_index[0], edge_index[1])
            n = x.shape[0]
            sums = jax.ops.segment_sum(x[src], dst, num_segments=n)
            cnt = jax.ops.segment_sum(jnp.ones((src.shape[0],), x.dtype), dst, num_segments=n)
            mean = sums / jnp.maximum(cnt, 1.0)[:, None]
            return mean @ W_l.T + b_l + x @ W_r.T
        key = jax.random.key(seed)
        k = jax.random.split(key, 8)
        x = jax.random.normal(k[0], (N, D), dtype=jnp.float32)
        edge_index = jax.random.randint(k[1], (2, E), 0, N, dtype=jnp.int64)
        edge_weight = jax.random.uniform(k[2], (E,), dtype=jnp.float32)
        s1 = 1.0 / np.sqrt(D)
        W1_l = jax.random.uniform(k[3], (D, D), minval=-s1, maxval=s1, dtype=jnp.float32)
        W1_r = jax.random.uniform(k[4], (D, D), minval=-s1, maxval=s1, dtype=jnp.float32)
        b1 = jnp.zeros((D,), jnp.float32)
        W2_l = jax.random.uniform(k[5], (D, D), minval=-s1, maxval=s1, dtype=jnp.float32)
        W2_r = jax.random.uniform(k[6], (D, D), minval=-s1, maxval=s1, dtype=jnp.float32)
        b2 = jnp.zeros((D,), jnp.float32)
        return {'x': x, 'edge_index': edge_index, 'edge_weight': edge_weight, 'W1_l': W1_l, 'b1': b1, 'W1_r': W1_r, 'W2_l': W2_l, 'b2': b2, 'W2_r': W2_r}
    _L0_gnn_all = _L0_gnn_setup()
    _L0_gnn_in = {k: v for k, v in _L0_gnn_all.items() if k in ('W1_l', 'b1', 'W1_r', 'W2_l', 'b2', 'W2_r')}
    del _L0_gnn_all

    def _L1_gnn_setup():
        import jax, jax.numpy as jnp
        import numpy as np
        N, E, D_IN, D_OUT = (1024, 16384, 64, 64)
        EPS = 1e-08
        key = jax.random.key(seed)
        ks = jax.random.split(key, 8)
        h = jax.random.normal(ks[0], (N, D_IN), dtype=jnp.float32)
        edge_index = jax.random.randint(ks[1], (2, E), 0, N, dtype=jnp.int64 if jax.config.jax_enable_x64 else jnp.int32)
        adj_v = jax.random.uniform(ks[2], (E,), dtype=jnp.float32)
        deg_v = jax.random.uniform(ks[3], (E,), dtype=jnp.float32)
        W = jax.random.normal(ks[4], (D_IN, D_OUT), dtype=jnp.float32) / np.sqrt(D_IN)
        b = jax.random.normal(ks[5], (D_OUT,), dtype=jnp.float32) * 0.01
        deg_coeff = jnp.array([0.5, 0.0], dtype=jnp.float32)
        coeff_param = jnp.zeros((3,), dtype=jnp.float32)
        scale_param = 2.0 * jnp.ones((1,), dtype=jnp.float32)
        return {'h': h, 'edge_index': edge_index, 'adj_v': adj_v, 'deg_v': deg_v, 'W': W, 'b': b, 'deg_coeff': deg_coeff, 'coeff_param': coeff_param, 'scale_param': scale_param}
    _L1_gnn_all = _L1_gnn_setup()
    _L1_gnn_in = {k: v for k, v in _L1_gnn_all.items() if k in ('W', 'b', 'deg_coeff', 'coeff_param', 'scale_param')}
    del _L1_gnn_all

    def _L2_gnn_setup():
        import jax, jax.numpy as jnp
        import numpy as np
        N_NODES = 100000
        N_EDGES = 12500
        D = 64
        H = 4
        key = jax.random.key(seed)
        k1, k2, k3, k4, k5 = jax.random.split(key, 5)
        xavier = float(np.sqrt(2.0 / (D + D)))
        all_embeddings = jax.random.normal(k1, (N_NODES, D), dtype=jnp.float32)
        Wq = jax.random.normal(k2, (D, D), dtype=jnp.float32) * xavier
        Wk = jax.random.normal(k3, (D, D), dtype=jnp.float32) * xavier
        Wv = jax.random.normal(k4, (D, D), dtype=jnp.float32) * xavier
        edge_index = jax.random.randint(k5, (2, N_EDGES), 0, N_NODES, dtype=jnp.int32)
        return {'all_embeddings': all_embeddings, 'Wq': Wq, 'Wk': Wk, 'Wv': Wv, 'edge_index': edge_index}
    _L2_gnn_all = _L2_gnn_setup()
    _L2_gnn_in = {k: v for k, v in _L2_gnn_all.items() if k in ('Wq', 'Wk', 'Wv')}
    del _L2_gnn_all

    def _L3_gnn_setup():
        import jax, jax.numpy as jnp
        import numpy as np
        NUM_NODES = 100000
        D_IN = 64
        D_OUT = 64
        NUM_EDGES = 18750
        key = jax.random.key(seed)
        k1, k2, k3, k4 = jax.random.split(key, 4)
        features = jax.random.normal(k1, (NUM_NODES, D_IN), dtype=jnp.float32)
        edge_index = jax.random.randint(k2, (2, NUM_EDGES), 0, NUM_NODES, dtype=jnp.int64)
        W = jax.random.normal(k3, (2 * D_IN, D_OUT), dtype=jnp.float32) / np.sqrt(2 * D_IN)
        b = jax.random.normal(k4, (D_OUT,), dtype=jnp.float32) * 0.01
        return {'features': features, 'edge_index': edge_index, 'W': W, 'b': b}
    _L3_gnn_all = _L3_gnn_setup()
    _L3_gnn_in = {k: v for k, v in _L3_gnn_all.items() if k in ('W', 'b')}
    del _L3_gnn_all
    return {'x': x, 'src': src, 'dst': dst, 'edge_weight': edge_weight, 'edge_weight_n2': edge_weight_n2, 'L0_gnn_W1_l': _L0_gnn_in['W1_l'], 'L0_gnn_b1': _L0_gnn_in['b1'], 'L0_gnn_W1_r': _L0_gnn_in['W1_r'], 'L0_gnn_W2_l': _L0_gnn_in['W2_l'], 'L0_gnn_b2': _L0_gnn_in['b2'], 'L0_gnn_W2_r': _L0_gnn_in['W2_r'], 'L1_gnn_W': _L1_gnn_in['W'], 'L1_gnn_b': _L1_gnn_in['b'], 'L1_gnn_deg_coeff': _L1_gnn_in['deg_coeff'], 'L1_gnn_coeff_param': _L1_gnn_in['coeff_param'], 'L1_gnn_scale_param': _L1_gnn_in['scale_param'], 'L2_gnn_Wq': _L2_gnn_in['Wq'], 'L2_gnn_Wk': _L2_gnn_in['Wk'], 'L2_gnn_Wv': _L2_gnn_in['Wv'], 'L3_gnn_W': _L3_gnn_in['W'], 'L3_gnn_b': _L3_gnn_in['b']}

def reference(x, src, dst, edge_weight, edge_weight_n2, L0_gnn_W1_l, L0_gnn_b1, L0_gnn_W1_r, L0_gnn_W2_l, L0_gnn_b2, L0_gnn_W2_r, L1_gnn_W, L1_gnn_b, L1_gnn_deg_coeff, L1_gnn_coeff_param, L1_gnn_scale_param, L2_gnn_Wq, L2_gnn_Wk, L2_gnn_Wv, L3_gnn_W, L3_gnn_b):
    import jax
    import jax.numpy as jnp

    def _L0_gnn_ref(x, edge_index, edge_weight, W1_l, b1, W1_r, W2_l, b2, W2_r):
        import jax, jax.numpy as jnp
        import numpy as np
        N = 50000
        E = 12500
        D = 64
        EPS = 1e-12
        NEG_SLOPE = 0.01

        def sage_conv(x, edge_index, W_l, b_l, W_r):
            src, dst = (edge_index[0], edge_index[1])
            n = x.shape[0]
            sums = jax.ops.segment_sum(x[src], dst, num_segments=n)
            cnt = jax.ops.segment_sum(jnp.ones((src.shape[0],), x.dtype), dst, num_segments=n)
            mean = sums / jnp.maximum(cnt, 1.0)[:, None]
            return mean @ W_l.T + b_l + x @ W_r.T
        h = sage_conv(x, edge_index, W1_l, b1, W1_r)
        h = jnp.where(h >= 0, h, NEG_SLOPE * h)
        h = sage_conv(h, edge_index, W2_l, b2, W2_r)
        norm = jnp.maximum(jnp.linalg.norm(h, axis=1, keepdims=True), EPS)
        return h / norm

    def _L1_gnn_ref(h, edge_index, adj_v, deg_v, W, b, deg_coeff, coeff_param, scale_param):
        import jax, jax.numpy as jnp
        import numpy as np
        N, E, D_IN, D_OUT = (1024, 16384, 64, 64)
        EPS = 1e-08
        n_nodes = h.shape[0]
        Wh = h @ W + b
        row, col = (edge_index[0], edge_index[1])
        sc = jax.nn.softplus(deg_coeff[0] * deg_v + deg_coeff[1])
        Wr = Wh[row]
        Wc = Wh[col]
        dot = jnp.sum(Wr * Wc, axis=-1)
        nr = jnp.sqrt(jnp.sum(Wr * Wr, axis=-1))
        nc = jnp.sqrt(jnp.sum(Wc * Wc, axis=-1))
        sim = dot / jnp.maximum(nr * nc, EPS)
        sim_pos = jax.nn.relu(sim)
        sim_neg = -jax.nn.relu(-sim)
        no_diag = (row != col).astype(Wh.dtype)
        base = adj_v * sc * no_diag
        prop_pos = jax.ops.segment_sum((base * sim_pos)[:, None] * Wc, row, num_segments=n_nodes)
        prop_neg = jax.ops.segment_sum((base * sim_neg)[:, None] * Wc, row, num_segments=n_nodes)
        coeff = jax.nn.softmax(coeff_param)
        scale = jax.nn.softplus(scale_param)
        return scale * (coeff[0] * prop_pos + coeff[1] * prop_neg + coeff[2] * Wh)

    def _L2_gnn_ref(all_embeddings, Wq, Wk, Wv, edge_index):
        import jax, jax.numpy as jnp
        import numpy as np
        N_NODES = 100000
        N_EDGES = 12500
        D = 64
        H = 4
        rows, cols = (edge_index[0], edge_index[1])
        n_nodes = all_embeddings.shape[0]
        e = rows.shape[0]
        dh = D // H
        row_emb = all_embeddings[rows]
        col_emb = all_embeddings[cols]
        q = (row_emb @ Wq).reshape(e, H, dh)
        k = (col_emb @ Wk).reshape(e, H, dh)
        v = (col_emb @ Wv).reshape(e, H, dh)
        att = jnp.einsum('ehd,ehd->eh', q, k)
        att = jnp.clip(att, -10.0, 10.0)
        exp_att = jnp.exp(att)
        att_norm = jax.ops.segment_sum(exp_att, rows, num_segments=n_nodes)
        att = exp_att / (att_norm[rows] + 1e-08)
        out_e = (att[:, :, None] * v).reshape(e, D)
        out = jax.ops.segment_sum(out_e, rows, num_segments=n_nodes)
        return out

    def _L3_gnn_ref(features, edge_index, W, b):
        import jax, jax.numpy as jnp
        import numpy as np
        NUM_NODES = 100000
        D_IN = 64
        D_OUT = 64
        NUM_EDGES = 18750
        num_nodes = features.shape[0]
        src, dst = (edge_index[0], edge_index[1])
        src_feats = features[src]
        neigh_sum = jax.ops.segment_sum(src_feats, dst, num_segments=num_nodes)
        degree = jax.ops.segment_sum(jnp.ones_like(dst, dtype=features.dtype), dst, num_segments=num_nodes)
        degree = jnp.clip(degree, 1.0)
        neigh_mean = neigh_sum / degree[:, None]
        combined = jnp.concatenate([features, neigh_mean], axis=-1)
        return combined @ W + b
    edge_index = jnp.stack([src, dst])
    x = _layernorm(x + _L0_gnn_ref(x, edge_index, edge_weight, L0_gnn_W1_l, L0_gnn_b1, L0_gnn_W1_r, L0_gnn_W2_l, L0_gnn_b2, L0_gnn_W2_r), axis=-1)
    x = _layernorm(x + _L1_gnn_ref(x, edge_index, edge_weight, edge_weight_n2, L1_gnn_W, L1_gnn_b, L1_gnn_deg_coeff, L1_gnn_coeff_param, L1_gnn_scale_param), axis=-1)
    x = _layernorm(x + _L2_gnn_ref(x, L2_gnn_Wq, L2_gnn_Wk, L2_gnn_Wv, edge_index), axis=-1)
    x = _layernorm(x + _L3_gnn_ref(x, edge_index, L3_gnn_W, L3_gnn_b), axis=-1)
    return x

_drawn_inputs = setup_inputs


def setup_inputs(seed=0):
    import zlib

    import numpy as np

    out = dict(_drawn_inputs(seed))
    spreads = {'L0_gnn_b1': (0.0, 0.377), 'L0_gnn_b2': (0.0, 0.1), 'L1_gnn_coeff_param': (0.0, 0.1)}
    factors = {'edge_weight': 3.524,
     'edge_weight_n2': 8.0,
     'L1_gnn_b': 8.0,
     'L1_gnn_deg_coeff': 8.0,
     'L3_gnn_b': 5.915}
    for name, (base, spread) in spreads.items():
        noise = np.random.default_rng([zlib.crc32(name.encode()), seed]).standard_normal(out[name].shape)
        drawn = base * np.exp(spread * noise) if base else spread * noise
        out[name] = jnp.asarray(drawn.astype(out[name].dtype))
    for name, factor in factors.items():
        out[name] = (out[name] * factor).astype(out[name].dtype)
    return out
```

```python
from contextlib import ExitStack

import concourse.bass as bass
from concourse import mybir

ALU = mybir.AluOpType
ACT = mybir.ActivationFunctionType
AX_X = mybir.AxisListType.X
F32 = mybir.dt.float32
I32 = mybir.dt.int32

P = 128
LANES = 125
D = 64
HEADS = 4
DH = D // HEADS
ROW2 = D + HEADS
G = 20
K = 16
SUB = 8
SKIP = 1 << 20
DMA = 16


def at(offset_ap):
    return bass.IndirectOffsetOnAxis(ap=offset_ap, axis=0)


class Memory:
    pass


class Phase(ExitStack):

    def __init__(self, nc, name):
        super().__init__()
        self.nc, self.name, self.sems = nc, name, []

    def sem(self, x):
        self.sems.append(self.nc.alloc_semaphore(self.name + x))
        return self.sems[-1]

    def sb(self, x, shape, dt=F32):
        return self.enter_context(self.nc.sbuf_tensor(self.name + x, shape, dt))

    def bank(self, x):
        return self.enter_context(self.nc.psum_tensor(self.name + x, [P, 512], F32))

    def block(self):
        return self.enter_context(self.nc.Block())

    def __exit__(self, *error):
        ended = super().__exit__(*error)
        if error[0] is None:
            self.nc.clear_and_free_semaphores(self.sems)
            self.nc.all_engine_barrier()
        return ended


def need(engine, sem, value):
    if not isinstance(value, int) or value > 0:
        engine.wait_ge(sem, value)


def rounds(engine, count, stages):
    last = max(lag for _, lag in stages)
    first = 2 + last + last % 2

    def straight(t):
        for f, lag in stages:
            if 0 <= t - lag < count:
                f(t - lag, (t - lag) % 2, (t - lag) // 2)

    assert count % 2 == 0 and count > first
    for t in range(first):
        straight(t)
    with engine.Fori(first // 2, count // 2) as i:
        for k in range(2):
            for f, lag in stages:
                f(2 * i + (k - lag), (k - lag) % 2, i + (k - lag) // 2)
    for t in range(count, count + last):
        straight(t)


def columns(dram):
    return dram.rearrange("(p t) d -> p t d", p=LANES)


def set_up(nc, m, w):
    name = "setup_"
    with Phase(nc, name) as ctx:
        sem, sb, bank = ctx.sem, ctx.sb, ctx.bank
        loaded, cleared, zeroed, zero_tile = sem("loaded"), sem("cleared"), sem("zeroed"), sem("zero_tile")
        vec_step, act_done = sem("vec_step"), sem("act_done")
        zw = m.tcols * D // 16
        zw2 = m.tcols * ROW2 // 16
        zero = sb("zero", [LANES, zw2])
        coef = sb("coef", [LANES, 3])
        cmax = sb("cmax", [LANES, 1])
        cexp = sb("cexp", [LANES, 3])
        csum = sb("csum", [LANES, 1])
        scp = sb("scp", [LANES, 1])
        sca = sb("sca", [LANES, 3])
        block = ctx.block()
        small = [
            (m.ident, w["ident"]), (m.before, w["before"]), (m.sgn, w["sgn"]),
            (m.deg, w["deg_coeff"].partition_broadcast(P)),
            (coef, w["coeff"].partition_broadcast(LANES)), (scp, w["scale"].partition_broadcast(LANES)),
            (m.b1, w["b1"].partition_broadcast(LANES)), (m.b2, w["b2"].partition_broadcast(LANES)),
            (m.bg, w["bg"].partition_broadcast(LANES)), (m.b3, w["b3"].partition_broadcast(LANES)),
        ]
        twice = [(m.w1r, w["w1r"]), (m.w1l, w["w1l"]), (m.w2r, w["w2r"]), (m.w2l, w["w2l"]),
                 (m.w3x, w["w3x"]), (m.w3m, w["w3m"]), (m.wg, w["wg"])]

        @block.sync
        def _(sp):
            for tile, src in small:
                sp.dma_start(tile[:, :], src).then_inc(loaded, DMA)
            sp.wait_ge(cleared, 1)
            for tile, src in twice:
                sp.dma_start(tile[0:D, 0:D], src).then_inc(loaded, DMA)
                sp.dma_start(tile[D:P, D:P], src).then_inc(loaded, DMA)
            sp.dma_start(m.wqkv[0:D, 0:D], w["wq"]).then_inc(loaded, DMA)
            sp.dma_start(m.wqkv[D:P, D:2 * D], w["wk"]).then_inc(loaded, DMA)
            sp.dma_start(m.wqkv[D:P, 2 * D:3 * D], w["wv"]).then_inc(loaded, DMA)
            sp.wait_ge(zero_tile, 1)
            sums_d = m.sum_d.rearrange("(p t) d -> p (t d)", p=LANES)
            sums_s = m.sum_s.rearrange("(p t) d -> p (t d)", p=LANES)
            for i in range(16):
                sp.dma_start(sums_d[:, i * zw:(i + 1) * zw], zero[:, 0:zw]).then_inc(zeroed, DMA)
            for i in range(16):
                sp.dma_start(sums_s[:, i * zw2:(i + 1) * zw2], zero[:, 0:zw2]).then_inc(zeroed, DMA)
            sp.wait_ge(zeroed, 32 * DMA)
            sp.wait_ge(loaded, DMA * (len(small) + 2 * len(twice) + 3))

        @block.gpsimd
        def _(pool):
            for tile, _ in twice:
                pool.memset(tile[:, :], 0.0)
            pool.memset(m.wqkv[:, :], 0.0).then_inc(cleared, 1)
            pool.memset(m.ones[:, :], 1.0)
            pool.memset(zero[:, :], 0.0).then_inc(zero_tile, 1)

        @block.scalar
        def _(act):
            act.wait_ge(vec_step, 2)
            act.activation(cexp[:, :], cexp[:, :], ACT.Exp).then_inc(act_done, 1)
            act.activation(sca[:, 0:1], scp[:, :], ACT.Abs).then_inc(act_done, 1)
            act.wait_ge(act_done, 2)
            act.activation(sca[:, 1:2], sca[:, 0:1], ACT.Exp, scale=-1.0).then_inc(act_done, 1)
            act.wait_ge(act_done, 3)
            act.activation(sca[:, 2:3], sca[:, 1:2], ACT.Ln, bias=1.0).then_inc(act_done, 1)

        @block.vector
        def _(vec):
            vec.wait_ge(loaded, DMA * (len(small) + 2 * len(twice) + 3))
            vec.tensor_reduce(cmax[:, :], coef[:, :], AX_X, ALU.max).then_inc(vec_step, 1)
            vec.wait_ge(vec_step, 1)
            vec.tensor_scalar(cexp[:, :], coef[:, :], cmax[:, 0:1], None, ALU.subtract).then_inc(vec_step, 1)
            vec.wait_ge(act_done, 1)
            vec.tensor_reduce(csum[:, :], cexp[:, :], AX_X, ALU.add).then_inc(vec_step, 1)
            vec.wait_ge(vec_step, 3)
            vec.reciprocal(csum[:, :], csum[:, :]).then_inc(vec_step, 1)
            vec.wait_ge(act_done, 4)
            vec.scalar_tensor_tensor(out=scp[:, :], in0=scp[:, :], scalar=0.0, in1=sca[:, 2:3],
                                     op0=ALU.max, op1=ALU.add).then_inc(vec_step, 1)
            vec.wait_ge(vec_step, 5)
            vec.tensor_scalar(m.mix[:, :], cexp[:, :], csum[:, 0:1], scp[:, 0:1], ALU.mult, ALU.mult)


def sort_edges(nc, m, name, key_in, other_in, weights, key_out, other_out, base_out):
    E = key_in.shape[0]
    n = P * P
    while n < E:
        n *= 2
    W = n // P
    LW = W.bit_length() - 1
    LN_ = n.bit_length() - 1
    blocks = W // P
    full, rest = E // W, E % W
    with Phase(nc, name) as ctx:
        sem, sb, bank = ctx.sem, ctx.sb, ctx.bank
        loaded, prepared, act_done, vec_step = sem("loaded"), sem("prepared"), sem("act_done"), sem("vec_step")
        swapped, copied, turned, stored = sem("swapped"), sem("copied"), sem("turned"), sem("stored")
        padded, flipped = sem("padded"), sem("flipped")
        ki, oi = sb("ki", [P, W], I32), sb("oi", [P, W], I32)
        wa, wb = sb("wa", [P, W]), sb("wb", [P, W])
        z, az = sb("z", [P, W]), sb("az", [P, W])
        key = [sb(f"key{i}", [P, W]) for i in range(2)]
        load = [sb(f"load{i}", [P, 2, W]) for i in range(2)]
        mask = sb("mask", [P, W // 2], I32)
        ps = [ctx.enter_context(nc.psum_tensor(f"{name}ps{i}", [P, W], F32)) for i in range(3)]
        block = ctx.block()
        steps = []
        for k in range(1, LN_ + 1):
            steps.append(("flip", k))
            j = k - 1
            if j >= LW:
                steps.append(("turn",))
                while j >= LW:
                    steps.append(("swap", 1 << (j - LW)))
                    j -= 1
                steps.append(("turn",))
            while j >= 0:
                steps.append(("swap", 1 << j))
                j -= 1

        def halves(ap, stride):
            v = ap.rearrange("p (a two r) -> p a two r", two=2, r=stride)
            return v[:, :, 0, :], v[:, :, 1, :]

        def halves2(ap, stride):
            v = ap.rearrange("p l (a two r) -> p l a two r", two=2, r=stride)
            return v, None

        ints = [(ki, key_in), (oi, other_in)]
        floats = [(wa, weights[0]), (wb, weights[1])] if weights else []

        @block.sync
        def _(sp):
            sp.wait_ge(padded, 2 + len(floats))
            for tile, src in ints + floats:
                sp.dma_start(tile[0:full, :], src[0:full * W].rearrange("(p c) -> p c", p=full)).then_inc(loaded, DMA)
                if rest:
                    sp.dma_start(tile[full:full + 1, 0:rest], src[full * W:E].rearrange("(p c) -> p c", p=1)).then_inc(loaded, DMA)
            sp.wait_ge(prepared, 2)
            outs = [(ki, key_out), (oi, other_out)] + ([(wa, base_out)] if weights else [])
            for tile, dst in outs:
                sp.dma_start(dst[0:full * W].rearrange("(p c) -> p c", p=full), tile[0:full, :]).then_inc(stored, DMA)
                if rest:
                    sp.dma_start(dst[full * W:E].rearrange("(p c) -> p c", p=1), tile[full:full + 1, 0:rest]).then_inc(stored, DMA)
            sp.wait_ge(stored, DMA * len(outs) * (2 if rest else 1))

        @block.gpsimd
        def _(pool):
            pool.memset(ki[:, :], SKIP).then_inc(padded, 1)
            pool.memset(oi[:, :], 0).then_inc(padded, 1)
            for tile, _ in floats:
                pool.memset(tile[:, :], 0.0).then_inc(padded, 1)

        n_loads = (2 + len(floats)) * (2 if rest else 1)

        @block.scalar
        def _(act):
            if weights:
                act.wait_ge(vec_step, 1)
                act.activation(az[:, :], z[:, :], ACT.Abs).then_inc(act_done, 1)
                act.wait_ge(act_done, 1)
                act.activation(az[:, :], az[:, :], ACT.Exp, scale=-1.0).then_inc(act_done, 1)
                act.wait_ge(act_done, 2)
                act.activation(az[:, :], az[:, :], ACT.Ln, bias=1.0).then_inc(act_done, 1)
            act.wait_ge(prepared, 1)
            cur, swaps, turns = 0, 0, 0
            for s in steps:
                if s[0] == "swap":
                    if swaps:
                        act.wait_ge(swapped, 3 * swaps)
                    if turns:
                        act.wait_ge(copied, turns)
                    act.copy(load[1 - cur][:, :, :], load[cur][:, :, :]).then_inc(act_done, 1)
                    cur, swaps = 1 - cur, swaps + 1
                elif s[0] == "turn":
                    turns += 1

        @block.tensor
        def _(pe):
            cur, swaps, turns, flips = 0, 0, 0, 0
            pe.wait_ge(prepared, 1)
            for s in steps:
                if s[0] == "swap":
                    cur, swaps = 1 - cur, swaps + 1
                elif s[0] == "flip":
                    flips += 1
                else:
                    pe.wait_ge(swapped, 3 * swaps)
                    if turns % 2 == 0:
                        pe.wait_ge(flipped, flips)
                    if turns:
                        pe.wait_ge(copied, turns)
                    for b in range(blocks):
                        c = slice(b * P, (b + 1) * P)
                        pe.transpose(ps[0][:, c], key[cur][:, c], m.ident[:, :])
                        pe.transpose(ps[1][:, c], load[cur][:, 0, c], m.ident[:, :])
                        t = pe.transpose(ps[2][:, c], load[cur][:, 1, c], m.ident[:, :])
                    t.then_inc(turned, 1)
                    turns += 1

        @block.vector
        def _(vec):
            vec.wait_ge(loaded, DMA * n_loads)
            if weights:
                vec.tensor_scalar(z[:, :], wb[:, :], m.deg[:, 0:1], m.deg[:, 1:2], ALU.mult, ALU.add).then_inc(vec_step, 1)
                vec.wait_ge(act_done, 3)
                vec.wait_ge(vec_step, 1)
                vec.scalar_tensor_tensor(out=z[:, :], in0=z[:, :], scalar=0.0, in1=az[:, :],
                                         op0=ALU.max, op1=ALU.add).then_inc(vec_step, 1)
                vec.wait_ge(vec_step, 2)
                vec.tensor_tensor(z[:, :], z[:, :], wa[:, :], ALU.mult).then_inc(vec_step, 1)
                vec.tensor_tensor(az[:, :], ki[:, :], oi[:, :], ALU.not_equal).then_inc(vec_step, 1)
                vec.wait_ge(vec_step, 4)
                vec.tensor_tensor(load[0][:, 1, :], z[:, :], az[:, :], ALU.mult)
            else:
                vec.memset(load[0][:, 1, :], 0.0)
            vec.tensor_copy(key[0][:, :], ki[:, :])
            vec.tensor_copy(load[0][:, 0, :], oi[:, :]).then_inc(prepared, 1)
            vec.wait_ge(prepared, 1)
            cur, swaps, turns, flips = 0, 0, 0, 0
            base_act = 3 if weights else 0
            for s in steps:
                a = key[cur]
                if s[0] == "flip":
                    k = s[1]
                    if swaps:
                        vec.wait_ge(swapped, 3 * swaps)
                    if k < LW:
                        if k == 1:
                            v = a[:, :].rearrange("p (a two r) -> p a two r", two=2, r=2)
                            parts = [v[:, :, 1, :]]
                        else:
                            v = a[:, :].rearrange("p (a x y r) -> p a x y r", x=2, y=2, r=1 << (k - 1))
                            parts = [v[:, :, 0, 1, :], v[:, :, 1, 0, :]]
                        for q in parts:
                            ins = vec.tensor_scalar(q, q, -1.0, None, ALU.mult)
                        ins.then_inc(flipped, 1)
                    elif k == LW:
                        h = a[:, W // 2:W]
                        lo = a[:, 0:W // 2]
                        vec.tensor_scalar(lo, lo, m.sgn[:, 0:1], None, ALU.mult)
                        vec.tensor_scalar(h, h, m.sgn[:, 0:1], -1.0, ALU.mult, ALU.mult).then_inc(flipped, 1)
                    else:
                        vec.tensor_scalar(a[:, :], a[:, :], m.sgn[:, k - LW:k - LW + 1], None, ALU.mult).then_inc(flipped, 1)
                    flips += 1
                    flipped_now = True
                elif s[0] == "turn":
                    vec.wait_ge(turned, turns + 1)
                    vec.tensor_copy(key[cur][:, :], ps[0][:, :])
                    vec.tensor_copy(load[cur][:, 0, :], ps[1][:, :])
                    vec.tensor_copy(load[cur][:, 1, :], ps[2][:, :]).then_inc(copied, 1)
                    turns += 1
                else:
                    lo, hi = halves(key[cur][:, :], s[1])
                    nlo, nhi = halves(key[1 - cur][:, :], s[1])
                    mk = mask[:, :].rearrange("p (a r) -> p a r", r=s[1])
                    if swaps:
                        vec.wait_ge(swapped, 3 * swaps)
                    vec.wait_ge(flipped, flips)
                    if turns:
                        vec.wait_ge(copied, turns)
                    vec.tensor_tensor(mk, lo, hi, ALU.is_gt).then_inc(vec_step, 1)
                    vec.tensor_tensor(nlo, lo, hi, ALU.min)
                    vec.tensor_tensor(nhi, lo, hi, ALU.max).then_inc(swapped, 1)
                    vec.wait_ge(act_done, base_act + swaps + 1)
                    vec.wait_ge(vec_step, (4 if weights else 0) + swaps + 1)
                    for l in range(2):
                        plo, phi = halves(load[cur][:, l, :], s[1])
                        qlo, qhi = halves(load[1 - cur][:, l, :], s[1])
                        vec.copy_predicated(qlo, mk, phi)
                        vec.copy_predicated(qhi, mk, plo).then_inc(swapped, 1)
                    cur, swaps = 1 - cur, swaps + 1
            vec.wait_ge(swapped, 3 * swaps)
            vec.tensor_copy(ki[:, :], key[cur][:, :])
            vec.tensor_copy(wa[:, :], load[cur][:, 1, :])
            vec.tensor_copy(oi[:, :], load[cur][:, 0, :]).then_inc(prepared, 1)


def edge_plan(nc, m, name, key_dram, columns_f, plan, fields, carry_mask, fix_idx, fix_inv):
    EC = m.ecols
    with Phase(nc, name) as ctx:
        sem, sb, bank = ctx.sem, ctx.sb, ctx.bank
        loaded, step, turned, next_set = sem("loaded"), sem("step"), sem("turned"), sem("next_set")
        ki = sb("ki", [LANES, EC], I32)
        nxt_i, nxt = sb("nxt_i", [LANES, 1], I32), sb("nxt", [LANES, 1])
        key, same, on = sb("key", [LANES, EC]), sb("same", [LANES, EC]), sb("on", [LANES, EC])
        ones, cnt, first = sb("ones", [LANES, EC]), sb("cnt", [LANES, EC]), sb("first", [LANES, EC])
        bc = sb("bc", [LANES, LANES])
        t1, t2, t3 = sb("t1", [LANES, 1]), sb("t2", [LANES, 1]), sb("t3", [LANES, 1])
        others = {f: sb("in_" + f, [LANES, EC], dt) for f, (_, dt) in columns_f.items()}
        psb = bank("psb")
        psc = bank("psc")
        block = ctx.block()
        lanes = lambda d: d[0:LANES * EC].rearrange("(p c) -> p c", p=LANES)
        field = lambda f: plan[:, :, fields.index(f), :]
        by_chunk = lambda t: t[:, :].rearrange("p (c g) -> p c g", g=G)

        @block.sync
        def _(sp):
            sp.dma_start(ki[:, :], lanes(key_dram)).then_inc(loaded, DMA)
            for f, (src, _) in columns_f.items():
                sp.dma_start(others[f][:, :], lanes(src)).then_inc(loaded, DMA)
            sp.wait_ge(next_set, 1)
            sp.dma_start(nxt_i[0:LANES - 1, :], lanes(key_dram)[1:LANES, 0:1],
                         allow_slow_non_contiguous=True).then_inc(loaded, DMA)

        @block.vector
        def _(vec):
            count = 0

            def did(ins):
                nonlocal count
                ins.then_inc(step, 1)
                count += 1
                vec.wait_ge(step, count)

            vec.memset(nxt_i[:, :], -1).then_inc(next_set, 1)
            vec.memset(same[:, 0:1], 0.0)
            did(vec.memset(ones[:, :], 1.0))
            vec.wait_ge(loaded, DMA * (2 + len(columns_f)))
            vec.tensor_copy(nxt[:, :], nxt_i[:, :])
            did(vec.tensor_copy(key[:, :], ki[:, :]))
            vec.tensor_tensor(same[:, 1:EC], key[:, 1:EC], key[:, 0:EC - 1], ALU.is_equal)
            vec.tensor_tensor(on[:, 0:EC - 1], key[:, 1:EC], key[:, 0:EC - 1], ALU.is_equal)
            vec.tensor_tensor(on[:, EC - 1:EC], key[:, EC - 1:EC], nxt[:, :], ALU.is_equal)
            vec.tensor_scalar(first[:, :], key[:, :], key[:, 0:1], None, ALU.is_equal)
            vec.tensor_tensor(t1[:, :], key[:, 0:1], key[:, EC - 1:EC], ALU.is_equal)
            did(vec.tensor_scalar(bc[:, :], m.ones[0:LANES, 0:LANES], key[:, 0:1], None, ALU.mult))
            vec.scalar_tensor_tensor(out=field("to"), in0=by_chunk(on), scalar=float(SKIP), in1=by_chunk(key),
                                     op0=ALU.mult, op1=ALU.add)
            vec.tensor_copy(field("same"), by_chunk(same))
            for f, tile in others.items():
                vec.tensor_copy(field(f), by_chunk(tile))
            vec.tensor_tensor_scan(cnt[:, :], same[:, :], ones[:, :], 0.0, ALU.mult, ALU.add)
            did(vec.tensor_tensor(t1[:, :], t1[:, :], on[:, EC - 1:EC], ALU.mult))
            did(vec.scalar_tensor_tensor(out=t2[:, :], in0=t1[:, :], scalar=float(SKIP), in1=key[:, 0:1],
                                         op0=ALU.mult, op1=ALU.add))
            vec.tensor_copy(fix_idx[:, :], t2[:, :])
            vec.wait_ge(turned, 1)
            did(vec.scalar_tensor_tensor(out=carry_mask[:, :], in0=psb[0:LANES, 0:LANES], scalar=key[:, EC - 1:EC],
                                         in1=m.before[:, :], op0=ALU.is_equal, op1=ALU.mult))
            vec.wait_ge(turned, 2)
            did(vec.tensor_copy(t3[:, :], psc[0:LANES, 0:1]))
            did(vec.scalar_tensor_tensor(out=cnt[:, :], in0=first[:, :], scalar=t3[:, 0:1], in1=cnt[:, :],
                                         op0=ALU.mult, op1=ALU.add))
            vec.tensor_reduce(t1[:, :], first[:, :], AX_X, ALU.add)
            did(vec.reciprocal(cnt[:, :], cnt[:, :]))
            did(vec.tensor_tensor(t1[:, :], t1[:, :], t3[:, :], ALU.add))
            if fix_inv is not None:
                vec.tensor_copy(field("inv"), by_chunk(cnt))
                did(vec.reciprocal(fix_inv[:, :], t1[:, :]))

        @block.tensor
        def _(pe):
            pe.wait_ge(step, 3)
            pe.transpose(psb[0:LANES, 0:LANES], bc[:, :], m.ident[0:LANES, 0:LANES]).then_inc(turned, 1)
            pe.wait_ge(step, 6)
            pe.matmul(psc[0:LANES, 0:1], carry_mask[:, :], cnt[:, EC - 1:EC], start=True, stop=True).then_inc(turned, 1)


def edge_phase(nc, m, name, kind, tables, plan, fields, sums, carry_mask, fix_idx, fix_inv=None):
    NCH = m.ecols // G
    NI = NCH // 2
    NF = len(fields)
    NG = fields.index("to")
    NS = NF - NG - 1
    flag = lambda f: fields.index(f) - NG - 1
    W = tables[0].shape[1]
    mean, cosine, heads = kind == "mean", kind == "cosine", kind == "heads"
    width = D if mean else ROW2
    SW = ROW2 if heads else D
    GATHERED = DMA * G * NG
    SCATTERED = DMA * G
    QC = 4
    T = G // QC
    with Phase(nc, name) as ctx:
        sem, sb, bank = ctx.sem, ctx.sb, ctx.bank
        gathered = [sem("gathered0"), sem("gathered1")]
        scattered = [sem("scattered0"), sem("scattered1")]
        from_ready, flags_ready, rows_used, scan = sem("from_ready"), sem("flags_ready"), sem("rows_used"), sem("scan")
        fixed, fix_in, fix_out, carried, fix_clear = sem("fixed"), sem("fix_in"), sem("fix_out"), sem("carried"), sem("fix_clear")
        idx_from = sb("idx_from", [LANES, 2, NG, G], I32)
        idx_to = sb("idx_to", [LANES, 2, G], I32)
        flags = sb("flags", [LANES, 2, NS, G])
        rows = sb("rows", [LANES, 2, G, NG * W])
        out = sb("out", [LANES, 2, G, width])
        fix = sb("fix", [LANES, width])
        chain = sb("chain", [LANES, 2, G, D]) if mean else out
        source = rows if mean else out
        ps_c = bank("ps_c")
        begun = sem("begun")
        if mean:
            scaled = sem("scaled")
        else:
            step, act_math = sem("step"), sem("act_math")
        if cosine:
            sq_read = sem("sq_read")
            prod, sq = sb("prod", [LANES, G, D]), sb("sq", [LANES, 2, G, D])
            dot, nrm, sim, att = sb("dot", [LANES, G]), sb("nrm", [LANES, 2, G]), sb("sim", [LANES, 2, G]), sb("att", [LANES, G])
        if heads:
            turned, turned_copied, projected, proj_copied, proj_used = sem("turned"), sem("turned_copied"), sem("projected"), sem("proj_copied"), sem("proj_used")
            prod = sb("prod", [LANES, G, D])
            att, wts = sb("att", [LANES, G * HEADS]), sb("wts", [LANES, G * HEADS])
            turned_rows = sb("turned_rows", [P, 2, QC * LANES])
            qkv = sb("qkv", [LANES, 2, G, 3 * D])
            ps_t = [bank("ps_t0"), bank("ps_t1")]
            ps_q = [bank(f"ps_q{i}") for i in range(4)]
        block = ctx.block()

        @block.gpsimd
        def _(pool):
            def gathers(c, h, u):
                need(pool, from_ready, c + 1)
                need(pool, rows_used, c - 1)
                pool.sem_inc(begun)
                for g in range(NG):
                    for j in range(G):
                        pool.indirect_dma_start(out=rows[:, h, j, g * W:(g + 1) * W], out_offset=None,
                                                in_=tables[g], in_offset=at(idx_from[:, h, g, j:j + 1])
                                                ).then_inc(gathered[h], DMA)

            def scatters(c, h, u):
                need(pool, flags_ready, c + 1)
                if mean:
                    need(pool, scaled, c + 1)
                else:
                    need(pool, scan, G * c + G + 1)
                pool.sem_inc(begun)
                for j in range(G):
                    pool.indirect_dma_start(out=sums, out_offset=at(idx_to[:, h, j:j + 1]), in_=out[:, h, j, :],
                                            in_offset=None, bounds_check=m.nodes - 1, oob_is_err=False
                                            ).then_inc(scattered[h], DMA)

            pool.memset(fix[:, :], 0.0).then_inc(fix_clear, 1)
            rounds(pool, NCH, [(gathers, 0), (scatters, 1)])
            for h in range(2):
                pool.wait_ge(scattered[h], SCATTERED * NI)
            pool.wait_ge(fix_clear, 1)
            pool.indirect_dma_start(out=fix[:, :], out_offset=None, in_=sums, in_offset=at(fix_idx[:, 0:1]),
                                    bounds_check=m.nodes - 1, oob_is_err=False).then_inc(fix_in, DMA)
            pool.wait_ge(fixed, 1)
            pool.indirect_dma_start(out=sums, out_offset=at(fix_idx[:, 0:1]), in_=fix[:, :], in_offset=None,
                                    bounds_check=m.nodes - 1, oob_is_err=False).then_inc(fix_out, DMA)
            pool.wait_ge(fix_out, DMA)

        @block.scalar
        def _(act):
            def stage_from(c, h, u):
                need(act, gathered[h], GATHERED * u)
                act.copy(idx_from[:, h, :, :], plan[:, c, 0:NG, :]).then_inc(from_ready, 1)

            def stage_flags(c, h, u):
                need(act, scattered[h], SCATTERED * u)
                act.copy(idx_to[:, h, :], plan[:, c, NG, :])
                act.copy(flags[:, h, :, :], plan[:, c, NG + 1:NF, :]).then_inc(flags_ready, 1)

            def copy_projections(c, h, q):
                for n in (2 * q, 2 * q + 1):
                    need(act, projected, 2 * T * c + n + 1)
                    if n == 0:
                        need(act, proj_used, c - 1)
                    act.copy(qkv[:, h, 2 * n:2 * n + 2, :],
                             ps_q[(2 * T * h + n) % 4][0:LANES, :].rearrange("p (a b) -> p a b", a=2)[:, :, 0:3 * D]
                             ).then_inc(proj_copied, 1)

            def lengths(c, h, u):
                need(act, gathered[h], GATHERED * (u + 1))
                need(act, sq_read, c)
                for e in range(2):
                    ins = act.activation(sq[:, e, :, :], rows[:, h, :, e * W + D:(e + 1) * W], ACT.Square)
                ins.then_inc(act_math, 1)
                need(act, sq_read, c + 1)
                act.activation(nrm[:, :, :], nrm[:, :, :], ACT.Sqrt).then_inc(act_math, 1)

            def projections(c, h, u):
                for q in range(T):
                    need(act, turned, T * c + q + 1)
                    need(act, projected, 2 * (T * c + q - 1))
                    act.copy(turned_rows[:, (T * h + q) % 2, :], ps_t[(T * h + q) % 2][:, 0:QC * LANES]).then_inc(turned_copied, 1)
                    if q:
                        copy_projections(c, h, q - 1)
                copy_projections(c, h, T - 1)
                need(act, step, 5 * c + 3)
                act.activation(wts[:, :], att[:, :], ACT.Exp).then_inc(act_math, 1)

            own = [(lengths, 0)] if cosine else [(projections, 0)] if heads else []
            rounds(act, NCH, [(stage_from, 0), (stage_flags, 0)] + own)

        @block.tensor
        def _(pe):
            def turn(c, h, q):
                need(pe, turned_copied, T * c + q - 1)
                for r in range(QC):
                    ins = pe.transpose(ps_t[(T * h + q) % 2][:, r * LANES:(r + 1) * LANES], rows[:, h, QC * q + r, :],
                                       m.ident[0:LANES, 0:LANES])
                ins.then_inc(turned, 1)

            def project(c, h, q):
                need(pe, turned_copied, T * c + q + 1)
                for n in (2 * q, 2 * q + 1):
                    need(pe, proj_copied, 2 * T * c + n - 3)
                    for r in range(2):
                        col = (n % 2) * 2 + r
                        ins = pe.matmul(ps_q[(2 * T * h + n) % 4][0:LANES, r * 256:r * 256 + 3 * D],
                                        turned_rows[:, (T * h + q) % 2, col * LANES:(col + 1) * LANES],
                                        m.wqkv[:, :], start=True, stop=True)
                    ins.then_inc(projected, 1)

            def project_chunk(c, h, u):
                need(pe, gathered[h], GATHERED * (u + 1))
                turn(c, h, 0)
                for q in range(1, T):
                    turn(c, h, q)
                    project(c, h, q - 1)
                need(pe, turned, T * (c + 1))
                pe.nop().then_inc(rows_used, 1)
                project(c, h, T - 1)

            if heads:
                rounds(pe, NCH, [(project_chunk, 0)])
            pe.wait_ge(scan, G * NCH + 1)
            pe.matmul(ps_c[0:LANES, 0:SW], carry_mask[:, :], chain[:, 1, G - 1, 0:SW], start=True, stop=True).then_inc(carried, 1)

        @block.vector
        def _(vec):
            STEPS = {"mean": 0, "cosine": 9, "heads": 5}[kind]

            def messages(c, h, u):
                n = 0

                def did(ins):
                    nonlocal n
                    n += 1
                    ins.then_inc(step, 1)
                    need(vec, step, STEPS * c + n)

                if cosine:
                    wr, wc = rows[:, h, :, D:2 * D], rows[:, h, :, 3 * D:4 * D]
                    did(vec.tensor_tensor(prod[:, :, :], wr, wc, ALU.mult))
                    vec.tensor_reduce(dot[:, :], prod[:, :, :], AX_X, ALU.add)
                    vec.wait_ge(act_math, 2 * c + 1)
                    vec.tensor_reduce(nrm[:, :, :], sq[:, :, :, :], AX_X, ALU.add).then_inc(sq_read, 1)
                    vec.wait_ge(act_math, 2 * c + 2)
                    did(vec.tensor_tensor(att[:, :], nrm[:, 0, :], nrm[:, 1, :], ALU.mult))
                    did(vec.tensor_scalar(att[:, :], att[:, :], 1e-8, None, ALU.max))
                    did(vec.reciprocal(att[:, :], att[:, :]))
                    did(vec.tensor_tensor(dot[:, :], dot[:, :], att[:, :], ALU.mult))
                    vec.tensor_scalar(sim[:, 0, :], dot[:, :], 0.0, m.mix[:, 0:1], ALU.max, ALU.mult)
                    did(vec.tensor_scalar(sim[:, 1, :], dot[:, :], 0.0, m.mix[:, 1:2], ALU.min, ALU.mult))
                    did(vec.tensor_tensor(att[:, :], sim[:, 0, :], sim[:, 1, :], ALU.add))
                    did(vec.tensor_tensor(att[:, :], att[:, :], flags[:, h, flag("base"), :], ALU.mult))
                    need(vec, scattered[h], SCATTERED * u)
                    did(vec.tensor_tensor(out[:, h, :, 0:D], wc, att[:, :].unsqueeze(2).to_broadcast([LANES, G, D]), ALU.mult))
                    vec.nop().then_inc(rows_used, 1)
                if heads:
                    vec.wait_ge(proj_copied, 2 * T * (c + 1))
                    did(vec.tensor_tensor(prod[:, :, :], qkv[:, h, :, 0:D], qkv[:, h, :, D:2 * D], ALU.mult))
                    did(vec.tensor_reduce(att[:, :], prod[:, :, :].rearrange("p g (a d) -> p (g a) d", a=HEADS), AX_X, ALU.add))
                    did(vec.tensor_scalar(att[:, :], att[:, :], 10.0, -10.0, ALU.min, ALU.max))
                    vec.wait_ge(act_math, c + 1)
                    need(vec, scattered[h], SCATTERED * u)
                    did(vec.tensor_copy(out[:, h, :, D:ROW2], wts[:, :].rearrange("p (g a) -> p g a", a=HEADS)))
                    did(vec.tensor_copy(prod[:, :, :].rearrange("p g (a d) -> p (g a) d", a=HEADS),
                                        wts[:, :].unsqueeze(2).to_broadcast([LANES, G * HEADS, DH])))
                    vec.tensor_tensor(out[:, h, :, 0:D], qkv[:, h, :, 2 * D:3 * D], prod[:, :, :], ALU.mult).then_inc(proj_used, 1)
                    vec.wait_ge(proj_used, c + 1)
                assert n == STEPS, n

            def chunk(c, h, u):
                need(vec, gathered[h], GATHERED * (u + 1))
                vec.wait_ge(flags_ready, c + 1)
                messages(c, h, u)
                for j in range(G):
                    prev = chain[:, 1 - h, G - 1, 0:SW] if j == 0 else chain[:, h, j - 1, 0:SW]
                    vec.wait_ge(scan, G * c + j + 1)
                    vec.scalar_tensor_tensor(out=chain[:, h, j, 0:SW], in0=prev, scalar=flags[:, h, flag("same"), j:j + 1],
                                             in1=source[:, h, j, 0:SW], op0=ALU.mult, op1=ALU.add).then_inc(scan, 1)
                if mean:
                    vec.wait_ge(scan, G * c + G + 1)
                    vec.nop().then_inc(rows_used, 1)
                    need(vec, scattered[h], SCATTERED * u)
                    vec.tensor_tensor(out[:, h, :, :], chain[:, h, :, :],
                                      flags[:, h, flag("inv"), :].unsqueeze(2).to_broadcast([LANES, G, D]), ALU.mult
                                      ).then_inc(scaled, 1)

            if not mean:
                vec.memset(out[:, 0, :, :], 0.0)
            vec.memset(chain[:, 1, :, :], 0.0).then_inc(scan, 1)
            rounds(vec, NCH, [(chunk, 0)])
            vec.wait_ge(fix_in, DMA)
            vec.wait_ge(carried, 1)
            if mean:
                vec.scalar_tensor_tensor(out=fix[:, 0:SW], in0=ps_c[0:LANES, 0:SW], scalar=fix_inv[:, 0:1], in1=fix[:, 0:SW],
                                         op0=ALU.mult, op1=ALU.add).then_inc(fixed, 1)
            else:
                vec.tensor_tensor(fix[:, 0:SW], ps_c[0:LANES, 0:SW], fix[:, 0:SW], ALU.add).then_inc(fixed, 1)


def node_phase(nc, m, name, kind, loads, weights, bias, dst):
    NCH = m.tcols // K
    relu, unit, cosine, heads, plain = (kind == k for k in ("relu", "unit", "cosine", "heads", "plain"))
    products = relu or unit or plain
    S = K // SUB
    PAIRS = SUB // 2
    ow = dst.shape[1]
    LOADED = DMA * 2
    with Phase(nc, name) as ctx:
        sem, sb, bank = ctx.sem, ctx.sb, ctx.bank
        loaded, stored = [sem("loaded0"), sem("loaded1")], [sem("stored0"), sem("stored1")]
        out_ready = sem("out_ready")
        if products:
            turned, turned_copied, multiplied, evacuated = sem("turned"), sem("turned_copied"), sem("multiplied"), sem("evacuated")
            tcp = sb("tcp", [P, 2, 2, PAIRS, LANES])
            ps_t = [[bank(f"ps_t{b}{e}") for e in range(2)] for b in range(2)]
            ps_o = [bank("ps_o0"), bank("ps_o1")]
        tin = [sb(f"in{n}", [LANES, 2, K, t.shape[1]]) for n, t in enumerate(loads)]
        out = sb("out", [LANES, 2, K, ow])
        raw = sb("raw", [LANES, 2, K, D])
        if not relu:
            raw_ready, xs_ready, var_ready, rooted = sem("raw_ready"), sem("xs_ready"), sem("var_ready"), sem("rooted")
            rstd_ready, xn_ready, x_ready, step, fin = sem("rstd_ready"), sem("xn_ready"), sem("x_ready"), sem("step"), sem("fin")
            xs, xn = sb("xs", [LANES, 2, K, D]), sb("xn", [LANES, 2, K, D])
            st = sb("st", [LANES, 2, K, nc.vector.BN_STATS_DIM])
            msum, mdif, var = sb("msum", [LANES, 2, K]), sb("mdif", [LANES, K]), sb("var", [LANES, 2, K])
            rstd, shift = sb("rstd", [LANES, 2, K]), sb("shift", [LANES, 2, K])
            eps = sb("eps", [LANES, 1])
        if unit:
            x_loaded = [sem("x_loaded0"), sem("x_loaded1")]
            squared, length_sq, length, unit_ready, unit_step, scaled = sem("squared"), sem("length_sq"), sem("length"), sem("unit_ready"), sem("unit_step"), sem("scaled")
            xturned, xturned_copied, wh_done, wh_out = sem("xturned"), sem("xturned_copied"), sem("wh_done"), sem("wh_out")
            sq, ss, rlen = sb("sq", [LANES, K, D]), sb("ss", [LANES, 2, K]), sb("rlen", [LANES, 2, K])
            x_new, x_copied = sb("x_new", [LANES, 2, K, D]), sem("x_copied")
            xt = sb("xt", [P, PAIRS * LANES])
            ps_x, ps_w = bank("ps_x"), bank("ps_w")
        if heads:
            rden, rden_step, divided = sb("rden", [LANES, 2, K * HEADS]), sem("rden_step"), sem("divided")
        block = ctx.block()
        in_cols = [columns(t) for t in loads]
        out_cols = columns(dst)
        wide = lambda t, h: t[:, h, :].unsqueeze(2).to_broadcast([LANES, K, D])
        LAG = 5 if unit else 2 if relu else 3

        @block.sync
        def _(sp):
            def load(c, h, u):
                if products:
                    need(sp, turned, S * (c - 1))
                if not relu and not unit:
                    need(sp, xs_ready, c - 1)
                for t, cols in zip(tin[0:2], in_cols):
                    sp.dma_start(t[:, h, :, :], cols[:, bass.ds(c * K, K), :]).then_inc(loaded[h], DMA)

            def load_x(c, h, u):
                need(sp, xs_ready, c - 1)
                sp.dma_start(tin[2][:, h, :, :], in_cols[2][:, bass.ds(c * K, K), :]).then_inc(x_loaded[h], DMA)

            def store(c, h, u):
                need(sp, out_ready, (S if unit else 1) * (c + 1))
                sp.dma_start(out_cols[:, bass.ds(c * K, K), :], out[:, h, :, :]).then_inc(stored[h], DMA)

            rounds(sp, NCH, [(load, 0)] + ([(load_x, 1)] if unit else []) + [(store, LAG)])
            for h in range(2):
                sp.wait_ge(stored[h], DMA * (NCH // 2))

        @block.tensor
        def _(pe):
            def turn(s):
                def stage(c, h, u):
                    need(pe, loaded[h], LOADED * (u + 1))
                    need(pe, turned_copied, S * c + s - 1)
                    for e in range(2):
                        for q in range(PAIRS):
                            col = SUB * s + 2 * q
                            ins = pe.transpose(ps_t[s % 2][e][:, q * LANES:(q + 1) * LANES],
                                               tin[e][:, h, col:col + 2, :].rearrange("p a d -> p (a d)"),
                                               m.ident[0:LANES, 0:LANES])
                    ins.then_inc(turned, 1)
                return stage

            def multiply(s):
                def stage(c, h, u):
                    need(pe, turned_copied, S * c + s + 1)
                    need(pe, evacuated, S * c + s - 1)
                    for q in range(PAIRS):
                        for e in range(2):
                            ins = pe.matmul(ps_o[s % 2][0:LANES, q * P:(q + 1) * P], tcp[:, s % 2, e, q, :],
                                            weights[e][:, :], start=(e == 0), stop=(e == 1))
                    ins.then_inc(multiplied, 1)
                return stage

            def turn_x(s):
                def stage(c, h, u):
                    need(pe, x_ready, c + 1)
                    need(pe, xturned_copied, S * c + s)
                    for q in range(PAIRS):
                        col = SUB * s + 2 * q
                        ins = pe.transpose(ps_x[:, q * LANES:(q + 1) * LANES],
                                           x_new[:, h, col:col + 2, :].rearrange("p a d -> p (a d)"),
                                           m.ident[0:LANES, 0:LANES])
                    ins.then_inc(xturned, 1)
                return stage

            def multiply_x(s):
                def stage(c, h, u):
                    need(pe, xturned_copied, S * c + s + 1)
                    need(pe, wh_out, S * c + s)
                    for q in range(PAIRS):
                        ins = pe.matmul(ps_w[0:LANES, q * P:(q + 1) * P], xt[:, q * LANES:(q + 1) * LANES], m.wg[:, :],
                                        start=True, stop=True)
                    ins.then_inc(wh_done, 1)
                return stage

            if unit:
                rounds(pe, NCH, [(turn_x(0), 4), (turn(0), 0), (multiply_x(0), 4), (turn_x(1), 4), (turn(1), 0),
                                 (multiply_x(1), 4), (multiply(0), 0), (multiply(1), 0)])
            elif products:
                rounds(pe, NCH, [(turn(0), 0), (turn(1), 0), (multiply(0), 0), (multiply(1), 0)])

        @block.scalar
        def _(act):
            def copy_turned(s):
                def stage(c, h, u):
                    need(act, turned, S * c + s + 1)
                    need(act, multiplied, S * c + s - 1)
                    for e in range(2):
                        ins = act.copy(tcp[:, s % 2, e, :, :],
                                       ps_t[s % 2][e][:, 0:PAIRS * LANES].rearrange("p (a b) -> p a b", a=PAIRS))
                    ins.then_inc(turned_copied, 1)
                return stage

            def square(c, h, u):
                need(act, raw_ready, c + 1)
                need(act, length_sq, c)
                act.activation(sq[:, :, :], raw[:, h, :, :], ACT.Square).then_inc(squared, 1)

            def root_length(c, h, u):
                need(act, length_sq, c + 1)
                act.activation(ss[:, h, :], ss[:, h, :], ACT.Sqrt).then_inc(length, 1)

            def root_variance(c, h, u):
                need(act, var_ready, c + 1)
                act.activation(var[:, h, :], var[:, h, :], ACT.Sqrt, bias=eps[:, 0:1], scale=1.0 / D).then_inc(rooted, 1)

            def copy_x(c, h, u):
                need(act, x_ready, c + 1)
                need(act, stored[h], DMA * u)
                act.copy(out[:, h, :, 0:D], x_new[:, h, :, :]).then_inc(x_copied, 1)

            def copy_xturned(s):
                def stage(c, h, u):
                    need(act, xturned, S * c + s + 1)
                    need(act, wh_done, S * c + s)
                    act.copy(xt[:, :], ps_x[:, 0:PAIRS * LANES]).then_inc(xturned_copied, 1)
                return stage

            if relu:
                rounds(act, NCH, [(copy_turned(0), 0), (copy_turned(1), 0)])
            elif unit:
                rounds(act, NCH, [(square, 1), (copy_xturned(0), 4), (copy_turned(0), 0), (root_length, 1), (root_variance, 3),
                                  (copy_xturned(1), 4), (copy_turned(1), 0), (copy_x, 4)])
            elif plain:
                rounds(act, NCH, [(copy_turned(0), 0), (copy_turned(1), 0), (root_variance, 1)])
            else:
                rounds(act, NCH, [(root_variance, 1)])

        @block.gpsimd
        def _(pool):
            def unit_sum(c, h, u):
                need(pool, unit_ready, c + 1)
                need(pool, x_loaded[h], DMA * (u + 1))
                need(pool, var_ready, c - 1)
                need(pool, xn_ready, c - 1)
                pool.tensor_tensor(xs[:, h, :, :], raw[:, h, :, :], wide(rlen, h), ALU.mult).then_inc(scaled, 1)
                need(pool, scaled, c + 1)
                pool.tensor_tensor(xs[:, h, :, :], xs[:, h, :, :], tin[2][:, h, :, :], ALU.add).then_inc(xs_ready, 1)

            def plain_sum(c, h, u):
                need(pool, raw_ready, c + 1)
                need(pool, var_ready, c - 1)
                need(pool, xn_ready, c - 1)
                other = tin[0][:, h, :, :] if plain else tin[1][:, h, :, 0:D]
                pool.tensor_tensor(xs[:, h, :, :], raw[:, h, :, :], other, ALU.add).then_inc(xs_ready, 1)

            def divide(c, h, u):
                need(pool, raw_ready, c + 1)
                need(pool, xs_ready, c - 1)
                pool.tensor_tensor(raw[:, h, :, :].rearrange("p k (a d) -> p k a d", a=HEADS),
                                   tin[1][:, h, :, 0:D].rearrange("p k (a d) -> p k a d", a=HEADS),
                                   rden[:, h, :].rearrange("p (k a) -> p k a", a=HEADS).unsqueeze(3).to_broadcast([LANES, K, HEADS, DH]),
                                   ALU.mult).then_inc(divided, 1)

            def normalise(c, h, u):
                need(pool, rstd_ready, c + 1)
                need(pool, x_ready, c - 1)
                pool.tensor_tensor(xn[:, h, :, :], xs[:, h, :, :], wide(rstd, h), ALU.mult).then_inc(xn_ready, 1)

            if not relu:
                first = divide if heads else plain_sum
                rounds(pool, NCH, [(normalise, 3), (unit_sum, 1)] if unit else [(first, 0), (normalise, 1)])

        @block.vector
        def _(vec):
            def chain(counter, per_chunk, c):
                n = 0

                def did(ins):
                    nonlocal n
                    n += 1
                    ins.then_inc(counter, 1)
                    need(vec, counter, per_chunk * c + n)
                return did

            def evacuate(c, h, u):
                if not relu:
                    need(vec, xs_ready, c - 1)
                for s in range(S):
                    need(vec, multiplied, S * c + s + 1)
                    vec.tensor_tensor(raw[:, h, SUB * s:SUB * (s + 1), :],
                                      ps_o[s % 2][0:LANES, :].rearrange("p (a d) -> p a d", d=D),
                                      bias[:, :].unsqueeze(1).to_broadcast([LANES, SUB, D]), ALU.add).then_inc(evacuated, 1)
                need(vec, evacuated, S * (c + 1))
                if not relu:
                    vec.nop().then_inc(raw_ready, 1)

            def leaky(c, h, u):
                need(vec, stored[h], DMA * u)
                vec.scalar_tensor_tensor(out=out[:, h, :, :], in0=raw[:, h, :, :], scalar=0.01, in1=raw[:, h, :, :],
                                         op0=ALU.mult, op1=ALU.max).then_inc(out_ready, 1)

            def add_product(c, h, u):
                need(vec, loaded[h], LOADED * (u + 1))
                need(vec, xs_ready, c - 1)
                vec.scalar_tensor_tensor(out=raw[:, h, :, :], in0=tin[0][:, h, :, D:2 * D], scalar=m.mix[:, 2:3],
                                         in1=tin[0][:, h, :, 0:D], op0=ALU.mult, op1=ALU.add).then_inc(raw_ready, 1)

            def invert_weights(c, h, u):
                need(vec, loaded[h], LOADED * (u + 1))
                need(vec, divided, c - 1)
                vec.tensor_scalar(rden[:, h, :].rearrange("p (k a) -> p k a", a=HEADS), tin[1][:, h, :, D:ROW2], 1e-8, None,
                                  ALU.add).then_inc(rden_step, 1)
                need(vec, rden_step, c + 1)
                vec.reciprocal(rden[:, h, :], rden[:, h, :]).then_inc(raw_ready, 1)

            def add_x(c, h, u):
                need(vec, divided, c + 1)
                need(vec, xn_ready, c - 1)
                vec.tensor_tensor(xs[:, h, :, :], raw[:, h, :, :], tin[0][:, h, :, :], ALU.add).then_inc(xs_ready, 1)

            def sum_squares(c, h, u):
                need(vec, squared, c + 1)
                vec.tensor_reduce(ss[:, h, :], sq[:, :, :], AX_X, ALU.add).then_inc(length_sq, 1)

            def invert_length(c, h, u):
                need(vec, length, c + 1)
                vec.tensor_scalar(rlen[:, h, :], ss[:, h, :], 1e-12, None, ALU.max).then_inc(unit_step, 1)
                need(vec, unit_step, c + 1)
                vec.reciprocal(rlen[:, h, :], rlen[:, h, :]).then_inc(unit_ready, 1)

            def statistics(c, h, u):
                did = chain(step, 4, c)
                need(vec, xs_ready, c + 1)
                for j in range(K):
                    ins = vec.bn_stats(st[:, h, j, :], xs[:, h, j, :])
                did(ins)
                vec.tensor_tensor(msum[:, h, :], st[:, h, :, 1], st[:, h, :, 4], ALU.add)
                vec.tensor_tensor(var[:, h, :], st[:, h, :, 2], st[:, h, :, 5], ALU.add)
                did(vec.tensor_tensor(mdif[:, :], st[:, h, :, 1], st[:, h, :, 4], ALU.subtract))
                did(vec.tensor_tensor(mdif[:, :], mdif[:, :], mdif[:, :], ALU.mult))
                did(vec.scalar_tensor_tensor(out=var[:, h, :], in0=mdif[:, :], scalar=D / 4.0, in1=var[:, h, :],
                                             op0=ALU.mult, op1=ALU.add))
                vec.nop().then_inc(var_ready, 1)

            def invert_deviation(c, h, u):
                need(vec, rooted, c + 1)
                need(vec, xn_ready, c - 1)
                vec.reciprocal(rstd[:, h, :], var[:, h, :]).then_inc(fin, 1)
                need(vec, fin, c + 1)
                vec.scalar_tensor_tensor(out=shift[:, h, :], in0=msum[:, h, :], scalar=-0.5, in1=rstd[:, h, :],
                                         op0=ALU.mult, op1=ALU.mult).then_inc(rstd_ready, 1)

            def shift_out(c, h, u):
                need(vec, xn_ready, c + 1)
                need(vec, rstd_ready, c + 1)
                if unit:
                    need(vec, x_copied, c - 1)
                    need(vec, xturned, S * (c - 1))
                else:
                    need(vec, stored[h], DMA * u)
                vec.tensor_tensor(x_new[:, h, :, :] if unit else out[:, h, :, :], xn[:, h, :, :], wide(shift, h),
                                  ALU.add).then_inc(x_ready, 1)
                if not unit:
                    need(vec, x_ready, c + 1)
                    vec.nop().then_inc(out_ready, 1)

            def products_out(c, h, u):
                need(vec, stored[h], DMA * u)
                for s in range(S):
                    need(vec, wh_done, S * c + s + 1)
                    vec.tensor_tensor(out[:, h, SUB * s:SUB * (s + 1), D:2 * D],
                                      ps_w[0:LANES, :].rearrange("p (a d) -> p a d", d=D),
                                      m.bg[0:LANES, :].unsqueeze(1).to_broadcast([LANES, SUB, D]), ALU.add).then_inc(wh_out, 1)
                need(vec, wh_out, S * (c + 1))
                need(vec, x_copied, c + 1)
                vec.nop().then_inc(out_ready, S)

            if not relu:
                vec.memset(eps[:, :], 1e-5)
            if relu:
                rounds(vec, NCH, [(evacuate, 0), (leaky, 0)])
            if unit:
                rounds(vec, NCH, [(sum_squares, 1), (invert_deviation, 3), (invert_length, 1), (products_out, 4), (evacuate, 0),
                                  (statistics, 2), (shift_out, 3)])
            if plain:
                rounds(vec, NCH, [(statistics, 1), (evacuate, 0), (invert_deviation, 1), (shift_out, 2)])
            if cosine:
                rounds(vec, NCH, [(statistics, 1), (add_product, 0), (invert_deviation, 1), (shift_out, 2)])
            if heads:
                rounds(vec, NCH, [(add_x, 1), (statistics, 1), (invert_weights, 0), (invert_deviation, 1), (shift_out, 2)])


def gnn_kernel(nc, w, out):
    m = Memory()
    m.nodes, m.edges = w["x"].shape[0], w["src"].shape[0]
    assert m.nodes % LANES == 0 and m.edges % LANES == 0
    m.tcols, m.ecols = m.nodes // LANES, m.edges // LANES
    assert m.tcols % (2 * K) == 0 and m.ecols % (2 * G) == 0
    NCH = m.ecols // G
    with ExitStack() as ctx:
        def dram(name, shape, dt=F32):
            return nc.dram_tensor(name, shape, dt, kind="Internal").ap()

        sb = lambda x, shape, dt=F32: ctx.enter_context(nc.sbuf_tensor(x, shape, dt))
        m.sum_d, m.sum_s = dram("sum_d", (m.nodes, D)), dram("sum_s", (m.nodes, ROW2))
        h1, xw1 = dram("h1", (m.nodes, D)), dram("xw1", (m.nodes, 2 * D))
        x2, x3 = dram("x2", (m.nodes, D)), dram("x3", (m.nodes, D))
        s_key, s_other, s_base = dram("s_key", (m.edges,), I32), dram("s_other", (m.edges,), I32), dram("s_base", (m.edges,))
        m.ident, m.before, m.sgn = sb("ident", [P, P]), sb("before", [LANES, LANES]), sb("sgn", [P, 8])
        m.ones = sb("ones", [P, P])
        m.deg, m.mix = sb("deg", [P, 2]), sb("mix", [LANES, 3])
        m.b1, m.b2, m.bg, m.b3 = (sb(b, [LANES, D]) for b in ("b1", "b2", "bg", "b3"))
        m.w1l, m.w1r, m.w2l, m.w2r, m.wg, m.w3x, m.w3m = (
            sb(n, [P, P]) for n in ("w1l", "w1r", "w2l", "w2r", "wg", "w3x", "w3m"))
        m.wqkv = sb("wqkv", [P, 3 * D])
        by_dst, by_src = ["from", "to", "same", "inv"], ["from_a", "from_b", "to", "same", "base"]
        plan_d = sb("plan_d", [LANES, NCH, len(by_dst), G])
        plan_s = sb("plan_s", [LANES, NCH, len(by_src), G])
        mask_d, mask_s = sb("mask_d", [LANES, LANES]), sb("mask_s", [LANES, LANES])
        fix_d, fix_s = sb("fix_d", [LANES, 1], I32), sb("fix_s", [LANES, 1], I32)
        inv_d = sb("inv_d", [LANES, 1])

        set_up(nc, m, w)
        edge_plan(nc, m, "plan_dst_", w["dst"], {"from": (w["src"], I32)}, plan_d, by_dst, mask_d, fix_d, inv_d)
        sort_edges(nc, m, "sort_src_", w["src"], w["dst"], (w["edge_weight"], w["edge_weight_n2"]), s_key, s_other, s_base)
        edge_plan(nc, m, "plan_src_", s_key, {"from_a": (s_key, I32), "from_b": (s_other, I32), "base": (s_base, F32)},
                  plan_s, by_src, mask_s, fix_s, None)
        edge_phase(nc, m, "e0_", "mean", [w["x"]], plan_d, by_dst, m.sum_d, mask_d, fix_d, inv_d)
        node_phase(nc, m, "n0_", "relu", [w["x"], m.sum_d], (m.w1r, m.w1l), m.b1, h1)
        edge_phase(nc, m, "e1_", "mean", [h1], plan_d, by_dst, m.sum_d, mask_d, fix_d, inv_d)
        node_phase(nc, m, "n1_", "unit", [h1, m.sum_d, w["x"]], (m.w2r, m.w2l), m.b2, xw1)
        edge_phase(nc, m, "e2_", "cosine", [xw1, xw1], plan_s, by_src, m.sum_s, mask_s, fix_s)
        node_phase(nc, m, "n2_", "cosine", [xw1, m.sum_s], None, None, x2)
        edge_phase(nc, m, "e3_", "heads", [x2, x2], plan_s, by_src, m.sum_s, mask_s, fix_s)
        node_phase(nc, m, "n3_", "heads", [x2, m.sum_s], None, None, x3)
        edge_phase(nc, m, "e4_", "mean", [x3], plan_d, by_dst, m.sum_d, mask_d, fix_d, inv_d)
        node_phase(nc, m, "n4_", "plain", [x3, m.sum_d], (m.w3x, m.w3m), m.b3, out)


def kernel(x, src, dst, edge_weight, edge_weight_n2, L0_gnn_W1_l, L0_gnn_b1, L0_gnn_W1_r, L0_gnn_W2_l, L0_gnn_b2,
           L0_gnn_W2_r, L1_gnn_W, L1_gnn_b, L1_gnn_deg_coeff, L1_gnn_coeff_param, L1_gnn_scale_param, L2_gnn_Wq,
           L2_gnn_Wk, L2_gnn_Wv, L3_gnn_W, L3_gnn_b):
    import numpy as np
    import concourse.bacc as bacc
    from concourse.bass_utils import run_bass_kernel_spmd

    arrays = {
        "x": x, "src": src, "dst": dst, "edge_weight": edge_weight, "edge_weight_n2": edge_weight_n2,
        "w1l": np.transpose(L0_gnn_W1_l), "w1r": np.transpose(L0_gnn_W1_r), "b1": L0_gnn_b1,
        "w2l": np.transpose(L0_gnn_W2_l), "w2r": np.transpose(L0_gnn_W2_r), "b2": L0_gnn_b2,
        "wg": L1_gnn_W, "bg": L1_gnn_b, "deg_coeff": L1_gnn_deg_coeff, "coeff": L1_gnn_coeff_param,
        "scale": L1_gnn_scale_param, "wq": L2_gnn_Wq, "wk": L2_gnn_Wk, "wv": L2_gnn_Wv,
        "w3x": L3_gnn_W[0:D], "w3m": L3_gnn_W[D:2 * D], "b3": L3_gnn_b,
    }
    arrays = {k: np.ascontiguousarray(v) for k, v in arrays.items()}
    q = np.arange(P)
    bit = lambda b: 1 - 2 * ((q >> b) & 1)
    arrays["ident"] = np.eye(P, dtype=np.float32)
    arrays["before"] = np.triu(np.ones((LANES, LANES), np.float32), 1)
    arrays["sgn"] = np.stack([bit(0)] + [bit(b) * bit(b - 1) for b in range(1, 7)] + [bit(6)], 1).astype(np.float32)

    nc = bacc.Bacc("TRN2", target_bir_lowering=False, num_devices=1)
    w = {k: nc.dram_tensor(f"in_{k}", a.shape, mybir.dt.from_np(a.dtype), kind="ExternalInput").ap()
         for k, a in arrays.items()}
    out = nc.dram_tensor("out_0", x.shape, F32, kind="ExternalOutput").ap()
    gnn_kernel(nc, w, out)
    r = run_bass_kernel_spmd(nc, [{f"in_{k}": a for k, a in arrays.items()}], core_ids=[0])
    return r.results[0]["out_0"]
```

```python
from contextlib import ExitStack

import concourse.bass as bass
from concourse import mybir

ALU = mybir.AluOpType
ACT = mybir.ActivationFunctionType
AX_X = mybir.AxisListType.X
F32 = mybir.dt.float32
I32 = mybir.dt.int32

P = 128
LANES = 125
D = 64
HEADS = 4
DH = D // HEADS
ROW2 = D + HEADS
G = 20
K = 16
SUB = 8
SKIP = 1 << 20
ZERO_PIECES = 16
DMA = 16


def at(offset_ap):
    return bass.IndirectOffsetOnAxis(ap=offset_ap, axis=0)


class Memory:
    pass


class Phase(ExitStack):

    def __init__(self, nc, name):
        super().__init__()
        self.nc, self.name, self.sems = nc, name, []

    def sem(self, x):
        self.sems.append(self.nc.alloc_semaphore(self.name + x))
        return self.sems[-1]

    def sb(self, x, shape, dt=F32):
        return self.enter_context(self.nc.sbuf_tensor(self.name + x, shape, dt))

    def bank(self, x):
        return self.enter_context(self.nc.psum_tensor(self.name + x, [P, 512], F32))

    def block(self):
        return self.enter_context(self.nc.Block())

    def __exit__(self, *error):
        ended = super().__exit__(*error)
        if error[0] is None:
            self.nc.clear_and_free_semaphores(self.sems)
            self.nc.all_engine_barrier()
        return ended


def need(engine, sem, value):
    if not isinstance(value, int) or value > 0:
        engine.wait_ge(sem, value)


def rounds(engine, count, stages):
    last = max(lag for _, lag in stages)
    first = 2 + last + last % 2

    def straight(t):
        for f, lag in stages:
            if 0 <= t - lag < count:
                f(t - lag, (t - lag) % 2, (t - lag) // 2)

    assert count % 2 == 0 and count > first
    for t in range(first):
        straight(t)
    with engine.Fori(first // 2, count // 2) as i:
        for k in range(2):
            for f, lag in stages:
                f(2 * i + (k - lag), (k - lag) % 2, i + (k - lag) // 2)
    for t in range(count, count + last):
        straight(t)


def columns(dram):
    return dram.rearrange("(p t) d -> p t d", p=LANES)


def set_up(nc, m, w):
    name = "setup_"
    with Phase(nc, name) as ctx:
        sem, sb, bank = ctx.sem, ctx.sb, ctx.bank
        loaded, cleared = sem("loaded"), sem("cleared")
        vec_step, act_done = sem("vec_step"), sem("act_done")
        coef = sb("coef", [LANES, 3])
        cmax = sb("cmax", [LANES, 1])
        cexp = sb("cexp", [LANES, 3])
        csum = sb("csum", [LANES, 1])
        scp = sb("scp", [LANES, 1])
        sca = sb("sca", [LANES, 3])
        edges_loaded, edges_copied, falls_ready, falls_summed, last_set = (
            sem("edges_loaded"), sem("edges_copied"), sem("falls_ready"), sem("falls_summed"), sem("last_set"))
        EC = m.ecols
        dst, src_ids, next_dst = sb("dst", [LANES, EC], I32), sb("src", [LANES, EC], I32), sb("next_dst", [LANES, 1], I32)
        falls, fall_count = sb("falls", [LANES, EC]), sb("fall_count", [LANES, 1])
        ps_falls = bank("ps_falls")
        lanes = lambda d: d.rearrange("(p c) -> p c", p=LANES)
        block = ctx.block()
        small = [
            (m.ident, w["ident"]), (m.before, w["before"]), (m.sgn, w["sgn"]),
            (m.deg, w["deg_coeff"].partition_broadcast(P)),
            (coef, w["coeff"].partition_broadcast(LANES)), (scp, w["scale"].partition_broadcast(LANES)),
            (m.b1, w["b1"].partition_broadcast(LANES)), (m.b2, w["b2"].partition_broadcast(LANES)),
            (m.bg, w["bg"].partition_broadcast(LANES)), (m.b3, w["b3"].partition_broadcast(LANES)),
        ]
        twice = [(m.w1r, w["w1r"]), (m.w1l, w["w1l"]), (m.w2r, w["w2r"]), (m.w2l, w["w2l"]),
                 (m.w3x, w["w3x"]), (m.w3m, w["w3m"]), (m.wg, w["wg"])]

        @block.sync
        def _(sp):
            sp.dma_start(dst[:, :], lanes(w["dst"])).then_inc(edges_loaded, DMA)
            sp.dma_start(src_ids[:, :], lanes(w["src"])).then_inc(edges_loaded, DMA)
            sp.wait_ge(last_set, 1)
            sp.dma_start(next_dst[0:LANES - 1, :], lanes(w["dst"])[1:LANES, 0:1],
                         allow_slow_non_contiguous=True).then_inc(edges_loaded, DMA)
            for tile, src in small:
                sp.dma_start(tile[:, :], src).then_inc(loaded, DMA)
            sp.wait_ge(cleared, 1)
            for tile, src in twice:
                sp.dma_start(tile[0:D, 0:D], src).then_inc(loaded, DMA)
                sp.dma_start(tile[D:P, D:P], src).then_inc(loaded, DMA)
            sp.dma_start(m.wqkv[0:D, 0:D], w["wq"]).then_inc(loaded, DMA)
            sp.dma_start(m.wqkv[D:P, D:2 * D], w["wk"]).then_inc(loaded, DMA)
            sp.dma_start(m.wqkv[D:P, 2 * D:3 * D], w["wv"]).then_inc(loaded, DMA)
            sp.wait_ge(edges_loaded, 3 * DMA)
            sp.dma_start(lanes(m.d_key), dst[:, :]).then_inc(edges_copied, DMA)
            sp.dma_start(lanes(m.d_other), src_ids[:, :]).then_inc(edges_copied, DMA)
            sp.wait_ge(edges_copied, 2 * DMA)
            sp.wait_ge(loaded, DMA * (len(small) + 2 * len(twice) + 3))

        @block.gpsimd
        def _(pool):
            for tile, _ in twice:
                pool.memset(tile[:, :], 0.0)
            pool.memset(m.wqkv[:, :], 0.0).then_inc(cleared, 1)

        @block.tensor
        def _(pe):
            pe.wait_ge(falls_ready, 3)
            pe.matmul(ps_falls[0:1, 0:1], fall_count[:, :], m.ones[0:LANES, 0:1], start=True, stop=True).then_inc(falls_summed, 1)

        @block.scalar
        def _(act):
            act.wait_ge(vec_step, 2)
            act.activation(cexp[:, :], cexp[:, :], ACT.Exp).then_inc(act_done, 1)
            act.activation(sca[:, 0:1], scp[:, :], ACT.Abs).then_inc(act_done, 1)
            act.wait_ge(act_done, 2)
            act.activation(sca[:, 1:2], sca[:, 0:1], ACT.Exp, scale=-1.0).then_inc(act_done, 1)
            act.wait_ge(act_done, 3)
            act.activation(sca[:, 2:3], sca[:, 1:2], ACT.Ln, bias=1.0).then_inc(act_done, 1)

        @block.vector
        def _(vec):
            vec.memset(next_dst[:, :], SKIP).then_inc(last_set, 1)
            vec.memset(m.ones[:, :], 1.0).then_inc(falls_ready, 1)
            vec.wait_ge(edges_loaded, 3 * DMA)
            vec.tensor_tensor(falls[:, EC - 1:EC], dst[:, EC - 1:EC], next_dst[:, :], ALU.is_gt)
            vec.tensor_tensor(falls[:, 0:EC - 1], dst[:, 0:EC - 1], dst[:, 1:EC], ALU.is_gt).then_inc(falls_ready, 1)
            vec.wait_ge(falls_ready, 2)
            vec.tensor_reduce(fall_count[:, :], falls[:, :], AX_X, ALU.add).then_inc(falls_ready, 1)
            vec.wait_ge(falls_summed, 1)
            vec.tensor_copy(m.unsorted[:, :], ps_falls[0:1, 0:1])
            vec.wait_ge(loaded, DMA * (len(small) + 2 * len(twice) + 3))
            vec.tensor_reduce(cmax[:, :], coef[:, :], AX_X, ALU.max).then_inc(vec_step, 1)
            vec.wait_ge(vec_step, 1)
            vec.tensor_scalar(cexp[:, :], coef[:, :], cmax[:, 0:1], None, ALU.subtract).then_inc(vec_step, 1)
            vec.wait_ge(act_done, 1)
            vec.tensor_reduce(csum[:, :], cexp[:, :], AX_X, ALU.add).then_inc(vec_step, 1)
            vec.wait_ge(vec_step, 3)
            vec.reciprocal(csum[:, :], csum[:, :]).then_inc(vec_step, 1)
            vec.wait_ge(act_done, 4)
            vec.scalar_tensor_tensor(out=scp[:, :], in0=scp[:, :], scalar=0.0, in1=sca[:, 2:3],
                                     op0=ALU.max, op1=ALU.add).then_inc(vec_step, 1)
            vec.wait_ge(vec_step, 5)
            vec.tensor_scalar(m.mix[:, :], cexp[:, :], csum[:, 0:1], scp[:, 0:1], ALU.mult, ALU.mult)


class EdgeSort:

    def __init__(self, nc, m, ctx, key_in, other_in, weights, key_out, other_out, base_out=None):
        self.m, self.E = m, key_in.shape[0]
        n = P * P
        while n < self.E:
            n *= 2
        W = self.W = n // P
        self.levels_in_row = W.bit_length() - 1
        self.full, self.rest = self.E // W, self.E % W
        sem, sb = ctx.sem, ctx.sb
        self.loaded, self.padded, self.prepared, self.stored = sem("loaded"), sem("padded"), sem("prepared"), sem("sorted_stored")
        self.act_done, self.vec_step, self.swapped = sem("act_done"), sem("vec_step"), sem("swapped")
        self.copied, self.turned, self.flipped = sem("copied"), sem("turned"), sem("flipped")
        self.ki, self.oi = sb("ki", [P, W], I32), sb("oi", [P, W], I32)
        self.wa, self.wb = sb("wa", [P, W]), sb("wb", [P, W])
        self.z, self.az = sb("z", [P, W]), sb("az", [P, W])
        self.key = [sb(f"key{i}", [P, W]) for i in range(2)]
        self.load = [sb(f"load{i}", [P, 2, W]) for i in range(2)]
        self.mask = sb("mask", [P, W // 2], I32)
        self.ps = [ctx.enter_context(nc.psum_tensor(f"{ctx.name}ps{i}", [P, W], F32)) for i in range(3)]
        self.weighted = weights is not None
        self.inputs = [(self.ki, key_in), (self.oi, other_in)]
        self.outputs = [(self.ki, key_out), (self.oi, other_out)]
        if self.weighted:
            self.inputs += [(self.wa, weights[0]), (self.wb, weights[1])]
            self.outputs += [(self.wa, base_out)]
        self.steps, cur, swaps, turns, flips = [], 0, 0, 0, 0

        def add(kind, arg=None):
            nonlocal cur, swaps, turns, flips
            self.steps.append((kind, arg, cur, swaps, turns, flips))
            if kind == "swap":
                cur, swaps = 1 - cur, swaps + 1
            turns, flips = turns + (kind == "turn"), flips + (kind == "flip")

        for level in range(1, n.bit_length()):
            add("flip", level)
            j = level - 1
            if j >= self.levels_in_row:
                add("turn")
                while j >= self.levels_in_row:
                    add("swap", 1 << (j - self.levels_in_row))
                    j -= 1
                add("turn")
            while j >= 0:
                add("swap", 1 << j)
                j -= 1
        self.cur, self.swaps = cur, swaps

    def part(self, c, count):
        n = len(self.steps)
        return self.steps[n * c // count:n * (c + 1) // count]

    def rows_of(self, tile, dram):
        full, rest, W = self.full, self.rest, self.W
        yield tile[0:full, :], dram[0:full * W].rearrange("(p c) -> p c", p=full)
        if rest:
            yield tile[full:full + 1, 0:rest], dram[full * W:self.E].rearrange("(p c) -> p c", p=1)

    def sync_load(self, sp):
        sp.wait_ge(self.padded, len(self.inputs))
        for tile, dram in self.inputs:
            for here, there in self.rows_of(tile, dram):
                sp.dma_start(here, there).then_inc(self.loaded, DMA)

    def sync_store(self, sp):
        sp.wait_ge(self.prepared, 2)
        for tile, dram in self.outputs:
            for here, there in self.rows_of(tile, dram):
                sp.dma_start(there, here).then_inc(self.stored, DMA)
        sp.wait_ge(self.stored, DMA * len(self.outputs) * (2 if self.rest else 1))

    def pool_pad(self, pool):
        for tile, _ in self.inputs:
            pool.memset(tile[:, :], SKIP if tile is self.ki else 0).then_inc(self.padded, 1)

    def scalar_prepare(self, act):
        if self.weighted:
            act.wait_ge(self.vec_step, 1)
            act.activation(self.az[:, :], self.z[:, :], ACT.Abs).then_inc(self.act_done, 1)
            act.wait_ge(self.act_done, 1)
            act.activation(self.az[:, :], self.az[:, :], ACT.Exp, scale=-1.0).then_inc(self.act_done, 1)
            act.wait_ge(self.act_done, 2)
            act.activation(self.az[:, :], self.az[:, :], ACT.Ln, bias=1.0).then_inc(self.act_done, 1)
        act.wait_ge(self.prepared, 1)

    def scalar_steps(self, act, steps):
        for kind, _, cur, swaps, turns, _ in steps:
            if kind == "swap":
                if swaps:
                    act.wait_ge(self.swapped, 3 * swaps)
                if turns:
                    act.wait_ge(self.copied, turns)
                act.copy(self.load[1 - cur][:, :, :], self.load[cur][:, :, :]).then_inc(self.act_done, 1)

    def tensor_steps(self, pe, steps):
        for kind, _, cur, swaps, turns, flips in steps:
            if kind == "turn":
                pe.wait_ge(self.swapped, 3 * swaps)
                if turns % 2 == 0:
                    pe.wait_ge(self.flipped, flips)
                if turns:
                    pe.wait_ge(self.copied, turns)
                for b in range(self.W // P):
                    c = slice(b * P, (b + 1) * P)
                    pe.transpose(self.ps[0][:, c], self.key[cur][:, c], self.m.ident[:, :])
                    pe.transpose(self.ps[1][:, c], self.load[cur][:, 0, c], self.m.ident[:, :])
                    t = pe.transpose(self.ps[2][:, c], self.load[cur][:, 1, c], self.m.ident[:, :])
                t.then_inc(self.turned, 1)

    def vector_prepare(self, vec):
        m, z, az = self.m, self.z, self.az
        vec.wait_ge(self.loaded, DMA * len(self.inputs) * (2 if self.rest else 1))
        if self.weighted:
            vec.tensor_scalar(z[:, :], self.wb[:, :], m.deg[:, 0:1], m.deg[:, 1:2], ALU.mult, ALU.add).then_inc(self.vec_step, 1)
            vec.wait_ge(self.act_done, 3)
            vec.wait_ge(self.vec_step, 1)
            vec.scalar_tensor_tensor(out=z[:, :], in0=z[:, :], scalar=0.0, in1=az[:, :],
                                     op0=ALU.max, op1=ALU.add).then_inc(self.vec_step, 1)
            vec.wait_ge(self.vec_step, 2)
            vec.tensor_tensor(z[:, :], z[:, :], self.wa[:, :], ALU.mult).then_inc(self.vec_step, 1)
            vec.tensor_tensor(az[:, :], self.ki[:, :], self.oi[:, :], ALU.not_equal).then_inc(self.vec_step, 1)
            vec.wait_ge(self.vec_step, 4)
            vec.tensor_tensor(self.load[0][:, 1, :], z[:, :], az[:, :], ALU.mult)
        else:
            vec.memset(self.load[0][:, 1, :], 0.0)
        vec.tensor_copy(self.key[0][:, :], self.ki[:, :])
        vec.tensor_copy(self.load[0][:, 0, :], self.oi[:, :]).then_inc(self.prepared, 1)
        vec.wait_ge(self.prepared, 1)

    def vector_steps(self, vec, steps):
        for kind, arg, cur, swaps, turns, flips in steps:
            if kind == "flip":
                self.vector_flip(vec, self.key[cur], arg, swaps)
            elif kind == "turn":
                vec.wait_ge(self.turned, turns + 1)
                vec.tensor_copy(self.key[cur][:, :], self.ps[0][:, :])
                vec.tensor_copy(self.load[cur][:, 0, :], self.ps[1][:, :])
                vec.tensor_copy(self.load[cur][:, 1, :], self.ps[2][:, :]).then_inc(self.copied, 1)
            else:
                self.vector_swap(vec, arg, cur, swaps, turns, flips)

    def vector_flip(self, vec, key, level, swaps):
        W, m = self.W, self.m
        if swaps:
            vec.wait_ge(self.swapped, 3 * swaps)
        if level < self.levels_in_row:
            if level == 1:
                parts = [key[:, :].rearrange("p (a two r) -> p a two r", two=2, r=2)[:, :, 1, :]]
            else:
                v = key[:, :].rearrange("p (a x y r) -> p a x y r", x=2, y=2, r=1 << (level - 1))
                parts = [v[:, :, 0, 1, :], v[:, :, 1, 0, :]]
            for q in parts:
                ins = vec.tensor_scalar(q, q, -1.0, None, ALU.mult)
            ins.then_inc(self.flipped, 1)
        elif level == self.levels_in_row:
            low, high = key[:, 0:W // 2], key[:, W // 2:W]
            vec.tensor_scalar(low, low, m.sgn[:, 0:1], None, ALU.mult)
            vec.tensor_scalar(high, high, m.sgn[:, 0:1], -1.0, ALU.mult, ALU.mult).then_inc(self.flipped, 1)
        else:
            k = level - self.levels_in_row
            vec.tensor_scalar(key[:, :], key[:, :], m.sgn[:, k:k + 1], None, ALU.mult).then_inc(self.flipped, 1)

    def vector_swap(self, vec, stride, cur, swaps, turns, flips):
        def halves(ap):
            v = ap.rearrange("p (a two r) -> p a two r", two=2, r=stride)
            return v[:, :, 0, :], v[:, :, 1, :]

        low, high = halves(self.key[cur][:, :])
        new_low, new_high = halves(self.key[1 - cur][:, :])
        falls = self.mask[:, :].rearrange("p (a r) -> p a r", r=stride)
        if swaps:
            vec.wait_ge(self.swapped, 3 * swaps)
        vec.wait_ge(self.flipped, flips)
        if turns:
            vec.wait_ge(self.copied, turns)
        vec.tensor_tensor(falls, low, high, ALU.is_gt).then_inc(self.vec_step, 1)
        vec.tensor_tensor(new_low, low, high, ALU.min)
        vec.tensor_tensor(new_high, low, high, ALU.max).then_inc(self.swapped, 1)
        vec.wait_ge(self.act_done, (3 if self.weighted else 0) + swaps + 1)
        vec.wait_ge(self.vec_step, (4 if self.weighted else 0) + swaps + 1)
        for carried in range(2):
            old_low, old_high = halves(self.load[cur][:, carried, :])
            to_low, to_high = halves(self.load[1 - cur][:, carried, :])
            vec.copy_predicated(to_low, falls, old_high)
            vec.copy_predicated(to_high, falls, old_low).then_inc(self.swapped, 1)

    def vector_finish(self, vec):
        vec.wait_ge(self.swapped, 3 * self.swaps)
        vec.tensor_copy(self.ki[:, :], self.key[self.cur][:, :])
        if self.weighted:
            vec.tensor_copy(self.wa[:, :], self.load[self.cur][:, 1, :])
        vec.tensor_copy(self.oi[:, :], self.load[self.cur][:, 0, :]).then_inc(self.prepared, 1)


def sort_if(nc, m, name, flag, key_in, other_in, key_out, other_out):
    with Phase(nc, name) as ctx:
        sort = EdgeSort(nc, m, ctx, key_in, other_in, None, key_out, other_out)
        block = ctx.block()
        wanted = lambda engine: engine.If(engine.value_load(flag) > 0)

        @block.sync
        def _(sp):
            with wanted(sp):
                sort.sync_load(sp)
                sort.sync_store(sp)

        @block.gpsimd
        def _(pool):
            with wanted(pool):
                sort.pool_pad(pool)

        @block.scalar
        def _(act):
            with wanted(act):
                sort.scalar_prepare(act)
                sort.scalar_steps(act, sort.steps)

        @block.tensor
        def _(pe):
            with wanted(pe):
                sort.tensor_steps(pe, sort.steps)

        @block.vector
        def _(vec):
            with wanted(vec):
                sort.vector_prepare(vec)
                sort.vector_steps(vec, sort.steps)
                sort.vector_finish(vec)


def edge_plan(nc, m, name, key_dram, columns_f, plan, fields, carry_mask, fix_idx, fix_inv):
    EC = m.ecols
    with Phase(nc, name) as ctx:
        sem, sb, bank = ctx.sem, ctx.sb, ctx.bank
        loaded, step, turned, next_set = sem("loaded"), sem("step"), sem("turned"), sem("next_set")
        ki = sb("ki", [LANES, EC], I32)
        nxt_i, nxt = sb("nxt_i", [LANES, 1], I32), sb("nxt", [LANES, 1])
        key, same, on = sb("key", [LANES, EC]), sb("same", [LANES, EC]), sb("on", [LANES, EC])
        ones, cnt, first = sb("ones", [LANES, EC]), sb("cnt", [LANES, EC]), sb("first", [LANES, EC])
        bc = sb("bc", [LANES, LANES])
        t1, t2, t3 = sb("t1", [LANES, 1]), sb("t2", [LANES, 1]), sb("t3", [LANES, 1])
        others = {f: sb("in_" + f, [LANES, EC], dt) for f, (_, dt) in columns_f.items()}
        psb = bank("psb")
        psc = bank("psc")
        block = ctx.block()
        lanes = lambda d: d[0:LANES * EC].rearrange("(p c) -> p c", p=LANES)
        field = lambda f: plan[:, :, fields.index(f), :]
        by_chunk = lambda t: t[:, :].rearrange("p (c g) -> p c g", g=G)

        @block.sync
        def _(sp):
            sp.dma_start(ki[:, :], lanes(key_dram)).then_inc(loaded, DMA)
            for f, (src, _) in columns_f.items():
                sp.dma_start(others[f][:, :], lanes(src)).then_inc(loaded, DMA)
            sp.wait_ge(next_set, 1)
            sp.dma_start(nxt_i[0:LANES - 1, :], lanes(key_dram)[1:LANES, 0:1],
                         allow_slow_non_contiguous=True).then_inc(loaded, DMA)

        @block.vector
        def _(vec):
            count = 0

            def did(ins):
                nonlocal count
                ins.then_inc(step, 1)
                count += 1
                vec.wait_ge(step, count)

            vec.memset(nxt_i[:, :], -1).then_inc(next_set, 1)
            vec.memset(same[:, 0:1], 0.0)
            did(vec.memset(ones[:, :], 1.0))
            vec.wait_ge(loaded, DMA * (2 + len(columns_f)))
            vec.tensor_copy(nxt[:, :], nxt_i[:, :])
            did(vec.tensor_copy(key[:, :], ki[:, :]))
            vec.tensor_tensor(same[:, 1:EC], key[:, 1:EC], key[:, 0:EC - 1], ALU.is_equal)
            vec.tensor_tensor(on[:, 0:EC - 1], key[:, 1:EC], key[:, 0:EC - 1], ALU.is_equal)
            vec.tensor_tensor(on[:, EC - 1:EC], key[:, EC - 1:EC], nxt[:, :], ALU.is_equal)
            vec.tensor_scalar(first[:, :], key[:, :], key[:, 0:1], None, ALU.is_equal)
            vec.tensor_tensor(t1[:, :], key[:, 0:1], key[:, EC - 1:EC], ALU.is_equal)
            did(vec.tensor_scalar(bc[:, :], m.ones[0:LANES, 0:LANES], key[:, 0:1], None, ALU.mult))
            vec.scalar_tensor_tensor(out=field("to"), in0=by_chunk(on), scalar=float(SKIP), in1=by_chunk(key),
                                     op0=ALU.mult, op1=ALU.add)
            vec.tensor_copy(field("same"), by_chunk(same))
            for f, tile in others.items():
                vec.tensor_copy(field(f), by_chunk(tile))
            vec.tensor_tensor_scan(cnt[:, :], same[:, :], ones[:, :], 0.0, ALU.mult, ALU.add)
            did(vec.tensor_tensor(t1[:, :], t1[:, :], on[:, EC - 1:EC], ALU.mult))
            did(vec.scalar_tensor_tensor(out=t2[:, :], in0=t1[:, :], scalar=float(SKIP), in1=key[:, 0:1],
                                         op0=ALU.mult, op1=ALU.add))
            vec.tensor_copy(fix_idx[:, :], t2[:, :])
            vec.wait_ge(turned, 1)
            did(vec.scalar_tensor_tensor(out=carry_mask[:, :], in0=psb[0:LANES, 0:LANES], scalar=key[:, EC - 1:EC],
                                         in1=m.before[:, :], op0=ALU.is_equal, op1=ALU.mult))
            vec.wait_ge(turned, 2)
            did(vec.tensor_copy(t3[:, :], psc[0:LANES, 0:1]))
            did(vec.scalar_tensor_tensor(out=cnt[:, :], in0=first[:, :], scalar=t3[:, 0:1], in1=cnt[:, :],
                                         op0=ALU.mult, op1=ALU.add))
            vec.tensor_reduce(t1[:, :], first[:, :], AX_X, ALU.add)
            did(vec.reciprocal(cnt[:, :], cnt[:, :]))
            did(vec.tensor_tensor(t1[:, :], t1[:, :], t3[:, :], ALU.add))
            if fix_inv is not None:
                vec.tensor_copy(field("inv"), by_chunk(cnt))
                did(vec.reciprocal(fix_inv[:, :], t1[:, :]))

        @block.tensor
        def _(pe):
            pe.wait_ge(step, 3)
            pe.transpose(psb[0:LANES, 0:LANES], bc[:, :], m.ident[0:LANES, 0:LANES]).then_inc(turned, 1)
            pe.wait_ge(step, 6)
            pe.matmul(psc[0:LANES, 0:1], carry_mask[:, :], cnt[:, EC - 1:EC], start=True, stop=True).then_inc(turned, 1)


def edge_phase(nc, m, name, kind, tables, plan, fields, sums, carry_mask, fix_idx, fix_inv=None, beside=None):
    NCH = m.ecols // G
    NI = NCH // 2
    NF = len(fields)
    NG = fields.index("to")
    NS = NF - NG - 1
    flag = lambda f: fields.index(f) - NG - 1
    W = tables[0].shape[1]
    mean, cosine, heads = kind == "mean", kind == "cosine", kind == "heads"
    width = D if mean else ROW2
    SW = ROW2 if heads else D
    GATHERED = DMA * G * NG
    SCATTERED = DMA * G
    QC = 4
    T = G // QC
    with Phase(nc, name) as ctx:
        sem, sb, bank = ctx.sem, ctx.sb, ctx.bank
        gathered = [sem("gathered0"), sem("gathered1")]
        scattered = [sem("scattered0"), sem("scattered1")]
        from_ready, flags_ready, rows_used, scan = sem("from_ready"), sem("flags_ready"), sem("rows_used"), sem("scan")
        fixed, fix_in, fix_out, carried, fix_clear = sem("fixed"), sem("fix_in"), sem("fix_out"), sem("carried"), sem("fix_clear")
        idx_from = sb("idx_from", [LANES, 2, NG, G], I32)
        idx_to = sb("idx_to", [LANES, 2, G], I32)
        flags = sb("flags", [LANES, 2, NS, G])
        rows = sb("rows", [LANES, 2, G, NG * W])
        out = sb("out", [LANES, 2, G, width])
        fix = sb("fix", [LANES, width])
        chain = sb("chain", [LANES, 2, G, D]) if mean else out
        source = rows if mean else out
        ps_c = bank("ps_c")
        if beside is not None:
            sort = EdgeSort(nc, m, ctx, *beside)
            zero_tile, zeroed_d, zeroed_s = sem("zero_tile"), sem("zeroed_d"), sem("zeroed_s")
            zero = sb("zero", [LANES, m.tcols * ROW2 // ZERO_PIECES])
        begun = sem("begun")
        if mean:
            scaled = sem("scaled")
        else:
            step, act_math = sem("step"), sem("act_math")
            turned, turned_copied, projected, proj_copied, proj_used = sem("turned"), sem("turned_copied"), sem("projected"), sem("proj_copied"), sem("proj_used")
            projection = m.wg if cosine else m.wqkv
            PW = projection.shape[1]
            prod = sb("prod", [LANES, G, D])
            turned_rows = sb("turned_rows", [P, 2, QC * LANES])
            proj = sb("proj", [LANES, 2, G, PW])
            ps_t = [bank("ps_t0"), bank("ps_t1")]
            ps_q = [bank(f"ps_q{i}") for i in range(4)]
        if cosine:
            sq_read, biased = sem("sq_read"), sem("biased")
            sq = sb("sq", [LANES, G, 2 * D])
            dot, nrm, sim, att = sb("dot", [LANES, G]), sb("nrm", [LANES, G, 2]), sb("sim", [LANES, 2, G]), sb("att", [LANES, G])
        if heads:
            att, wts = sb("att", [LANES, G * HEADS]), sb("wts", [LANES, G * HEADS])
        block = ctx.block()

        if beside is not None:
            @block.sync
            def _(sp):
                sp.wait_ge(zero_tile, 1)
                for table, zeroed in ((m.sum_d, zeroed_d), (m.sum_s, zeroed_s)):
                    rows_of_zero = table.rearrange("(p t) d -> p (t d)", p=LANES)
                    piece = m.tcols * table.shape[1] // ZERO_PIECES
                    for i in range(ZERO_PIECES):
                        sp.dma_start(rows_of_zero[:, i * piece:(i + 1) * piece], zero[:, 0:piece]).then_inc(zeroed, DMA)
                    if table is m.sum_d:
                        sort.sync_load(sp)
                sort.sync_store(sp)
                sp.wait_ge(zeroed_s, ZERO_PIECES * DMA)

        @block.gpsimd
        def _(pool):
            def gathers(c, h, u):
                need(pool, from_ready, c + 1)
                need(pool, rows_used, c - 1)
                pool.sem_inc(begun)
                for g in range(NG):
                    for j in range(G):
                        pool.indirect_dma_start(out=rows[:, h, j, g * W:(g + 1) * W], out_offset=None,
                                                in_=tables[g], in_offset=at(idx_from[:, h, g, j:j + 1])
                                                ).then_inc(gathered[h], DMA)

            def scatters(c, h, u):
                need(pool, flags_ready, c + 1)
                if mean:
                    need(pool, scaled, c + 1)
                else:
                    need(pool, scan, G * c + G + 1)
                if beside is not None and isinstance(c, int) and c == 0:
                    pool.wait_ge(zeroed_d, ZERO_PIECES * DMA)
                pool.sem_inc(begun)
                for j in range(G):
                    pool.indirect_dma_start(out=sums, out_offset=at(idx_to[:, h, j:j + 1]), in_=out[:, h, j, :],
                                            in_offset=None, bounds_check=m.nodes - 1, oob_is_err=False
                                            ).then_inc(scattered[h], DMA)

            pool.memset(fix[:, :], 0.0).then_inc(fix_clear, 1)
            if beside is not None:
                pool.memset(zero[:, :], 0.0).then_inc(zero_tile, 1)
                sort.pool_pad(pool)
            rounds(pool, NCH, [(gathers, 0), (scatters, 1)])
            for h in range(2):
                pool.wait_ge(scattered[h], SCATTERED * NI)
            pool.wait_ge(fix_clear, 1)
            pool.indirect_dma_start(out=fix[:, :], out_offset=None, in_=sums, in_offset=at(fix_idx[:, 0:1]),
                                    bounds_check=m.nodes - 1, oob_is_err=False).then_inc(fix_in, DMA)
            pool.wait_ge(fixed, 1)
            pool.indirect_dma_start(out=sums, out_offset=at(fix_idx[:, 0:1]), in_=fix[:, :], in_offset=None,
                                    bounds_check=m.nodes - 1, oob_is_err=False).then_inc(fix_out, DMA)
            pool.wait_ge(fix_out, DMA)

        @block.scalar
        def _(act):
            def stage_from(c, h, u):
                need(act, gathered[h], GATHERED * u)
                act.copy(idx_from[:, h, :, :], plan[:, c, 0:NG, :]).then_inc(from_ready, 1)

            def stage_flags(c, h, u):
                need(act, scattered[h], SCATTERED * u)
                act.copy(idx_to[:, h, :], plan[:, c, NG, :])
                act.copy(flags[:, h, :, :], plan[:, c, NG + 1:NF, :]).then_inc(flags_ready, 1)

            def copy_projections(c, h, q):
                for n in (2 * q, 2 * q + 1):
                    need(act, projected, 2 * T * c + n + 1)
                    if n == 0:
                        need(act, proj_used, c - 1)
                    act.copy(proj[:, h, 2 * n:2 * n + 2, :],
                             ps_q[(2 * T * h + n) % 4][0:LANES, :].rearrange("p (a b) -> p a b", a=2)[:, :, 0:PW]
                             ).then_inc(proj_copied, 1)

            def lengths(c, h, u):
                need(act, biased, c + 1)
                need(act, sq_read, c)
                act.activation(sq[:, :, :], proj[:, h, :, :], ACT.Square).then_inc(act_math, 1)
                need(act, sq_read, c + 1)
                act.activation(nrm[:, :, :], nrm[:, :, :], ACT.Sqrt).then_inc(act_math, 1)

            def projections(c, h, u):
                for q in range(T):
                    need(act, turned, T * c + q + 1)
                    need(act, projected, 2 * (T * c + q - 1))
                    act.copy(turned_rows[:, (T * h + q) % 2, :], ps_t[(T * h + q) % 2][:, 0:QC * LANES]).then_inc(turned_copied, 1)
                    if q:
                        copy_projections(c, h, q - 1)
                copy_projections(c, h, T - 1)

            def exponentials(c, h, u):
                need(act, step, 5 * c + 3)
                act.activation(wts[:, :], att[:, :], ACT.Exp).then_inc(act_math, 1)

            own = [(projections, 0), (lengths, 0)] if cosine else [(projections, 0), (exponentials, 0)] if heads else []
            if beside is None:
                rounds(act, NCH, [(stage_from, 0), (stage_flags, 0)] + own)
            else:
                for c in range(NCH):
                    stage_from(c, c % 2, c // 2)
                    stage_flags(c, c % 2, c // 2)
                    if c == 0:
                        sort.scalar_prepare(act)
                    sort.scalar_steps(act, sort.part(c, NCH))

        @block.tensor
        def _(pe):
            def turn(c, h, q):
                need(pe, turned_copied, T * c + q - 1)
                for r in range(QC):
                    ins = pe.transpose(ps_t[(T * h + q) % 2][:, r * LANES:(r + 1) * LANES], rows[:, h, QC * q + r, :],
                                       m.ident[0:LANES, 0:LANES])
                ins.then_inc(turned, 1)

            def project(c, h, q):
                need(pe, turned_copied, T * c + q + 1)
                for n in (2 * q, 2 * q + 1):
                    need(pe, proj_copied, 2 * T * c + n - 3)
                    for r in range(2):
                        col = (n % 2) * 2 + r
                        ins = pe.matmul(ps_q[(2 * T * h + n) % 4][0:LANES, r * 256:r * 256 + PW],
                                        turned_rows[:, (T * h + q) % 2, col * LANES:(col + 1) * LANES],
                                        projection[:, :], start=True, stop=True)
                    ins.then_inc(projected, 1)

            def project_chunk(c, h, u):
                need(pe, gathered[h], GATHERED * (u + 1))
                turn(c, h, 0)
                for q in range(1, T):
                    turn(c, h, q)
                    project(c, h, q - 1)
                need(pe, turned, T * (c + 1))
                pe.nop().then_inc(rows_used, 1)
                project(c, h, T - 1)

            if not mean:
                rounds(pe, NCH, [(project_chunk, 0)])
            if beside is not None:
                sort.tensor_steps(pe, sort.steps)
            pe.wait_ge(scan, G * NCH + 1)
            pe.matmul(ps_c[0:LANES, 0:SW], carry_mask[:, :], chain[:, 1, G - 1, 0:SW], start=True, stop=True).then_inc(carried, 1)

        @block.vector
        def _(vec):
            STEPS = {"mean": 0, "cosine": 8, "heads": 5}[kind]

            def messages(c, h, u):
                n = 0

                def did(ins):
                    nonlocal n
                    n += 1
                    ins.then_inc(step, 1)
                    need(vec, step, STEPS * c + n)

                if cosine:
                    wr, wc = proj[:, h, :, 0:D], proj[:, h, :, D:2 * D]
                    vec.wait_ge(proj_copied, 2 * T * (c + 1))
                    both = proj[:, h, :, :].rearrange("p g (a d) -> p (g a) d", a=2)
                    vec.tensor_tensor(both, both, m.bg[:, :].unsqueeze(1).to_broadcast([LANES, 2 * G, D]), ALU.add
                                      ).then_inc(biased, 1)
                    vec.wait_ge(biased, c + 1)
                    did(vec.tensor_tensor(prod[:, :, :], wr, wc, ALU.mult))
                    vec.tensor_reduce(dot[:, :], prod[:, :, :], AX_X, ALU.add)
                    vec.wait_ge(act_math, 2 * c + 1)
                    vec.tensor_reduce(nrm[:, :, :], sq[:, :, :].rearrange("p g (a d) -> p g a d", a=2), AX_X, ALU.add).then_inc(sq_read, 1)
                    vec.wait_ge(act_math, 2 * c + 2)
                    did(vec.tensor_tensor(att[:, :], nrm[:, :, 0], nrm[:, :, 1], ALU.mult))
                    did(vec.tensor_scalar(att[:, :], att[:, :], 1e-8, None, ALU.max))
                    did(vec.reciprocal(att[:, :], att[:, :]))
                    did(vec.tensor_tensor(dot[:, :], dot[:, :], att[:, :], ALU.mult))
                    vec.tensor_scalar(sim[:, 0, :], dot[:, :], 0.0, m.mix[:, 0:1], ALU.max, ALU.mult)
                    did(vec.tensor_scalar(sim[:, 1, :], dot[:, :], 0.0, m.mix[:, 1:2], ALU.min, ALU.mult))
                    did(vec.tensor_tensor(att[:, :], sim[:, 0, :], sim[:, 1, :], ALU.add))
                    did(vec.tensor_tensor(att[:, :], att[:, :], flags[:, h, flag("base"), :], ALU.mult))
                    need(vec, scattered[h], SCATTERED * u)
                    vec.tensor_tensor(out[:, h, :, 0:D], wc, att[:, :].unsqueeze(2).to_broadcast([LANES, G, D]), ALU.mult
                                      ).then_inc(proj_used, 1)
                    vec.wait_ge(proj_used, c + 1)
                if heads:
                    vec.wait_ge(proj_copied, 2 * T * (c + 1))
                    did(vec.tensor_tensor(prod[:, :, :], proj[:, h, :, 0:D], proj[:, h, :, D:2 * D], ALU.mult))
                    did(vec.tensor_reduce(att[:, :], prod[:, :, :].rearrange("p g (a d) -> p (g a) d", a=HEADS), AX_X, ALU.add))
                    did(vec.tensor_scalar(att[:, :], att[:, :], 10.0, -10.0, ALU.min, ALU.max))
                    vec.wait_ge(act_math, c + 1)
                    need(vec, scattered[h], SCATTERED * u)
                    did(vec.tensor_copy(out[:, h, :, D:ROW2], wts[:, :].rearrange("p (g a) -> p g a", a=HEADS)))
                    did(vec.tensor_copy(prod[:, :, :].rearrange("p g (a d) -> p (g a) d", a=HEADS),
                                        wts[:, :].unsqueeze(2).to_broadcast([LANES, G * HEADS, DH])))
                    vec.tensor_tensor(out[:, h, :, 0:D], proj[:, h, :, 2 * D:3 * D], prod[:, :, :], ALU.mult).then_inc(proj_used, 1)
                    vec.wait_ge(proj_used, c + 1)
                assert n == STEPS, n

            def chunk(c, h, u):
                need(vec, gathered[h], GATHERED * (u + 1))
                vec.wait_ge(flags_ready, c + 1)
                messages(c, h, u)
                for j in range(G):
                    prev = chain[:, 1 - h, G - 1, 0:SW] if j == 0 else chain[:, h, j - 1, 0:SW]
                    vec.wait_ge(scan, G * c + j + 1)
                    vec.scalar_tensor_tensor(out=chain[:, h, j, 0:SW], in0=prev, scalar=flags[:, h, flag("same"), j:j + 1],
                                             in1=source[:, h, j, 0:SW], op0=ALU.mult, op1=ALU.add).then_inc(scan, 1)
                if mean:
                    vec.wait_ge(scan, G * c + G + 1)
                    vec.nop().then_inc(rows_used, 1)
                    need(vec, scattered[h], SCATTERED * u)
                    vec.tensor_tensor(out[:, h, :, :], chain[:, h, :, :],
                                      flags[:, h, flag("inv"), :].unsqueeze(2).to_broadcast([LANES, G, D]), ALU.mult
                                      ).then_inc(scaled, 1)

            if not mean:
                vec.memset(out[:, 0, :, :], 0.0)
            vec.memset(chain[:, 1, :, :], 0.0).then_inc(scan, 1)
            if beside is None:
                rounds(vec, NCH, [(chunk, 0)])
            else:
                sort.vector_prepare(vec)
                for c in range(NCH):
                    sort.vector_steps(vec, sort.part(c, NCH))
                    chunk(c, c % 2, c // 2)
                sort.vector_finish(vec)
            vec.wait_ge(fix_in, DMA)
            vec.wait_ge(carried, 1)
            if mean:
                vec.scalar_tensor_tensor(out=fix[:, 0:SW], in0=ps_c[0:LANES, 0:SW], scalar=fix_inv[:, 0:1], in1=fix[:, 0:SW],
                                         op0=ALU.mult, op1=ALU.add).then_inc(fixed, 1)
            else:
                vec.tensor_tensor(fix[:, 0:SW], ps_c[0:LANES, 0:SW], fix[:, 0:SW], ALU.add).then_inc(fixed, 1)


def node_phase(nc, m, name, kind, loads, weights, bias, dst):
    NCH = m.tcols // K
    relu, unit, cosine, heads, plain = (kind == k for k in ("relu", "unit", "cosine", "heads", "plain"))
    products = not heads
    S = K // SUB
    PAIRS = SUB // 2
    ow = dst.shape[1]
    LOADED = DMA * 2
    with Phase(nc, name) as ctx:
        sem, sb, bank = ctx.sem, ctx.sb, ctx.bank
        loaded, stored = [sem("loaded0"), sem("loaded1")], [sem("stored0"), sem("stored1")]
        out_ready = sem("out_ready")
        if products:
            turned, turned_copied, multiplied, evacuated = sem("turned"), sem("turned_copied"), sem("multiplied"), sem("evacuated")
            TURNED = len(weights)
            tcp = sb("tcp", [P, 2, TURNED, PAIRS, LANES])
            ps_t = [[bank(f"ps_t{b}{e}") for e in range(TURNED)] for b in range(2)]
            ps_o = [bank("ps_o0"), bank("ps_o1")]
        tin = [sb(f"in{n}", [LANES, 2, K, t.shape[1]]) for n, t in enumerate(loads)]
        out = sb("out", [LANES, 2, K, ow])
        raw = sb("raw", [LANES, 2, K, D])
        if not relu:
            raw_ready, xs_ready, var_ready, rooted = sem("raw_ready"), sem("xs_ready"), sem("var_ready"), sem("rooted")
            rstd_ready, xn_ready, step, fin = sem("rstd_ready"), sem("xn_ready"), sem("step"), sem("fin")
            xs, xn = sb("xs", [LANES, 2, K, D]), sb("xn", [LANES, 2, K, D])
            st = sb("st", [LANES, 2, K, nc.vector.BN_STATS_DIM])
            msum, mdif, var = sb("msum", [LANES, 2, K]), sb("mdif", [LANES, K]), sb("var", [LANES, 2, K])
            rstd, shift = sb("rstd", [LANES, 2, K]), sb("shift", [LANES, 2, K])
            eps = sb("eps", [LANES, 1])
        if cosine:
            prod = sb("prod", [LANES, K, D])
        if unit:
            x_loaded = [sem("x_loaded0"), sem("x_loaded1")]
            squared, length_sq, length, unit_ready, unit_step, scaled = sem("squared"), sem("length_sq"), sem("length"), sem("unit_ready"), sem("unit_step"), sem("scaled")
            sq, ss, rlen = sb("sq", [LANES, K, D]), sb("ss", [LANES, 2, K]), sb("rlen", [LANES, 2, K])
        if heads:
            rden, rden_step, divided = sb("rden", [LANES, 2, K * HEADS]), sem("rden_step"), sem("divided")
        block = ctx.block()
        in_cols = [columns(t) for t in loads]
        out_cols = columns(dst)
        wide = lambda t, h: t[:, h, :].unsqueeze(2).to_broadcast([LANES, K, D])
        LAG = 6 if unit else 3 if relu else 4 if heads else 5

        @block.sync
        def _(sp):
            def load(c, h, u):
                if products:
                    need(sp, turned, S * (c - 1))
                if heads:
                    need(sp, xs_ready, c - 1)
                if plain or cosine:
                    need(sp, raw_ready, c - 1)
                for t, cols in zip(tin[0:2], in_cols):
                    sp.dma_start(t[:, h, :, :], cols[:, bass.ds(c * K, K), :]).then_inc(loaded[h], DMA)

            def load_x(c, h, u):
                need(sp, xs_ready, c - 1)
                sp.dma_start(tin[2][:, h, :, :], in_cols[2][:, bass.ds(c * K, K), :]).then_inc(x_loaded[h], DMA)

            def store(c, h, u):
                need(sp, out_ready, c + 1)
                sp.dma_start(out_cols[:, bass.ds(c * K, K), :], out[:, h, :, :]).then_inc(stored[h], DMA)

            rounds(sp, NCH, [(load, 0)] + ([(load_x, 2)] if unit else []) + [(store, LAG)])
            for h in range(2):
                sp.wait_ge(stored[h], DMA * (NCH // 2))

        @block.tensor
        def _(pe):
            def turn(s):
                def stage(c, h, u):
                    need(pe, loaded[h], LOADED * (u + 1))
                    need(pe, turned_copied, S * c + s - 1)
                    for e in range(TURNED):
                        for q in range(PAIRS):
                            col = SUB * s + 2 * q
                            ins = pe.transpose(ps_t[s % 2][e][:, q * LANES:(q + 1) * LANES],
                                               tin[e][:, h, col:col + 2, :].rearrange("p a d -> p (a d)"),
                                               m.ident[0:LANES, 0:LANES])
                    ins.then_inc(turned, 1)
                return stage

            def multiply(s):
                def stage(c, h, u):
                    need(pe, turned_copied, S * c + s + 1)
                    need(pe, evacuated, S * c + s - 1)
                    for q in range(PAIRS):
                        for e in range(TURNED):
                            ins = pe.matmul(ps_o[s % 2][0:LANES, q * P:(q + 1) * P], tcp[:, s % 2, e, q, :],
                                            weights[e][:, :], start=(e == 0), stop=(e == TURNED - 1))
                    ins.then_inc(multiplied, 1)
                return stage

            if products:
                rounds(pe, NCH, [(turn(0), 0), (multiply(0), 1), (turn(1), 0), (multiply(1), 1)])

        @block.scalar
        def _(act):
            def copy_turned(s):
                def stage(c, h, u):
                    need(act, turned, S * c + s + 1)
                    need(act, multiplied, S * c + s - 1)
                    for e in range(TURNED):
                        ins = act.copy(tcp[:, s % 2, e, :, :],
                                       ps_t[s % 2][e][:, 0:PAIRS * LANES].rearrange("p (a b) -> p a b", a=PAIRS))
                    ins.then_inc(turned_copied, 1)
                return stage

            def square(c, h, u):
                need(act, raw_ready, c + 1)
                need(act, length_sq, c)
                act.activation(sq[:, :, :], raw[:, h, :, :], ACT.Square).then_inc(squared, 1)

            def root_length(c, h, u):
                need(act, length_sq, c + 1)
                act.activation(ss[:, h, :], ss[:, h, :], ACT.Sqrt).then_inc(length, 1)

            def root_variance(c, h, u):
                need(act, var_ready, c + 1)
                act.activation(var[:, h, :], var[:, h, :], ACT.Sqrt, bias=eps[:, 0:1], scale=1.0 / D).then_inc(rooted, 1)

            if relu:
                rounds(act, NCH, [(copy_turned(0), 0), (copy_turned(1), 0)])
            elif unit:
                rounds(act, NCH, [(square, 2), (root_variance, 4), (copy_turned(0), 0), (root_length, 2), (copy_turned(1), 0)])
            elif plain or cosine:
                rounds(act, NCH, [(root_variance, 3), (copy_turned(0), 0), (copy_turned(1), 0)])
            else:
                rounds(act, NCH, [(root_variance, 1)])

        @block.gpsimd
        def _(pool):
            def unit_sum(c, h, u):
                need(pool, unit_ready, c + 1)
                need(pool, x_loaded[h], DMA * (u + 1))
                need(pool, var_ready, c - 1)
                need(pool, xn_ready, c - 1)
                pool.tensor_tensor(xs[:, h, :, :], raw[:, h, :, :], wide(rlen, h), ALU.mult).then_inc(scaled, 1)
                need(pool, scaled, c + 1)
                pool.tensor_tensor(xs[:, h, :, :], xs[:, h, :, :], tin[2][:, h, :, :], ALU.add).then_inc(xs_ready, 1)

            def first_sum(c, h, u):
                need(pool, loaded[h], LOADED * (u + 1))
                need(pool, xs_ready, c - 1)
                other = bias[:, :].unsqueeze(1).to_broadcast([LANES, K, D]) if plain else tin[1][:, h, :, 0:D]
                pool.tensor_tensor(raw[:, h, :, :], tin[0][:, h, :, :], other, ALU.add).then_inc(raw_ready, 1)

            def divide(c, h, u):
                need(pool, raw_ready, c + 1)
                need(pool, xs_ready, c - 1)
                pool.tensor_tensor(raw[:, h, :, :].rearrange("p k (a d) -> p k a d", a=HEADS),
                                   tin[1][:, h, :, 0:D].rearrange("p k (a d) -> p k a d", a=HEADS),
                                   rden[:, h, :].rearrange("p (k a) -> p k a", a=HEADS).unsqueeze(3).to_broadcast([LANES, K, HEADS, DH]),
                                   ALU.mult).then_inc(divided, 1)

            def normalise(c, h, u):
                need(pool, rstd_ready, c + 1)
                need(pool, out_ready, c - 1)
                pool.tensor_tensor(xn[:, h, :, :], xs[:, h, :, :], wide(rstd, h), ALU.mult).then_inc(xn_ready, 1)

            if not relu:
                rounds(pool, NCH, [(normalise, 4), (unit_sum, 2)] if unit else
                       [(divide, 0), (normalise, 1)] if heads else [(first_sum, 0), (normalise, 3)])

        @block.vector
        def _(vec):
            def chain(counter, per_chunk, c):
                n = 0

                def did(ins):
                    nonlocal n
                    n += 1
                    ins.then_inc(counter, 1)
                    need(vec, counter, per_chunk * c + n)
                return did

            def evacuate(c, h, u):
                if unit:
                    need(vec, xs_ready, c - 1)
                if plain or cosine:
                    need(vec, raw_ready, c + 1)
                if cosine:
                    need(vec, xs_ready, c)
                if plain:
                    need(vec, xn_ready, c - 1)
                for s in range(S):
                    need(vec, multiplied, S * c + s + 1)
                    cols = slice(SUB * s, SUB * (s + 1))
                    target = xs[:, h, cols, :] if plain else prod[:, cols, :] if cosine else raw[:, h, cols, :]
                    other = raw[:, h, cols, :] if plain else bias[:, :].unsqueeze(1).to_broadcast([LANES, SUB, D])
                    vec.tensor_tensor(target, ps_o[s % 2][0:LANES, :].rearrange("p (a d) -> p a d", d=D), other, ALU.add
                                      ).then_inc(evacuated, 1)
                need(vec, evacuated, S * (c + 1))
                if unit or plain:
                    vec.nop().then_inc(raw_ready if unit else xs_ready, 1)

            def leaky(c, h, u):
                need(vec, stored[h], DMA * u)
                vec.scalar_tensor_tensor(out=out[:, h, :, :], in0=raw[:, h, :, :], scalar=0.01, in1=raw[:, h, :, :],
                                         op0=ALU.mult, op1=ALU.max).then_inc(out_ready, 1)

            def add_product(c, h, u):
                need(vec, xn_ready, c - 1)
                vec.scalar_tensor_tensor(out=xs[:, h, :, :], in0=prod[:, :, :], scalar=m.mix[:, 2:3],
                                         in1=raw[:, h, :, :], op0=ALU.mult, op1=ALU.add).then_inc(xs_ready, 1)

            def invert_weights(c, h, u):
                need(vec, loaded[h], LOADED * (u + 1))
                need(vec, divided, c - 1)
                vec.tensor_scalar(rden[:, h, :].rearrange("p (k a) -> p k a", a=HEADS), tin[1][:, h, :, D:ROW2], 1e-8, None,
                                  ALU.add).then_inc(rden_step, 1)
                need(vec, rden_step, c + 1)
                vec.reciprocal(rden[:, h, :], rden[:, h, :]).then_inc(raw_ready, 1)

            def add_x(c, h, u):
                need(vec, divided, c + 1)
                need(vec, xn_ready, c - 1)
                vec.tensor_tensor(xs[:, h, :, :], raw[:, h, :, :], tin[0][:, h, :, :], ALU.add).then_inc(xs_ready, 1)

            def sum_squares(c, h, u):
                need(vec, squared, c + 1)
                vec.tensor_reduce(ss[:, h, :], sq[:, :, :], AX_X, ALU.add).then_inc(length_sq, 1)

            def invert_length(c, h, u):
                need(vec, length, c + 1)
                vec.tensor_scalar(rlen[:, h, :], ss[:, h, :], 1e-12, None, ALU.max).then_inc(unit_step, 1)
                need(vec, unit_step, c + 1)
                vec.reciprocal(rlen[:, h, :], rlen[:, h, :]).then_inc(unit_ready, 1)

            def statistics(c, h, u):
                did = chain(step, 4, c)
                need(vec, xs_ready, c + 1)
                for j in range(K):
                    ins = vec.bn_stats(st[:, h, j, :], xs[:, h, j, :])
                did(ins)
                vec.tensor_tensor(msum[:, h, :], st[:, h, :, 1], st[:, h, :, 4], ALU.add)
                vec.tensor_tensor(var[:, h, :], st[:, h, :, 2], st[:, h, :, 5], ALU.add)
                did(vec.tensor_tensor(mdif[:, :], st[:, h, :, 1], st[:, h, :, 4], ALU.subtract))
                did(vec.tensor_tensor(mdif[:, :], mdif[:, :], mdif[:, :], ALU.mult))
                did(vec.scalar_tensor_tensor(out=var[:, h, :], in0=mdif[:, :], scalar=D / 4.0, in1=var[:, h, :],
                                             op0=ALU.mult, op1=ALU.add))
                vec.nop().then_inc(var_ready, 1)

            def invert_deviation(c, h, u):
                need(vec, rooted, c + 1)
                need(vec, xn_ready, c - 1)
                vec.reciprocal(rstd[:, h, :], var[:, h, :]).then_inc(fin, 1)
                need(vec, fin, c + 1)
                vec.scalar_tensor_tensor(out=shift[:, h, :], in0=msum[:, h, :], scalar=-0.5, in1=rstd[:, h, :],
                                         op0=ALU.mult, op1=ALU.mult).then_inc(rstd_ready, 1)

            def shift_out(c, h, u):
                need(vec, xn_ready, c + 1)
                need(vec, rstd_ready, c + 1)
                need(vec, stored[h], DMA * u)
                vec.tensor_tensor(out[:, h, :, :], xn[:, h, :, :], wide(shift, h),
                                  ALU.add).then_inc(out_ready, 1)

            if not relu:
                vec.memset(eps[:, :], 1e-5)
            if relu:
                rounds(vec, NCH, [(evacuate, 1), (leaky, 1)])
            if unit:
                rounds(vec, NCH, [(evacuate, 1), (invert_deviation, 4), (sum_squares, 2), (invert_length, 2), (statistics, 3),
                                  (shift_out, 4)])
            if plain:
                rounds(vec, NCH, [(invert_deviation, 3), (statistics, 2), (evacuate, 1), (shift_out, 3)])
            if cosine:
                rounds(vec, NCH, [(invert_deviation, 3), (statistics, 2), (evacuate, 1), (add_product, 1), (shift_out, 3)])
            if heads:
                rounds(vec, NCH, [(add_x, 1), (statistics, 1), (invert_weights, 0), (invert_deviation, 1), (shift_out, 2)])


def gnn_kernel(nc, w, out):
    m = Memory()
    m.nodes, m.edges = w["x"].shape[0], w["src"].shape[0]
    assert m.nodes % LANES == 0 and m.edges % LANES == 0
    m.tcols, m.ecols = m.nodes // LANES, m.edges // LANES
    assert m.tcols % (2 * K) == 0 and m.ecols % (2 * G) == 0
    NCH = m.ecols // G
    with ExitStack() as ctx:
        def dram(name, shape, dt=F32):
            return nc.dram_tensor(name, shape, dt, kind="Internal").ap()

        sb = lambda x, shape, dt=F32: ctx.enter_context(nc.sbuf_tensor(x, shape, dt))
        m.sum_d, m.sum_s = dram("sum_d", (m.nodes, D)), dram("sum_s", (m.nodes, ROW2))
        h1, x1, x2, x3 = (dram(n, (m.nodes, D)) for n in ("h1", "x1", "x2", "x3"))
        s_key, s_other, s_base = dram("s_key", (m.edges,), I32), dram("s_other", (m.edges,), I32), dram("s_base", (m.edges,))
        m.d_key, m.d_other = dram("d_key", (m.edges,), I32), dram("d_other", (m.edges,), I32)
        m.unsorted = sb("unsorted", [1, 1], I32)
        m.ident, m.before, m.sgn = sb("ident", [P, P]), sb("before", [LANES, LANES]), sb("sgn", [P, 8])
        m.ones = sb("ones", [P, P])
        m.deg, m.mix = sb("deg", [P, 2]), sb("mix", [LANES, 3])
        m.b1, m.b2, m.bg, m.b3 = (sb(b, [LANES, D]) for b in ("b1", "b2", "bg", "b3"))
        m.w1l, m.w1r, m.w2l, m.w2r, m.wg, m.w3x, m.w3m = (
            sb(n, [P, P]) for n in ("w1l", "w1r", "w2l", "w2r", "wg", "w3x", "w3m"))
        m.wqkv = sb("wqkv", [P, 3 * D])
        by_dst, by_src = ["from", "to", "same", "inv"], ["from_a", "from_b", "to", "same", "base"]
        plan_d = sb("plan_d", [LANES, NCH, len(by_dst), G])
        plan_s = sb("plan_s", [LANES, NCH, len(by_src), G])
        mask_d, mask_s = sb("mask_d", [LANES, LANES]), sb("mask_s", [LANES, LANES])
        fix_d, fix_s = sb("fix_d", [LANES, 1], I32), sb("fix_s", [LANES, 1], I32)
        inv_d = sb("inv_d", [LANES, 1])

        set_up(nc, m, w)
        sort_if(nc, m, "sort_dst_", m.unsorted[0:1, 0:1], w["dst"], w["src"], m.d_key, m.d_other)
        edge_plan(nc, m, "plan_dst_", m.d_key, {"from": (m.d_other, I32)}, plan_d, by_dst, mask_d, fix_d, inv_d)
        edge_phase(nc, m, "e0_", "mean", [w["x"]], plan_d, by_dst, m.sum_d, mask_d, fix_d, inv_d,
                   beside=(w["src"], w["dst"], (w["edge_weight"], w["edge_weight_n2"]), s_key, s_other, s_base))
        edge_plan(nc, m, "plan_src_", s_key, {"from_a": (s_key, I32), "from_b": (s_other, I32), "base": (s_base, F32)},
                  plan_s, by_src, mask_s, fix_s, None)
        node_phase(nc, m, "n0_", "relu", [w["x"], m.sum_d], (m.w1r, m.w1l), m.b1, h1)
        edge_phase(nc, m, "e1_", "mean", [h1], plan_d, by_dst, m.sum_d, mask_d, fix_d, inv_d)
        node_phase(nc, m, "n1_", "unit", [h1, m.sum_d, w["x"]], (m.w2r, m.w2l), m.b2, x1)
        edge_phase(nc, m, "e2_", "cosine", [x1, x1], plan_s, by_src, m.sum_s, mask_s, fix_s)
        node_phase(nc, m, "n2_", "cosine", [x1, m.sum_s], (m.wg,), m.bg, x2)
        edge_phase(nc, m, "e3_", "heads", [x2, x2], plan_s, by_src, m.sum_s, mask_s, fix_s)
        node_phase(nc, m, "n3_", "heads", [x2, m.sum_s], None, None, x3)
        edge_phase(nc, m, "e4_", "mean", [x3], plan_d, by_dst, m.sum_d, mask_d, fix_d, inv_d)
        node_phase(nc, m, "n4_", "plain", [x3, m.sum_d], (m.w3x, m.w3m), m.b3, out)


def kernel(x, src, dst, edge_weight, edge_weight_n2, L0_gnn_W1_l, L0_gnn_b1, L0_gnn_W1_r, L0_gnn_W2_l, L0_gnn_b2,
           L0_gnn_W2_r, L1_gnn_W, L1_gnn_b, L1_gnn_deg_coeff, L1_gnn_coeff_param, L1_gnn_scale_param, L2_gnn_Wq,
           L2_gnn_Wk, L2_gnn_Wv, L3_gnn_W, L3_gnn_b):
    import numpy as np
    import concourse.bacc as bacc
    from concourse.bass_utils import run_bass_kernel_spmd

    arrays = {
        "x": x, "src": src, "dst": dst, "edge_weight": edge_weight, "edge_weight_n2": edge_weight_n2,
        "w1l": np.transpose(L0_gnn_W1_l), "w1r": np.transpose(L0_gnn_W1_r), "b1": L0_gnn_b1,
        "w2l": np.transpose(L0_gnn_W2_l), "w2r": np.transpose(L0_gnn_W2_r), "b2": L0_gnn_b2,
        "wg": L1_gnn_W, "bg": L1_gnn_b, "deg_coeff": L1_gnn_deg_coeff, "coeff": L1_gnn_coeff_param,
        "scale": L1_gnn_scale_param, "wq": L2_gnn_Wq, "wk": L2_gnn_Wk, "wv": L2_gnn_Wv,
        "w3x": L3_gnn_W[0:D], "w3m": L3_gnn_W[D:2 * D], "b3": L3_gnn_b,
    }
    arrays = {k: np.ascontiguousarray(v) for k, v in arrays.items()}
    q = np.arange(P)
    bit = lambda b: 1 - 2 * ((q >> b) & 1)
    arrays["ident"] = np.eye(P, dtype=np.float32)
    arrays["before"] = np.triu(np.ones((LANES, LANES), np.float32), 1)
    arrays["sgn"] = np.stack([bit(0)] + [bit(b) * bit(b - 1) for b in range(1, 7)] + [bit(6)], 1).astype(np.float32)

    nc = bacc.Bacc("TRN2", target_bir_lowering=False, num_devices=1)
    w = {k: nc.dram_tensor(f"in_{k}", a.shape, mybir.dt.from_np(a.dtype), kind="ExternalInput").ap()
         for k, a in arrays.items()}
    out = nc.dram_tensor("out_0", x.shape, F32, kind="ExternalOutput").ap()
    gnn_kernel(nc, w, out)
    r = run_bass_kernel_spmd(nc, [{f"in_{k}": a for k, a in arrays.items()}], core_ids=[0])
    return r.results[0]["out_0"]
```

```python
from contextlib import ExitStack

import concourse.bass as bass
from concourse import mybir

ALU = mybir.AluOpType
ACT = mybir.ActivationFunctionType
AX_X = mybir.AxisListType.X
F32 = mybir.dt.float32
I32 = mybir.dt.int32

P = 128
LANES = 125
D = 64
HEADS = 4
DH = D // HEADS
ROW2 = D + HEADS
G = 28
K = 16
SUB = 8
SKIP = 1 << 20
ZERO_PIECES = 16
DMA = 16


def at(offset_ap):
    return bass.IndirectOffsetOnAxis(ap=offset_ap, axis=0)


class Memory:
    pass


class Phase(ExitStack):

    def __init__(self, nc, name):
        super().__init__()
        self.nc, self.name, self.sems = nc, name, []

    def sem(self, x):
        self.sems.append(self.nc.alloc_semaphore(self.name + x))
        return self.sems[-1]

    def sb(self, x, shape, dt=F32):
        return self.enter_context(self.nc.sbuf_tensor(self.name + x, shape, dt))

    def bank(self, x):
        return self.enter_context(self.nc.psum_tensor(self.name + x, [P, 512], F32))

    def block(self):
        return self.enter_context(self.nc.Block())

    def __exit__(self, *error):
        ended = super().__exit__(*error)
        if error[0] is None:
            self.nc.clear_and_free_semaphores(self.sems)
            self.nc.all_engine_barrier()
        return ended


def need(engine, sem, value):
    if not isinstance(value, int) or value > 0:
        engine.wait_ge(sem, value)


def rounds(engine, count, stages):
    last = max(lag for _, lag in stages)
    first = 2 + last + last % 2

    def straight(t):
        for f, lag in stages:
            if 0 <= t - lag < count:
                f(t - lag, (t - lag) % 2, (t - lag) // 2)

    assert count % 2 == 0 and count > first
    for t in range(first):
        straight(t)
    with engine.Fori(first // 2, count // 2) as i:
        for k in range(2):
            for f, lag in stages:
                f(2 * i + (k - lag), (k - lag) % 2, i + (k - lag) // 2)
    for t in range(count, count + last):
        straight(t)


def columns(dram):
    return dram.rearrange("(p t) d -> p t d", p=LANES)


def row_parts(tile, dram, count):
    width = tile.shape[1]
    full, rest = count // width, count % width
    yield tile[0:full, :], dram[0:full * width].rearrange("(p c) -> p c", p=full)
    if rest:
        yield tile[full:full + 1, 0:rest], dram[full * width:count].rearrange("(p c) -> p c", p=1)


def next_starts(tile, dram, count, width):
    full, rest = count // width, count % width
    yield tile[0:full - 1, :], dram[0:full * width].rearrange("(p c) -> p c", p=full)[1:full, 0:1]
    if rest:
        yield tile[full - 1:full, :], dram[full * width:full * width + 1].rearrange("(p c) -> p c", p=1)


def zero_table(sp, m, table, zeroed, first, last):
    flat = table.rearrange("(p t) d -> p (t d)", p=LANES)
    piece = m.tcols * table.shape[1] // ZERO_PIECES
    sp.wait_ge(m.zero_tile, 1)
    for i in range(first, last):
        sp.dma_start(flat[:, i * piece:(i + 1) * piece], m.zero[:, 0:piece]).then_inc(zeroed, DMA)


def set_up(nc, m, w):
    name = "setup_"
    with Phase(nc, name) as ctx:
        sem, sb, bank = ctx.sem, ctx.sb, ctx.bank
        loaded, cleared = sem("loaded"), sem("cleared")
        vec_step, act_done = sem("vec_step"), sem("act_done")
        coef = sb("coef", [P, 3])
        cmax = sb("cmax", [P, 1])
        cexp = sb("cexp", [P, 3])
        csum = sb("csum", [P, 1])
        scp = sb("scp", [P, 1])
        sca = sb("sca", [P, 3])
        edges_loaded, edges_copied, falls_ready, falls_summed, padded = (
            sem("edges_loaded"), sem("edges_copied"), sem("falls_ready"), sem("falls_summed"), sem("padded"))
        EC = m.ecols
        dst, src_ids, next_dst = sb("dst", [P, EC], I32), sb("src", [P, EC], I32), sb("next_dst", [P, 1], I32)
        falls, fall_count = sb("falls", [P, EC]), sb("fall_count", [P, 1])
        ps_falls = bank("ps_falls")
        parts = 2 if m.edges % EC else 1
        block = ctx.block()
        small = [
            (m.ident, w["ident"]), (m.before, w["before"]), (m.sgn, w["sgn"]),
            (m.deg, w["deg_coeff"].partition_broadcast(P)),
            (coef, w["coeff"].partition_broadcast(P)), (scp, w["scale"].partition_broadcast(P)),
            (m.b1, w["b1"].partition_broadcast(LANES)), (m.b2, w["b2"].partition_broadcast(LANES)),
            (m.bg, w["bg"].partition_broadcast(P)), (m.b3, w["b3"].partition_broadcast(LANES)),
        ]
        twice = [(m.w1r, w["w1r"]), (m.w1l, w["w1l"]), (m.w2r, w["w2r"]), (m.w2l, w["w2l"]),
                 (m.w3x, w["w3x"]), (m.w3m, w["w3m"]), (m.wg, w["wg"])]

        @block.sync
        def _(sp):
            sp.wait_ge(padded, 1)
            for tile, src in ((dst, w["dst"]), (src_ids, w["src"])):
                for here, there in row_parts(tile, src, m.edges):
                    sp.dma_start(here, there).then_inc(edges_loaded, DMA)
            for here, there in next_starts(next_dst, w["dst"], m.edges, EC):
                sp.dma_start(here, there, allow_slow_non_contiguous=True).then_inc(edges_loaded, DMA)
            for tile, src in small:
                sp.dma_start(tile[:, :], src).then_inc(loaded, DMA)
            sp.wait_ge(cleared, 1)
            for tile, src in twice:
                sp.dma_start(tile[0:D, 0:D], src).then_inc(loaded, DMA)
                sp.dma_start(tile[D:P, D:P], src).then_inc(loaded, DMA)
            sp.dma_start(m.wqkv[0:D, 0:D], w["wq"]).then_inc(loaded, DMA)
            sp.dma_start(m.wqkv[D:P, D:2 * D], w["wk"]).then_inc(loaded, DMA)
            sp.dma_start(m.wqkv[D:P, 2 * D:3 * D], w["wv"]).then_inc(loaded, DMA)
            sp.wait_ge(edges_loaded, 3 * parts * DMA)
            for tile, copy in ((dst, m.d_key), (src_ids, m.d_other)):
                for here, there in row_parts(tile, copy, m.edges):
                    sp.dma_start(there, here).then_inc(edges_copied, DMA)
            zero_table(sp, m, m.sum_d, m.zeroed_d, 0, ZERO_PIECES // 4)
            sp.wait_ge(edges_copied, 2 * parts * DMA)
            sp.wait_ge(loaded, DMA * (len(small) + 2 * len(twice) + 3))

        @block.gpsimd
        def _(pool):
            pool.memset(m.zero[:, :], 0.0).then_inc(m.zero_tile, 1)
            for tile, _ in twice:
                pool.memset(tile[:, :], 0.0)
            pool.memset(m.wqkv[:, :], 0.0).then_inc(cleared, 1)

        @block.tensor
        def _(pe):
            pe.wait_ge(falls_ready, 3)
            pe.matmul(ps_falls[0:1, 0:1], fall_count[:, :], m.ones[0:P, 0:1], start=True, stop=True).then_inc(falls_summed, 1)

        @block.scalar
        def _(act):
            act.wait_ge(vec_step, 2)
            act.activation(cexp[:, :], cexp[:, :], ACT.Exp).then_inc(act_done, 1)
            act.activation(sca[:, 0:1], scp[:, :], ACT.Abs).then_inc(act_done, 1)
            act.wait_ge(act_done, 2)
            act.activation(sca[:, 1:2], sca[:, 0:1], ACT.Exp, scale=-1.0).then_inc(act_done, 1)
            act.wait_ge(act_done, 3)
            act.activation(sca[:, 2:3], sca[:, 1:2], ACT.Ln, bias=1.0).then_inc(act_done, 1)

        @block.vector
        def _(vec):
            vec.memset(dst[:, :], SKIP)
            vec.memset(next_dst[:, :], SKIP).then_inc(padded, 1)
            vec.memset(m.ones[:, :], 1.0).then_inc(falls_ready, 1)
            vec.wait_ge(edges_loaded, 3 * parts * DMA)
            vec.tensor_tensor(falls[:, EC - 1:EC], dst[:, EC - 1:EC], next_dst[:, :], ALU.is_gt)
            vec.tensor_tensor(falls[:, 0:EC - 1], dst[:, 0:EC - 1], dst[:, 1:EC], ALU.is_gt).then_inc(falls_ready, 1)
            vec.wait_ge(falls_ready, 2)
            vec.tensor_reduce(fall_count[:, :], falls[:, :], AX_X, ALU.add).then_inc(falls_ready, 1)
            vec.wait_ge(falls_summed, 1)
            vec.tensor_copy(m.unsorted[:, :], ps_falls[0:1, 0:1])
            vec.wait_ge(loaded, DMA * (len(small) + 2 * len(twice) + 3))
            vec.tensor_reduce(cmax[:, :], coef[:, :], AX_X, ALU.max).then_inc(vec_step, 1)
            vec.wait_ge(vec_step, 1)
            vec.tensor_scalar(cexp[:, :], coef[:, :], cmax[:, 0:1], None, ALU.subtract).then_inc(vec_step, 1)
            vec.wait_ge(act_done, 1)
            vec.tensor_reduce(csum[:, :], cexp[:, :], AX_X, ALU.add).then_inc(vec_step, 1)
            vec.wait_ge(vec_step, 3)
            vec.reciprocal(csum[:, :], csum[:, :]).then_inc(vec_step, 1)
            vec.wait_ge(act_done, 4)
            vec.scalar_tensor_tensor(out=scp[:, :], in0=scp[:, :], scalar=0.0, in1=sca[:, 2:3],
                                     op0=ALU.max, op1=ALU.add).then_inc(vec_step, 1)
            vec.wait_ge(vec_step, 5)
            vec.tensor_scalar(m.mix[:, :], cexp[:, :], csum[:, 0:1], scp[:, 0:1], ALU.mult, ALU.mult)


class EdgeSort:

    def __init__(self, nc, m, ctx, key_in, other_in, weights, key_out, other_out, base_out=None):
        self.m, self.E = m, key_in.shape[0]
        n = P * P
        while n < self.E:
            n *= 2
        W = self.W = n // P
        self.levels_in_row = W.bit_length() - 1
        self.parts = 2 if self.E % W else 1
        sem, sb = ctx.sem, ctx.sb
        self.loaded, self.padded, self.prepared, self.stored = sem("loaded"), sem("padded"), sem("prepared"), sem("sorted_stored")
        self.act_done, self.vec_step, self.swapped = sem("act_done"), sem("vec_step"), sem("swapped")
        self.copied, self.turned, self.flipped = sem("copied"), sem("turned"), sem("flipped")
        self.ki, self.oi = sb("ki", [P, W], I32), sb("oi", [P, W], I32)
        self.wa, self.wb = sb("wa", [P, W]), sb("wb", [P, W])
        self.z, self.az = sb("z", [P, W]), sb("az", [P, W])
        self.key = [sb(f"key{i}", [P, W]) for i in range(2)]
        self.load = [sb(f"load{i}", [P, 2, W]) for i in range(2)]
        self.mask = sb("mask", [P, W // 2], I32)
        self.ps = [ctx.enter_context(nc.psum_tensor(f"{ctx.name}ps{i}", [P, W], F32)) for i in range(3)]
        self.weighted = weights is not None
        self.inputs = [(self.ki, key_in), (self.oi, other_in)]
        self.outputs = [(self.ki, key_out), (self.oi, other_out)]
        if self.weighted:
            self.inputs += [(self.wa, weights[0]), (self.wb, weights[1])]
            self.outputs += [(self.wa, base_out)]
        self.steps, cur, swaps, turns, flips = [], 0, 0, 0, 0

        def add(kind, arg=None):
            nonlocal cur, swaps, turns, flips
            self.steps.append((kind, arg, cur, swaps, turns, flips))
            if kind == "swap":
                cur, swaps = 1 - cur, swaps + 1
            turns, flips = turns + (kind == "turn"), flips + (kind == "flip")

        for level in range(1, n.bit_length()):
            add("flip", level)
            j = level - 1
            if j >= self.levels_in_row:
                add("turn")
                while j >= self.levels_in_row:
                    add("swap", 1 << (j - self.levels_in_row))
                    j -= 1
                add("turn")
            while j >= 0:
                add("swap", 1 << j)
                j -= 1
        self.cur, self.swaps = cur, swaps

    def part(self, c, count):
        n = len(self.steps)
        return self.steps[n * c // count:n * (c + 1) // count]

    def sync_load(self, sp):
        sp.wait_ge(self.padded, len(self.inputs))
        for tile, dram in self.inputs:
            for here, there in row_parts(tile, dram, self.E):
                sp.dma_start(here, there).then_inc(self.loaded, DMA)

    def sync_store(self, sp):
        sp.wait_ge(self.prepared, 2)
        for tile, dram in self.outputs:
            for here, there in row_parts(tile, dram, self.E):
                sp.dma_start(there, here).then_inc(self.stored, DMA)
        sp.wait_ge(self.stored, DMA * len(self.outputs) * self.parts)

    def pool_pad(self, pool):
        for tile, _ in self.inputs:
            pool.memset(tile[:, :], SKIP if tile is self.ki else 0).then_inc(self.padded, 1)

    def scalar_prepare(self, act):
        if self.weighted:
            act.wait_ge(self.vec_step, 1)
            act.activation(self.az[:, :], self.z[:, :], ACT.Abs).then_inc(self.act_done, 1)
            act.wait_ge(self.act_done, 1)
            act.activation(self.az[:, :], self.az[:, :], ACT.Exp, scale=-1.0).then_inc(self.act_done, 1)
            act.wait_ge(self.act_done, 2)
            act.activation(self.az[:, :], self.az[:, :], ACT.Ln, bias=1.0).then_inc(self.act_done, 1)
        act.wait_ge(self.prepared, 1)

    def scalar_steps(self, act, steps):
        for kind, _, cur, swaps, turns, _ in steps:
            if kind == "swap":
                if swaps:
                    act.wait_ge(self.swapped, 3 * swaps)
                if turns:
                    act.wait_ge(self.copied, turns)
                act.copy(self.load[1 - cur][:, :, :], self.load[cur][:, :, :]).then_inc(self.act_done, 1)

    def tensor_steps(self, pe, steps):
        for kind, _, cur, swaps, turns, flips in steps:
            if kind == "turn":
                pe.wait_ge(self.swapped, 3 * swaps)
                if turns % 2 == 0:
                    pe.wait_ge(self.flipped, flips)
                if turns:
                    pe.wait_ge(self.copied, turns)
                for b in range(self.W // P):
                    c = slice(b * P, (b + 1) * P)
                    pe.transpose(self.ps[0][:, c], self.key[cur][:, c], self.m.ident[:, :])
                    pe.transpose(self.ps[1][:, c], self.load[cur][:, 0, c], self.m.ident[:, :])
                    t = pe.transpose(self.ps[2][:, c], self.load[cur][:, 1, c], self.m.ident[:, :])
                t.then_inc(self.turned, 1)

    def vector_prepare(self, vec):
        m, z, az = self.m, self.z, self.az
        vec.wait_ge(self.loaded, DMA * len(self.inputs) * self.parts)
        if self.weighted:
            vec.tensor_scalar(z[:, :], self.wb[:, :], m.deg[:, 0:1], m.deg[:, 1:2], ALU.mult, ALU.add).then_inc(self.vec_step, 1)
            vec.wait_ge(self.act_done, 3)
            vec.wait_ge(self.vec_step, 1)
            vec.scalar_tensor_tensor(out=z[:, :], in0=z[:, :], scalar=0.0, in1=az[:, :],
                                     op0=ALU.max, op1=ALU.add).then_inc(self.vec_step, 1)
            vec.wait_ge(self.vec_step, 2)
            vec.tensor_tensor(z[:, :], z[:, :], self.wa[:, :], ALU.mult).then_inc(self.vec_step, 1)
            vec.tensor_tensor(az[:, :], self.ki[:, :], self.oi[:, :], ALU.not_equal).then_inc(self.vec_step, 1)
            vec.wait_ge(self.vec_step, 4)
            vec.tensor_tensor(self.load[0][:, 1, :], z[:, :], az[:, :], ALU.mult)
        else:
            vec.memset(self.load[0][:, 1, :], 0.0)
        vec.tensor_copy(self.key[0][:, :], self.ki[:, :])
        vec.tensor_copy(self.load[0][:, 0, :], self.oi[:, :]).then_inc(self.prepared, 1)
        vec.wait_ge(self.prepared, 1)

    def vector_steps(self, vec, steps):
        for kind, arg, cur, swaps, turns, flips in steps:
            if kind == "flip":
                self.vector_flip(vec, self.key[cur], arg, swaps)
            elif kind == "turn":
                vec.wait_ge(self.turned, turns + 1)
                vec.tensor_copy(self.key[cur][:, :], self.ps[0][:, :])
                vec.tensor_copy(self.load[cur][:, 0, :], self.ps[1][:, :])
                vec.tensor_copy(self.load[cur][:, 1, :], self.ps[2][:, :]).then_inc(self.copied, 1)
            else:
                self.vector_swap(vec, arg, cur, swaps, turns, flips)

    def vector_flip(self, vec, key, level, swaps):
        W, m = self.W, self.m
        if swaps:
            vec.wait_ge(self.swapped, 3 * swaps)
        if level < self.levels_in_row:
            if level == 1:
                parts = [key[:, :].rearrange("p (a two r) -> p a two r", two=2, r=2)[:, :, 1, :]]
            else:
                v = key[:, :].rearrange("p (a x y r) -> p a x y r", x=2, y=2, r=1 << (level - 1))
                parts = [v[:, :, 0, 1, :], v[:, :, 1, 0, :]]
            for q in parts:
                ins = vec.tensor_scalar(q, q, -1.0, None, ALU.mult)
            ins.then_inc(self.flipped, 1)
        elif level == self.levels_in_row:
            low, high = key[:, 0:W // 2], key[:, W // 2:W]
            vec.tensor_scalar(low, low, m.sgn[:, 0:1], None, ALU.mult)
            vec.tensor_scalar(high, high, m.sgn[:, 0:1], -1.0, ALU.mult, ALU.mult).then_inc(self.flipped, 1)
        else:
            k = level - self.levels_in_row
            vec.tensor_scalar(key[:, :], key[:, :], m.sgn[:, k:k + 1], None, ALU.mult).then_inc(self.flipped, 1)

    def vector_swap(self, vec, stride, cur, swaps, turns, flips):
        def halves(ap):
            v = ap.rearrange("p (a two r) -> p a two r", two=2, r=stride)
            return v[:, :, 0, :], v[:, :, 1, :]

        low, high = halves(self.key[cur][:, :])
        new_low, new_high = halves(self.key[1 - cur][:, :])
        falls = self.mask[:, :].rearrange("p (a r) -> p a r", r=stride)
        if swaps:
            vec.wait_ge(self.swapped, 3 * swaps)
        vec.wait_ge(self.flipped, flips)
        if turns:
            vec.wait_ge(self.copied, turns)
        vec.tensor_tensor(falls, low, high, ALU.is_gt).then_inc(self.vec_step, 1)
        vec.tensor_tensor(new_low, low, high, ALU.min)
        vec.tensor_tensor(new_high, low, high, ALU.max).then_inc(self.swapped, 1)
        vec.wait_ge(self.act_done, (3 if self.weighted else 0) + swaps + 1)
        vec.wait_ge(self.vec_step, (4 if self.weighted else 0) + swaps + 1)
        for carried in range(2):
            old_low, old_high = halves(self.load[cur][:, carried, :])
            to_low, to_high = halves(self.load[1 - cur][:, carried, :])
            vec.copy_predicated(to_low, falls, old_high)
            vec.copy_predicated(to_high, falls, old_low).then_inc(self.swapped, 1)

    def vector_finish(self, vec):
        vec.wait_ge(self.swapped, 3 * self.swaps)
        vec.tensor_copy(self.ki[:, :], self.key[self.cur][:, :])
        if self.weighted:
            vec.tensor_copy(self.wa[:, :], self.load[self.cur][:, 1, :])
        vec.tensor_copy(self.oi[:, :], self.load[self.cur][:, 0, :]).then_inc(self.prepared, 1)


def sort_if(nc, m, name, flag, key_in, other_in, key_out, other_out):
    with Phase(nc, name) as ctx:
        sort = EdgeSort(nc, m, ctx, key_in, other_in, None, key_out, other_out)
        block = ctx.block()
        wanted = lambda engine: engine.If(engine.value_load(flag) > 0)

        @block.sync
        def _(sp):
            with wanted(sp):
                sort.sync_load(sp)
                sort.sync_store(sp)

        @block.gpsimd
        def _(pool):
            with wanted(pool):
                sort.pool_pad(pool)

        @block.scalar
        def _(act):
            with wanted(act):
                sort.scalar_prepare(act)
                sort.scalar_steps(act, sort.steps)

        @block.tensor
        def _(pe):
            with wanted(pe):
                sort.tensor_steps(pe, sort.steps)

        @block.vector
        def _(vec):
            with wanted(vec):
                sort.vector_prepare(vec)
                sort.vector_steps(vec, sort.steps)
                sort.vector_finish(vec)


def edge_plan(nc, m, name, key_dram, columns_f, plan, fields, carry_mask, fix_idx, fix_inv, zero_beside=None):
    EC = m.ecols
    with Phase(nc, name) as ctx:
        sem, sb, bank = ctx.sem, ctx.sb, ctx.bank
        loaded, step, turned, padded = sem("loaded"), sem("step"), sem("turned"), sem("padded")
        ki = sb("ki", [P, EC], I32)
        nxt_i, nxt = sb("nxt_i", [P, 1], I32), sb("nxt", [P, 1])
        key, same, on = sb("key", [P, EC]), sb("same", [P, EC]), sb("on", [P, EC])
        ones, cnt, first = sb("ones", [P, EC]), sb("cnt", [P, EC]), sb("first", [P, EC])
        bc = sb("bc", [P, P])
        t1, t2, t3 = sb("t1", [P, 1]), sb("t2", [P, 1]), sb("t3", [P, 1])
        others = {f: sb("in_" + f, [P, EC], dt) for f, (_, dt) in columns_f.items()}
        psb = bank("psb")
        psc = bank("psc")
        block = ctx.block()
        parts = 2 if m.edges % EC else 1
        field = lambda f: plan[:, :, fields.index(f), :]
        by_chunk = lambda t: t[:, :].rearrange("p (c g) -> p c g", g=G)

        @block.sync
        def _(sp):
            sp.wait_ge(padded, 1)
            for tile, src in [(ki, key_dram)] + [(others[f], src) for f, (src, _) in columns_f.items()]:
                for here, there in row_parts(tile, src, m.edges):
                    sp.dma_start(here, there).then_inc(loaded, DMA)
            for here, there in next_starts(nxt_i, key_dram, m.edges, EC):
                sp.dma_start(here, there, allow_slow_non_contiguous=True).then_inc(loaded, DMA)
            if zero_beside is not None:
                zero_table(sp, m, *zero_beside)

        @block.vector
        def _(vec):
            count = 0

            def did(ins):
                nonlocal count
                ins.then_inc(step, 1)
                count += 1
                vec.wait_ge(step, count)

            vec.memset(ki[:, :], SKIP)
            for tile in others.values():
                vec.memset(tile[:, :], 0)
            vec.memset(nxt_i[:, :], -1).then_inc(padded, 1)
            vec.memset(same[:, 0:1], 0.0)
            did(vec.memset(ones[:, :], 1.0))
            vec.wait_ge(loaded, DMA * parts * (2 + len(columns_f)))
            vec.tensor_copy(nxt[:, :], nxt_i[:, :])
            did(vec.tensor_copy(key[:, :], ki[:, :]))
            vec.tensor_tensor(same[:, 1:EC], key[:, 1:EC], key[:, 0:EC - 1], ALU.is_equal)
            vec.tensor_tensor(on[:, 0:EC - 1], key[:, 1:EC], key[:, 0:EC - 1], ALU.is_equal)
            vec.tensor_tensor(on[:, EC - 1:EC], key[:, EC - 1:EC], nxt[:, :], ALU.is_equal)
            vec.tensor_scalar(first[:, :], key[:, :], key[:, 0:1], None, ALU.is_equal)
            vec.tensor_tensor(t1[:, :], key[:, 0:1], key[:, EC - 1:EC], ALU.is_equal)
            did(vec.tensor_scalar(bc[:, :], m.ones[0:P, 0:P], key[:, 0:1], None, ALU.mult))
            vec.scalar_tensor_tensor(out=field("to"), in0=by_chunk(on), scalar=float(SKIP), in1=by_chunk(key),
                                     op0=ALU.mult, op1=ALU.add)
            vec.tensor_copy(field("same"), by_chunk(same))
            for f, tile in others.items():
                vec.tensor_copy(field(f), by_chunk(tile))
            vec.tensor_tensor_scan(cnt[:, :], same[:, :], ones[:, :], 0.0, ALU.mult, ALU.add)
            did(vec.tensor_tensor(t1[:, :], t1[:, :], on[:, EC - 1:EC], ALU.mult))
            did(vec.scalar_tensor_tensor(out=t2[:, :], in0=t1[:, :], scalar=float(SKIP), in1=key[:, 0:1],
                                         op0=ALU.mult, op1=ALU.add))
            vec.tensor_copy(fix_idx[:, :], t2[:, :])
            vec.wait_ge(turned, 1)
            did(vec.scalar_tensor_tensor(out=carry_mask[:, :], in0=psb[0:P, 0:P], scalar=key[:, EC - 1:EC],
                                         in1=m.before[:, :], op0=ALU.is_equal, op1=ALU.mult))
            vec.wait_ge(turned, 2)
            did(vec.tensor_copy(t3[:, :], psc[0:P, 0:1]))
            did(vec.scalar_tensor_tensor(out=cnt[:, :], in0=first[:, :], scalar=t3[:, 0:1], in1=cnt[:, :],
                                         op0=ALU.mult, op1=ALU.add))
            vec.tensor_reduce(t1[:, :], first[:, :], AX_X, ALU.add)
            did(vec.reciprocal(cnt[:, :], cnt[:, :]))
            did(vec.tensor_tensor(t1[:, :], t1[:, :], t3[:, :], ALU.add))
            if fix_inv is not None:
                vec.tensor_copy(field("inv"), by_chunk(cnt))
                did(vec.reciprocal(fix_inv[:, :], t1[:, :]))

        @block.tensor
        def _(pe):
            pe.wait_ge(step, 3)
            pe.transpose(psb[0:P, 0:P], bc[:, :], m.ident[0:P, 0:P]).then_inc(turned, 1)
            pe.wait_ge(step, 6)
            pe.matmul(psc[0:P, 0:1], carry_mask[:, :], cnt[:, EC - 1:EC], start=True, stop=True).then_inc(turned, 1)


def edge_phase(nc, m, name, kind, tables, plan, fields, sums, carry_mask, fix_idx, fix_inv=None, beside=None):
    NCH = m.ecols // G
    NF = len(fields)
    NG = fields.index("to")
    NS = NF - NG - 1
    flag = lambda f: fields.index(f) - NG - 1
    W = tables[0].shape[1]
    mean, cosine, heads = kind == "mean", kind == "cosine", kind == "heads"
    width = D if mean else ROW2
    SW = ROW2 if heads else D
    GATHERED = DMA * G * NG
    SCATTERED = DMA * G
    QC = 4
    T = G // QC
    with Phase(nc, name) as ctx:
        sem, sb, bank = ctx.sem, ctx.sb, ctx.bank
        gathered = [sem("gathered0"), sem("gathered1")]
        scattered = [sem("scattered0"), sem("scattered1")]
        from_ready, flags_ready, rows_used, scan = sem("from_ready"), sem("flags_ready"), sem("rows_used"), sem("scan")
        fixed, fix_in, fix_out, carried, fix_clear = sem("fixed"), sem("fix_in"), sem("fix_out"), sem("carried"), sem("fix_clear")
        idx_from = sb("idx_from", [P, 2, NG, G], I32)
        idx_to = sb("idx_to", [P, 2, G], I32)
        flags = sb("flags", [P, 2, NS, G])
        rows = sb("rows", [P, 2, G, NG * W])
        out = sb("out", [P, 2, G, width])
        fix = sb("fix", [P, width])
        chain = sb("chain", [P, 2, G, D]) if mean else out
        source = rows if mean else out
        ps_c = bank("ps_c")
        if beside is not None:
            sort = EdgeSort(nc, m, ctx, *beside)
            zeroed_s = sem("zeroed_s")
        begun = sem("begun")
        if mean:
            scaled = sem("scaled")
        else:
            step, act_math = sem("step"), sem("act_math")
            turned, turned_copied, projected = sem("turned"), sem("turned_copied"), sem("projected")
            proj_copied, proj_used = sem("proj_copied"), sem("proj_used")
            projection = m.wg if cosine else m.wqkv
            PW = projection.shape[1]
            prod = sb("prod", [P, G, D])
            turned_rows = sb("turned_rows", [P, 2, QC * P])
            proj = sb("proj", [P, 2, G, PW])
            ps_t = [bank("ps_t0"), bank("ps_t1")]
            ps_q = [bank(f"ps_q{i}") for i in range(4)]
        if cosine:
            sq_read, biased = sem("sq_read"), sem("biased")
            sq = sb("sq", [P, G, 2 * D])
            dot, nrm, sim, att = sb("dot", [P, G]), sb("nrm", [P, G, 2]), sb("sim", [P, 2, G]), sb("att", [P, G])
        if heads:
            att, wts = sb("att", [P, G * HEADS]), sb("wts", [P, G * HEADS])
        block = ctx.block()

        if beside is not None:
            @block.sync
            def _(sp):
                sort.sync_load(sp)
                zero_table(sp, m, m.sum_d, m.zeroed_d, ZERO_PIECES // 2, ZERO_PIECES)
                sp.wait_ge(m.zeroed_d, ZERO_PIECES * DMA)
                zero_table(sp, m, m.sum_s, zeroed_s, 0, ZERO_PIECES)
                sort.sync_store(sp)
                sp.wait_ge(zeroed_s, ZERO_PIECES * DMA)

        @block.gpsimd
        def _(pool):
            def gathers(c, h, u):
                need(pool, from_ready, c + 1)
                need(pool, rows_used, c - 1)
                pool.sem_inc(begun)
                for g in range(NG):
                    for j in range(G):
                        pool.indirect_dma_start(out=rows[:, h, j, g * W:(g + 1) * W], out_offset=None,
                                                in_=tables[g], in_offset=at(idx_from[:, h, g, j:j + 1])
                                                ).then_inc(gathered[h], DMA)

            def scatters(c, h, u):
                need(pool, flags_ready, c + 1)
                if mean:
                    need(pool, scaled, c + 1)
                else:
                    need(pool, scan, G * c + G + 1)
                if beside is not None and isinstance(c, int) and c == 0:
                    pool.wait_ge(m.zeroed_d, ZERO_PIECES * DMA)
                pool.sem_inc(begun)
                for j in range(G):
                    pool.indirect_dma_start(out=sums, out_offset=at(idx_to[:, h, j:j + 1]), in_=out[:, h, j, :],
                                            in_offset=None, bounds_check=m.nodes - 1, oob_is_err=False
                                            ).then_inc(scattered[h], DMA)

            pool.memset(fix[:, :], 0.0).then_inc(fix_clear, 1)
            if beside is not None:
                sort.pool_pad(pool)
            rounds(pool, NCH, [(gathers, 0), (scatters, 1)])
            for h in range(2):
                pool.wait_ge(scattered[h], SCATTERED * (NCH // 2))
            pool.wait_ge(fix_clear, 1)
            pool.indirect_dma_start(out=fix[:, :], out_offset=None, in_=sums, in_offset=at(fix_idx[:, 0:1]),
                                    bounds_check=m.nodes - 1, oob_is_err=False).then_inc(fix_in, DMA)
            pool.wait_ge(fixed, 1)
            pool.indirect_dma_start(out=sums, out_offset=at(fix_idx[:, 0:1]), in_=fix[:, :], in_offset=None,
                                    bounds_check=m.nodes - 1, oob_is_err=False).then_inc(fix_out, DMA)
            pool.wait_ge(fix_out, DMA)

        @block.scalar
        def _(act):
            def stage_from(c, h, u):
                need(act, gathered[h], GATHERED * u)
                act.copy(idx_from[:, h, :, :], plan[:, c, 0:NG, :]).then_inc(from_ready, 1)

            def stage_flags(c, h, u):
                need(act, scattered[h], SCATTERED * u)
                act.copy(idx_to[:, h, :], plan[:, c, NG, :])
                act.copy(flags[:, h, :, :], plan[:, c, NG + 1:NF, :]).then_inc(flags_ready, 1)

            def copy_projections(c, h, q):
                for n in (2 * q, 2 * q + 1):
                    need(act, projected, 2 * T * c + n + 1)
                    if n == 0:
                        need(act, proj_used, c - 1)
                    act.copy(proj[:, h, 2 * n:2 * n + 2, :],
                             ps_q[(2 * T * h + n) % 4][0:P, :].rearrange("p (a b) -> p a b", a=2)[:, :, 0:PW]
                             ).then_inc(proj_copied, 1)

            def lengths(c, h, u):
                need(act, biased, c + 1)
                need(act, sq_read, c)
                act.activation(sq[:, :, :], proj[:, h, :, :], ACT.Square).then_inc(act_math, 1)
                need(act, sq_read, c + 1)
                act.activation(nrm[:, :, :], nrm[:, :, :], ACT.Sqrt).then_inc(act_math, 1)

            def projections(c, h, u):
                for q in range(T):
                    need(act, turned, T * c + q + 1)
                    need(act, projected, 2 * (T * c + q - 1))
                    act.copy(turned_rows[:, (T * h + q) % 2, :], ps_t[(T * h + q) % 2][:, 0:QC * P]).then_inc(turned_copied, 1)
                    if q:
                        copy_projections(c, h, q - 1)
                copy_projections(c, h, T - 1)

            def exponentials(c, h, u):
                need(act, step, 5 * c + 3)
                act.activation(wts[:, :], att[:, :], ACT.Exp).then_inc(act_math, 1)

            own = [(projections, 0), (lengths, 0)] if cosine else [(projections, 0), (exponentials, 0)] if heads else []
            if beside is None:
                rounds(act, NCH, [(stage_from, 0), (stage_flags, 0)] + own)
            else:
                for c in range(NCH):
                    stage_from(c, c % 2, c // 2)
                    stage_flags(c, c % 2, c // 2)
                    if c == 0:
                        sort.scalar_prepare(act)
                    sort.scalar_steps(act, sort.part(c, NCH))

        @block.tensor
        def _(pe):
            def turn(c, h, q):
                need(pe, turned_copied, T * c + q - 1)
                for r in range(QC):
                    ins = pe.transpose(ps_t[(T * h + q) % 2][:, r * P:(r + 1) * P], rows[:, h, QC * q + r, :],
                                       m.ident[0:P, 0:P])
                ins.then_inc(turned, 1)

            def project(c, h, q):
                need(pe, turned_copied, T * c + q + 1)
                for n in (2 * q, 2 * q + 1):
                    need(pe, proj_copied, 2 * T * c + n - 3)
                    for r in range(2):
                        col = (n % 2) * 2 + r
                        ins = pe.matmul(ps_q[(2 * T * h + n) % 4][0:P, r * 256:r * 256 + PW],
                                        turned_rows[:, (T * h + q) % 2, col * P:(col + 1) * P],
                                        projection[:, :], start=True, stop=True)
                    ins.then_inc(projected, 1)

            def project_chunk(c, h, u):
                need(pe, gathered[h], GATHERED * (u + 1))
                turn(c, h, 0)
                for q in range(1, T):
                    turn(c, h, q)
                    project(c, h, q - 1)
                need(pe, turned, T * (c + 1))
                pe.nop().then_inc(rows_used, 1)
                project(c, h, T - 1)

            if not mean:
                rounds(pe, NCH, [(project_chunk, 0)])
            if beside is not None:
                sort.tensor_steps(pe, sort.steps)
            pe.wait_ge(scan, G * NCH + 1)
            pe.matmul(ps_c[0:P, 0:SW], carry_mask[:, :], chain[:, 1, G - 1, 0:SW], start=True, stop=True).then_inc(carried, 1)

        @block.vector
        def _(vec):
            STEPS = {"mean": 0, "cosine": 8, "heads": 5}[kind]

            def messages(c, h, u):
                n = 0

                def did(ins):
                    nonlocal n
                    n += 1
                    ins.then_inc(step, 1)
                    need(vec, step, STEPS * c + n)

                if cosine:
                    wr, wc = proj[:, h, :, 0:D], proj[:, h, :, D:2 * D]
                    vec.wait_ge(proj_copied, 2 * T * (c + 1))
                    both = proj[:, h, :, :].rearrange("p g (a d) -> p (g a) d", a=2)
                    vec.tensor_tensor(both, both, m.bg[:, :].unsqueeze(1).to_broadcast([P, 2 * G, D]), ALU.add
                                      ).then_inc(biased, 1)
                    vec.wait_ge(biased, c + 1)
                    did(vec.tensor_tensor(prod[:, :, :], wr, wc, ALU.mult))
                    vec.tensor_reduce(dot[:, :], prod[:, :, :], AX_X, ALU.add)
                    vec.wait_ge(act_math, 2 * c + 1)
                    vec.tensor_reduce(nrm[:, :, :], sq[:, :, :].rearrange("p g (a d) -> p g a d", a=2), AX_X, ALU.add).then_inc(sq_read, 1)
                    vec.wait_ge(act_math, 2 * c + 2)
                    did(vec.tensor_tensor(att[:, :], nrm[:, :, 0], nrm[:, :, 1], ALU.mult))
                    did(vec.tensor_scalar(att[:, :], att[:, :], 1e-8, None, ALU.max))
                    did(vec.reciprocal(att[:, :], att[:, :]))
                    did(vec.tensor_tensor(dot[:, :], dot[:, :], att[:, :], ALU.mult))
                    vec.tensor_scalar(sim[:, 0, :], dot[:, :], 0.0, m.mix[:, 0:1], ALU.max, ALU.mult)
                    did(vec.tensor_scalar(sim[:, 1, :], dot[:, :], 0.0, m.mix[:, 1:2], ALU.min, ALU.mult))
                    did(vec.tensor_tensor(att[:, :], sim[:, 0, :], sim[:, 1, :], ALU.add))
                    did(vec.tensor_tensor(att[:, :], att[:, :], flags[:, h, flag("base"), :], ALU.mult))
                    need(vec, scattered[h], SCATTERED * u)
                    vec.tensor_tensor(out[:, h, :, 0:D], wc, att[:, :].unsqueeze(2).to_broadcast([P, G, D]), ALU.mult
                                      ).then_inc(proj_used, 1)
                    vec.wait_ge(proj_used, c + 1)
                if heads:
                    vec.wait_ge(proj_copied, 2 * T * (c + 1))
                    did(vec.tensor_tensor(prod[:, :, :], proj[:, h, :, 0:D], proj[:, h, :, D:2 * D], ALU.mult))
                    did(vec.tensor_reduce(att[:, :], prod[:, :, :].rearrange("p g (a d) -> p (g a) d", a=HEADS), AX_X, ALU.add))
                    did(vec.tensor_scalar(att[:, :], att[:, :], 10.0, -10.0, ALU.min, ALU.max))
                    vec.wait_ge(act_math, c + 1)
                    need(vec, scattered[h], SCATTERED * u)
                    did(vec.tensor_copy(out[:, h, :, D:ROW2], wts[:, :].rearrange("p (g a) -> p g a", a=HEADS)))
                    did(vec.tensor_copy(prod[:, :, :].rearrange("p g (a d) -> p (g a) d", a=HEADS),
                                        wts[:, :].unsqueeze(2).to_broadcast([P, G * HEADS, DH])))
                    vec.tensor_tensor(out[:, h, :, 0:D], proj[:, h, :, 2 * D:3 * D], prod[:, :, :], ALU.mult).then_inc(proj_used, 1)
                    vec.wait_ge(proj_used, c + 1)
                assert n == STEPS, n

            def chunk(c, h, u):
                need(vec, gathered[h], GATHERED * (u + 1))
                vec.wait_ge(flags_ready, c + 1)
                messages(c, h, u)
                for j in range(G):
                    prev = chain[:, 1 - h, G - 1, 0:SW] if j == 0 else chain[:, h, j - 1, 0:SW]
                    vec.wait_ge(scan, G * c + j + 1)
                    vec.scalar_tensor_tensor(out=chain[:, h, j, 0:SW], in0=prev, scalar=flags[:, h, flag("same"), j:j + 1],
                                             in1=source[:, h, j, 0:SW], op0=ALU.mult, op1=ALU.add).then_inc(scan, 1)
                if mean:
                    vec.wait_ge(scan, G * c + G + 1)
                    vec.nop().then_inc(rows_used, 1)
                    need(vec, scattered[h], SCATTERED * u)
                    vec.tensor_tensor(out[:, h, :, :], chain[:, h, :, :],
                                      flags[:, h, flag("inv"), :].unsqueeze(2).to_broadcast([P, G, D]), ALU.mult
                                      ).then_inc(scaled, 1)

            if not mean:
                vec.memset(out[:, 0, :, :], 0.0)
            vec.memset(chain[:, 1, :, :], 0.0).then_inc(scan, 1)
            if beside is None:
                rounds(vec, NCH, [(chunk, 0)])
            else:
                sort.vector_prepare(vec)
                for c in range(NCH):
                    sort.vector_steps(vec, sort.part(c, NCH))
                    chunk(c, c % 2, c // 2)
                sort.vector_finish(vec)
            vec.wait_ge(fix_in, DMA)
            vec.wait_ge(carried, 1)
            if mean:
                vec.scalar_tensor_tensor(out=fix[:, 0:SW], in0=ps_c[0:P, 0:SW], scalar=fix_inv[:, 0:1], in1=fix[:, 0:SW],
                                         op0=ALU.mult, op1=ALU.add).then_inc(fixed, 1)
            else:
                vec.tensor_tensor(fix[:, 0:SW], ps_c[0:P, 0:SW], fix[:, 0:SW], ALU.add).then_inc(fixed, 1)


def node_phase(nc, m, name, kind, loads, weights, bias, dst):
    NCH = m.tcols // K
    relu, unit, cosine, heads, plain = (kind == k for k in ("relu", "unit", "cosine", "heads", "plain"))
    products = not heads
    S = K // SUB
    PAIRS = SUB // 2
    ow = dst.shape[1]
    LOADED = DMA * 2
    with Phase(nc, name) as ctx:
        sem, sb, bank = ctx.sem, ctx.sb, ctx.bank
        loaded, stored = [sem("loaded0"), sem("loaded1")], [sem("stored0"), sem("stored1")]
        out_ready = sem("out_ready")
        if products:
            turned, turned_copied, multiplied, evacuated = sem("turned"), sem("turned_copied"), sem("multiplied"), sem("evacuated")
            TURNED = len(weights)
            tcp = sb("tcp", [P, 2, TURNED, PAIRS, LANES])
            ps_t = [[bank(f"ps_t{b}{e}") for e in range(TURNED)] for b in range(2)]
            ps_o = [bank("ps_o0"), bank("ps_o1")]
        tin = [sb(f"in{n}", [LANES, 2, K, t.shape[1]]) for n, t in enumerate(loads)]
        out = sb("out", [LANES, 2, K, ow])
        raw = sb("raw", [LANES, 2, K, D])
        if not relu:
            raw_ready, xs_ready, var_ready, rooted = sem("raw_ready"), sem("xs_ready"), sem("var_ready"), sem("rooted")
            rstd_ready, xn_ready, step, fin = sem("rstd_ready"), sem("xn_ready"), sem("step"), sem("fin")
            xs, xn = sb("xs", [LANES, 2, K, D]), sb("xn", [LANES, 2, K, D])
            st = sb("st", [LANES, 2, K, nc.vector.BN_STATS_DIM])
            msum, mdif, var = sb("msum", [LANES, 2, K]), sb("mdif", [LANES, K]), sb("var", [LANES, 2, K])
            rstd, shift = sb("rstd", [LANES, 2, K]), sb("shift", [LANES, 2, K])
            eps = sb("eps", [LANES, 1])
        if cosine:
            prod = sb("prod", [LANES, K, D])
        if unit:
            x_loaded = [sem("x_loaded0"), sem("x_loaded1")]
            squared, length_sq, length = sem("squared"), sem("length_sq"), sem("length")
            unit_step, unit_ready, scaled = sem("unit_step"), sem("unit_ready"), sem("scaled")
            sq, ss, rlen = sb("sq", [LANES, K, D]), sb("ss", [LANES, 2, K]), sb("rlen", [LANES, 2, K])
        if heads:
            rden, rden_step, divided = sb("rden", [LANES, 2, K * HEADS]), sem("rden_step"), sem("divided")
        block = ctx.block()
        in_cols = [columns(t) for t in loads]
        out_cols = columns(dst)
        wide = lambda t, h: t[:, h, :].unsqueeze(2).to_broadcast([LANES, K, D])
        LAG = 6 if unit else 3 if relu else 5

        @block.sync
        def _(sp):
            def load(c, h, u):
                if products:
                    need(sp, turned, S * (c - 1))
                if heads:
                    need(sp, xs_ready, c - 1)
                if plain or cosine:
                    need(sp, raw_ready, c - 1)
                for t, cols in zip(tin[0:2], in_cols):
                    sp.dma_start(t[:, h, :, :], cols[:, bass.ds(c * K, K), :]).then_inc(loaded[h], DMA)

            def load_x(c, h, u):
                need(sp, xs_ready, c - 1)
                sp.dma_start(tin[2][:, h, :, :], in_cols[2][:, bass.ds(c * K, K), :]).then_inc(x_loaded[h], DMA)

            def store(c, h, u):
                need(sp, out_ready, c + 1)
                sp.dma_start(out_cols[:, bass.ds(c * K, K), :], out[:, h, :, :]).then_inc(stored[h], DMA)

            rounds(sp, NCH, [(load, 0)] + ([(load_x, 2)] if unit else []) + [(store, LAG)])
            for h in range(2):
                sp.wait_ge(stored[h], DMA * (NCH // 2))

        @block.tensor
        def _(pe):
            def turn(s):
                def stage(c, h, u):
                    need(pe, loaded[h], LOADED * (u + 1))
                    need(pe, turned_copied, S * c + s - 1)
                    for e in range(TURNED):
                        for q in range(PAIRS):
                            col = SUB * s + 2 * q
                            ins = pe.transpose(ps_t[s % 2][e][:, q * LANES:(q + 1) * LANES],
                                               tin[e][:, h, col:col + 2, :].rearrange("p a d -> p (a d)"),
                                               m.ident[0:LANES, 0:LANES])
                    ins.then_inc(turned, 1)
                return stage

            def multiply(s):
                def stage(c, h, u):
                    need(pe, turned_copied, S * c + s + 1)
                    need(pe, evacuated, S * c + s - 1)
                    for q in range(PAIRS):
                        for e in range(TURNED):
                            ins = pe.matmul(ps_o[s % 2][0:LANES, q * P:(q + 1) * P], tcp[:, s % 2, e, q, :],
                                            weights[e][:, :], start=(e == 0), stop=(e == TURNED - 1))
                    ins.then_inc(multiplied, 1)
                return stage

            if products:
                rounds(pe, NCH, [(turn(0), 0), (multiply(0), 1), (turn(1), 0), (multiply(1), 1)])

        @block.scalar
        def _(act):
            def copy_turned(s):
                def stage(c, h, u):
                    need(act, turned, S * c + s + 1)
                    need(act, multiplied, S * c + s - 1)
                    for e in range(TURNED):
                        ins = act.copy(tcp[:, s % 2, e, :, :],
                                       ps_t[s % 2][e][:, 0:PAIRS * LANES].rearrange("p (a b) -> p a b", a=PAIRS))
                    ins.then_inc(turned_copied, 1)
                return stage

            def square(c, h, u):
                need(act, raw_ready, c + 1)
                need(act, length_sq, c)
                act.activation(sq[:, :, :], raw[:, h, :, :], ACT.Square).then_inc(squared, 1)

            def root_length(c, h, u):
                need(act, length_sq, c + 1)
                act.activation(ss[:, h, :], ss[:, h, :], ACT.Sqrt).then_inc(length, 1)

            def root_variance(c, h, u):
                need(act, var_ready, c + 1)
                act.activation(var[:, h, :], var[:, h, :], ACT.Sqrt, bias=eps[:, 0:1], scale=1.0 / D).then_inc(rooted, 1)

            if relu:
                rounds(act, NCH, [(copy_turned(0), 0), (copy_turned(1), 0)])
            elif unit:
                rounds(act, NCH, [(square, 2), (root_variance, 4), (copy_turned(0), 0), (root_length, 2), (copy_turned(1), 0)])
            elif plain or cosine:
                rounds(act, NCH, [(root_variance, 3), (copy_turned(0), 0), (copy_turned(1), 0)])
            else:
                rounds(act, NCH, [(root_variance, 3)])

        @block.gpsimd
        def _(pool):
            def unit_sum(c, h, u):
                need(pool, unit_ready, c + 1)
                need(pool, x_loaded[h], DMA * (u + 1))
                need(pool, var_ready, c - 1)
                need(pool, xn_ready, c - 1)
                pool.tensor_tensor(xs[:, h, :, :], raw[:, h, :, :], wide(rlen, h), ALU.mult).then_inc(scaled, 1)
                need(pool, scaled, c + 1)
                pool.tensor_tensor(xs[:, h, :, :], xs[:, h, :, :], tin[2][:, h, :, :], ALU.add).then_inc(xs_ready, 1)

            def first_sum(c, h, u):
                need(pool, loaded[h], LOADED * (u + 1))
                need(pool, xs_ready, c - 1)
                other = bias[0:LANES, :].unsqueeze(1).to_broadcast([LANES, K, D]) if plain else tin[1][:, h, :, 0:D]
                pool.tensor_tensor(raw[:, h, :, :], tin[0][:, h, :, :], other, ALU.add).then_inc(raw_ready, 1)

            def divide(c, h, u):
                need(pool, raw_ready, c + 1)
                need(pool, xs_ready, c - 1)
                pool.tensor_tensor(raw[:, h, :, :].rearrange("p k (a d) -> p k a d", a=HEADS),
                                   tin[1][:, h, :, 0:D].rearrange("p k (a d) -> p k a d", a=HEADS),
                                   rden[:, h, :].rearrange("p (k a) -> p k a", a=HEADS).unsqueeze(3).to_broadcast([LANES, K, HEADS, DH]),
                                   ALU.mult).then_inc(divided, 1)

            def normalise(c, h, u):
                need(pool, rstd_ready, c + 1)
                need(pool, out_ready, c - 1)
                pool.tensor_tensor(xn[:, h, :, :], xs[:, h, :, :], wide(rstd, h), ALU.mult).then_inc(xn_ready, 1)

            if not relu:
                rounds(pool, NCH, [(normalise, 4), (unit_sum, 2)] if unit else
                       [(normalise, 3), (divide, 0)] if heads else [(first_sum, 0), (normalise, 3)])

        @block.vector
        def _(vec):
            def chain(counter, per_chunk, c):
                n = 0

                def did(ins):
                    nonlocal n
                    n += 1
                    ins.then_inc(counter, 1)
                    need(vec, counter, per_chunk * c + n)
                return did

            def evacuate(c, h, u):
                if unit:
                    need(vec, xs_ready, c - 1)
                if plain or cosine:
                    need(vec, raw_ready, c + 1)
                if cosine:
                    need(vec, xs_ready, c)
                if plain:
                    need(vec, xn_ready, c - 1)
                for s in range(S):
                    need(vec, multiplied, S * c + s + 1)
                    cols = slice(SUB * s, SUB * (s + 1))
                    target = xs[:, h, cols, :] if plain else prod[:, cols, :] if cosine else raw[:, h, cols, :]
                    other = raw[:, h, cols, :] if plain else bias[0:LANES, :].unsqueeze(1).to_broadcast([LANES, SUB, D])
                    vec.tensor_tensor(target, ps_o[s % 2][0:LANES, :].rearrange("p (a d) -> p a d", d=D), other, ALU.add
                                      ).then_inc(evacuated, 1)
                need(vec, evacuated, S * (c + 1))
                if unit or plain:
                    vec.nop().then_inc(raw_ready if unit else xs_ready, 1)

            def leaky(c, h, u):
                need(vec, stored[h], DMA * u)
                vec.scalar_tensor_tensor(out=out[:, h, :, :], in0=raw[:, h, :, :], scalar=0.01, in1=raw[:, h, :, :],
                                         op0=ALU.mult, op1=ALU.max).then_inc(out_ready, 1)

            def add_product(c, h, u):
                need(vec, xn_ready, c - 1)
                vec.scalar_tensor_tensor(out=xs[:, h, :, :], in0=prod[:, :, :], scalar=m.mix[0:LANES, 2:3],
                                         in1=raw[:, h, :, :], op0=ALU.mult, op1=ALU.add).then_inc(xs_ready, 1)

            def invert_weights(c, h, u):
                need(vec, loaded[h], LOADED * (u + 1))
                need(vec, divided, c - 1)
                vec.tensor_scalar(rden[:, h, :].rearrange("p (k a) -> p k a", a=HEADS), tin[1][:, h, :, D:ROW2], 1e-8, None,
                                  ALU.add).then_inc(rden_step, 1)
                need(vec, rden_step, c + 1)
                vec.reciprocal(rden[:, h, :], rden[:, h, :]).then_inc(raw_ready, 1)

            def add_x(c, h, u):
                need(vec, divided, c + 1)
                need(vec, xn_ready, c - 1)
                vec.tensor_tensor(xs[:, h, :, :], raw[:, h, :, :], tin[0][:, h, :, :], ALU.add).then_inc(xs_ready, 1)

            def sum_squares(c, h, u):
                need(vec, squared, c + 1)
                vec.tensor_reduce(ss[:, h, :], sq[:, :, :], AX_X, ALU.add).then_inc(length_sq, 1)

            def invert_length(c, h, u):
                need(vec, length, c + 1)
                vec.tensor_scalar(rlen[:, h, :], ss[:, h, :], 1e-12, None, ALU.max).then_inc(unit_step, 1)
                need(vec, unit_step, c + 1)
                vec.reciprocal(rlen[:, h, :], rlen[:, h, :]).then_inc(unit_ready, 1)

            def statistics(c, h, u):
                did = chain(step, 4, c)
                need(vec, xs_ready, c + 1)
                for j in range(K):
                    ins = vec.bn_stats(st[:, h, j, :], xs[:, h, j, :])
                did(ins)
                vec.tensor_tensor(msum[:, h, :], st[:, h, :, 1], st[:, h, :, 4], ALU.add)
                vec.tensor_tensor(var[:, h, :], st[:, h, :, 2], st[:, h, :, 5], ALU.add)
                did(vec.tensor_tensor(mdif[:, :], st[:, h, :, 1], st[:, h, :, 4], ALU.subtract))
                did(vec.tensor_tensor(mdif[:, :], mdif[:, :], mdif[:, :], ALU.mult))
                did(vec.scalar_tensor_tensor(out=var[:, h, :], in0=mdif[:, :], scalar=D / 4.0, in1=var[:, h, :],
                                             op0=ALU.mult, op1=ALU.add))
                vec.nop().then_inc(var_ready, 1)

            def invert_deviation(c, h, u):
                need(vec, rooted, c + 1)
                need(vec, xn_ready, c - 1)
                vec.reciprocal(rstd[:, h, :], var[:, h, :]).then_inc(fin, 1)
                need(vec, fin, c + 1)
                vec.scalar_tensor_tensor(out=shift[:, h, :], in0=msum[:, h, :], scalar=-0.5, in1=rstd[:, h, :],
                                         op0=ALU.mult, op1=ALU.mult).then_inc(rstd_ready, 1)

            def shift_out(c, h, u):
                need(vec, xn_ready, c + 1)
                need(vec, rstd_ready, c + 1)
                need(vec, stored[h], DMA * u)
                vec.tensor_tensor(out[:, h, :, :], xn[:, h, :, :], wide(shift, h),
                                  ALU.add).then_inc(out_ready, 1)

            if not relu:
                vec.memset(eps[:, :], 1e-5)
            if relu:
                rounds(vec, NCH, [(evacuate, 1), (leaky, 1)])
            if unit:
                rounds(vec, NCH, [(invert_deviation, 4), (sum_squares, 2), (evacuate, 1), (invert_length, 2), (statistics, 3),
                                  (shift_out, 4)])
            if plain:
                rounds(vec, NCH, [(invert_deviation, 3), (statistics, 2), (evacuate, 1), (shift_out, 3)])
            if cosine:
                rounds(vec, NCH, [(invert_deviation, 3), (statistics, 2), (evacuate, 1), (add_product, 1), (shift_out, 3)])
            if heads:
                rounds(vec, NCH, [(invert_deviation, 3), (statistics, 2), (invert_weights, 0), (add_x, 1), (shift_out, 3)])


def gnn_kernel(nc, w, out):
    m = Memory()
    m.nodes, m.edges = w["x"].shape[0], w["src"].shape[0]
    m.tcols = m.nodes // LANES
    assert m.nodes % (LANES * 2 * K) == 0 and m.nodes < SKIP
    m.ecols = -(-m.edges // (P * 2 * G)) * 2 * G
    NCH = m.ecols // G
    with Phase(nc, "gnn_") as ctx:
        def dram(name, shape, dt=F32):
            return nc.dram_tensor(name, shape, dt, kind="Internal").ap()

        sb = ctx.sb
        m.sum_d, m.sum_s = dram("sum_d", (m.nodes, D)), dram("sum_s", (m.nodes, ROW2))
        h1, x1, x2, x3 = (dram(n, (m.nodes, D)) for n in ("h1", "x1", "x2", "x3"))
        s_key, s_other, s_base = dram("s_key", (m.edges,), I32), dram("s_other", (m.edges,), I32), dram("s_base", (m.edges,))
        m.d_key, m.d_other = dram("d_key", (m.edges,), I32), dram("d_other", (m.edges,), I32)
        m.zero_tile, m.zeroed_d = ctx.sem("zero_tile"), ctx.sem("zeroed_d")
        m.zero = sb("zero", [LANES, m.tcols * ROW2 // ZERO_PIECES])
        m.unsorted = sb("unsorted", [1, 1], I32)
        m.ident, m.before, m.sgn = sb("ident", [P, P]), sb("before", [P, P]), sb("sgn", [P, 8])
        m.ones = sb("ones", [P, P])
        m.deg, m.mix = sb("deg", [P, 2]), sb("mix", [P, 3])
        m.b1, m.b2, m.b3 = (sb(b, [LANES, D]) for b in ("b1", "b2", "b3"))
        m.bg = sb("bg", [P, D])
        m.w1l, m.w1r, m.w2l, m.w2r, m.wg, m.w3x, m.w3m = (
            sb(n, [P, P]) for n in ("w1l", "w1r", "w2l", "w2r", "wg", "w3x", "w3m"))
        m.wqkv = sb("wqkv", [P, 3 * D])
        by_dst, by_src = ["from", "to", "same", "inv"], ["from_a", "from_b", "to", "same", "base"]
        plan_d = sb("plan_d", [P, NCH, len(by_dst), G])
        plan_s = sb("plan_s", [P, NCH, len(by_src), G])
        mask_d, mask_s = sb("mask_d", [P, P]), sb("mask_s", [P, P])
        fix_d, fix_s = sb("fix_d", [P, 1], I32), sb("fix_s", [P, 1], I32)
        inv_d = sb("inv_d", [P, 1])

        set_up(nc, m, w)
        sort_if(nc, m, "sort_dst_", m.unsorted[0:1, 0:1], w["dst"], w["src"], m.d_key, m.d_other)
        edge_plan(nc, m, "plan_dst_", m.d_key, {"from": (m.d_other, I32)}, plan_d, by_dst, mask_d, fix_d, inv_d,
                  zero_beside=(m.sum_d, m.zeroed_d, ZERO_PIECES // 4, ZERO_PIECES // 2))
        edge_phase(nc, m, "e0_", "mean", [w["x"]], plan_d, by_dst, m.sum_d, mask_d, fix_d, inv_d,
                   beside=(w["src"], w["dst"], (w["edge_weight"], w["edge_weight_n2"]), s_key, s_other, s_base))
        edge_plan(nc, m, "plan_src_", s_key, {"from_a": (s_key, I32), "from_b": (s_other, I32), "base": (s_base, F32)},
                  plan_s, by_src, mask_s, fix_s, None)
        node_phase(nc, m, "n0_", "relu", [w["x"], m.sum_d], (m.w1r, m.w1l), m.b1, h1)
        edge_phase(nc, m, "e1_", "mean", [h1], plan_d, by_dst, m.sum_d, mask_d, fix_d, inv_d)
        node_phase(nc, m, "n1_", "unit", [h1, m.sum_d, w["x"]], (m.w2r, m.w2l), m.b2, x1)
        edge_phase(nc, m, "e2_", "cosine", [x1, x1], plan_s, by_src, m.sum_s, mask_s, fix_s)
        node_phase(nc, m, "n2_", "cosine", [x1, m.sum_s], (m.wg,), m.bg, x2)
        edge_phase(nc, m, "e3_", "heads", [x2, x2], plan_s, by_src, m.sum_s, mask_s, fix_s)
        node_phase(nc, m, "n3_", "heads", [x2, m.sum_s], None, None, x3)
        edge_phase(nc, m, "e4_", "mean", [x3], plan_d, by_dst, m.sum_d, mask_d, fix_d, inv_d)
        node_phase(nc, m, "n4_", "plain", [x3, m.sum_d], (m.w3x, m.w3m), m.b3, out)


def kernel(x, src, dst, edge_weight, edge_weight_n2, L0_gnn_W1_l, L0_gnn_b1, L0_gnn_W1_r, L0_gnn_W2_l, L0_gnn_b2,
           L0_gnn_W2_r, L1_gnn_W, L1_gnn_b, L1_gnn_deg_coeff, L1_gnn_coeff_param, L1_gnn_scale_param, L2_gnn_Wq,
           L2_gnn_Wk, L2_gnn_Wv, L3_gnn_W, L3_gnn_b):
    import numpy as np
    import concourse.bacc as bacc
    from concourse.bass_utils import run_bass_kernel_spmd

    arrays = {
        "x": x, "src": src, "dst": dst, "edge_weight": edge_weight, "edge_weight_n2": edge_weight_n2,
        "w1l": np.transpose(L0_gnn_W1_l), "w1r": np.transpose(L0_gnn_W1_r), "b1": L0_gnn_b1,
        "w2l": np.transpose(L0_gnn_W2_l), "w2r": np.transpose(L0_gnn_W2_r), "b2": L0_gnn_b2,
        "wg": L1_gnn_W, "bg": L1_gnn_b, "deg_coeff": L1_gnn_deg_coeff, "coeff": L1_gnn_coeff_param,
        "scale": L1_gnn_scale_param, "wq": L2_gnn_Wq, "wk": L2_gnn_Wk, "wv": L2_gnn_Wv,
        "w3x": L3_gnn_W[0:D], "w3m": L3_gnn_W[D:2 * D], "b3": L3_gnn_b,
    }
    arrays = {k: np.ascontiguousarray(v) for k, v in arrays.items()}
    q = np.arange(P)
    bit = lambda b: 1 - 2 * ((q >> b) & 1)
    arrays["ident"] = np.eye(P, dtype=np.float32)
    arrays["before"] = np.triu(np.ones((P, P), np.float32), 1)
    arrays["sgn"] = np.stack([bit(0)] + [bit(b) * bit(b - 1) for b in range(1, 7)] + [bit(6)], 1).astype(np.float32)

    nc = bacc.Bacc("TRN2", target_bir_lowering=False, num_devices=1)
    w = {k: nc.dram_tensor(f"in_{k}", a.shape, mybir.dt.from_np(a.dtype), kind="ExternalInput").ap()
         for k, a in arrays.items()}
    out = nc.dram_tensor("out_0", x.shape, F32, kind="ExternalOutput").ap()
    gnn_kernel(nc, w, out)
    r = run_bass_kernel_spmd(nc, [{f"in_{k}": a for k, a in arrays.items()}], core_ids=[0])
    return r.results[0]["out_0"]
```
